# Optimizing a Trainium2 kernel written in Bass

```python
import numpy as np
import jax
import jax.numpy as jnp

def _softmax(x, axis=-1):
    return jax.nn.softmax(x, axis=axis)

def _gelu(x):
    return jax.nn.gelu(x, approximate=True)

def _silu(x):
    return jax.nn.silu(x)

def _sigmoid(x):
    return jax.nn.sigmoid(x)

def _layernorm(x, axis=-1, eps=1e-05):
    m = jnp.mean(x, axis=axis, keepdims=True)
    v = jnp.var(x, axis=axis, keepdims=True)
    return (x - m) / jnp.sqrt(v + eps)

def _scatter_add(tgt, idx, src, axis=0):
    return tgt.at[idx].add(src)

def _segment_sum(src, seg, n):
    return jax.ops.segment_sum(src, seg, n)
kernel_name = 'mk_gnn_preln_d4_gnn_r16_283d7e'

def setup_inputs(seed: int=0):
    np.random.seed(seed)
    _w = jnp.asarray

    def _rec_inputs():
        import jax
        import jax.numpy as jnp
        _gk = jax.random.key(seed)
        x = -0.0003713 + 1 * jax.random.normal(jax.random.fold_in(_gk, 1), (3125, 128), jnp.float32)
        _s = jax.random.randint(jax.random.fold_in(_gk, 2), (50000,), 0, 3125, jnp.int32)
        _d = jax.random.randint(jax.random.fold_in(_gk, 3), (50000,), 0, 3125, jnp.int32)
        _loop = jnp.arange(3125, dtype=jnp.int32)
        src = jnp.concatenate([_s, _d, _loop])
        dst = jnp.concatenate([_d, _s, _loop])
        _o = jnp.argsort(dst, stable=True)
        src = src[_o]
        dst = dst[_o]
        edge_type_8 = jax.random.randint(jax.random.fold_in(_gk, 13), (103125,), 0, 8, jnp.int32)
        edge_weight = jax.random.uniform(jax.random.fold_in(_gk, 14), (103125,), jnp.float32, 0.0, 0.999998)
        node_type_8 = jax.random.randint(jax.random.fold_in(_gk, 15), (3125,), 0, 8, jnp.int32)
        return (x, src, dst, edge_type_8, edge_weight, node_type_8)
    x, src, dst, edge_type_8, edge_weight, node_type_8 = _rec_inputs()

    def _L0_gnn_setup():
        import jax, jax.numpy as jnp
        import numpy as np
        N = 6250
        D = 128
        E = 37500
        key = jax.random.key(seed)
        k = jax.random.split(key, 7)
        x = jax.random.normal(k[0], (N, D), dtype=jnp.float32)
        edge_index = jax.random.randint(k[1], (2, E), 0, N, dtype=jnp.int32)
        edge_weight = jax.random.uniform(k[2], (E,), dtype=jnp.float32)
        s = 1.0 / np.sqrt(D)
        W1 = jax.random.uniform(k[3], (D, D), minval=-s, maxval=s, dtype=jnp.float32)
        b1 = jax.random.uniform(k[4], (D,), minval=-s, maxval=s, dtype=jnp.float32)
        W2 = jax.random.uniform(k[5], (D, D), minval=-s, maxval=s, dtype=jnp.float32)
        b2 = jax.random.uniform(k[6], (D,), minval=-s, maxval=s, dtype=jnp.float32)
        return {'x': x, 'edge_index': edge_index, 'edge_weight': edge_weight, 'W1': W1, 'b1': b1, 'W2': W2, 'b2': b2}
    _L0_gnn_all = _L0_gnn_setup()
    _L0_gnn_in = {k: v for k, v in _L0_gnn_all.items() if k in ('W1', 'b1', 'W2', 'b2')}
    del _L0_gnn_all

    def _L1_gnn_setup():
        import jax, jax.numpy as jnp
        import numpy as np
        N, IN, H, D = (3125, 128, 4, 32)
        HID = H * D
        E = 50000
        key = jax.random.key(seed)
        ks = jax.random.split(key, 16)
        s_in = 1.0 / np.sqrt(IN)
        s_g = 1.0 / np.sqrt(3 * HID)
        inp = {'feat': jax.random.normal(ks[0], (N, IN), jnp.float32), 'src': jax.random.randint(ks[1], (E,), 0, N, jnp.int32), 'dst': jax.random.randint(ks[2], (E,), 0, N, jnp.int32), 'Wq': jax.random.normal(ks[3], (IN, HID), jnp.float32) * s_in, 'bq': jnp.zeros((HID,), jnp.float32), 'Wk': jax.random.normal(ks[4], (IN, HID), jnp.float32) * s_in, 'bk': jnp.zeros((HID,), jnp.float32), 'Wv': jax.random.normal(ks[5], (IN, HID), jnp.float32) * s_in, 'bv': jnp.zeros((HID,), jnp.float32), 'Ws': jax.random.normal(ks[6], (IN, HID), jnp.float32) * s_in, 'bs': jnp.zeros((HID,), jnp.float32), 'Wg': jax.random.normal(ks[7], (3 * HID, 1), jnp.float32) * s_g, 'bg': jnp.zeros((1,), jnp.float32), 'gamma': jnp.ones((HID,), jnp.float32), 'beta': jnp.zeros((HID,), jnp.float32), 'alpha': jnp.asarray(0.25, jnp.float32)}
        return inp
    _L1_gnn_all = _L1_gnn_setup()
    _L1_gnn_in = {k: v for k, v in _L1_gnn_all.items() if k in ('Wq', 'bq', 'Wk', 'bk', 'Wv', 'bv', 'Ws', 'bs', 'Wg', 'bg', 'gamma', 'beta', 'alpha')}
    del _L1_gnn_all

    def _L2_gnn_setup():
        import jax, jax.numpy as jnp
        import numpy as np
        N, D, E = (3125, 128, 50000)
        NEG_SLOPE = 0.2

        def gatv2(x, src, dst, Wl, bl, Wr, br, att, bias, heads, out_ch):
            n = x.shape[0]
            xl = (x @ Wl + bl).reshape(n, heads, out_ch)
            xr = (x @ Wr + br).reshape(n, heads, out_ch)
            e = jax.nn.leaky_relu(xl[src] + xr[dst], NEG_SLOPE)
            score = jnp.einsum('ehc,hc->eh', e, att)
            smax = jax.ops.segment_max(score, dst, num_segments=n)
            ex = jnp.exp(score - smax[dst])
            denom = jax.ops.segment_sum(ex, dst, num_segments=n)
            alpha = ex / (denom[dst] + 1e-16)
            out = jax.ops.segment_sum(xl[src] * alpha[:, :, None], dst, num_segments=n)
            return out.reshape(n, heads * out_ch) + bias
        key = jax.random.key(seed)
        ks = jax.random.split(key, 16)
        src = jax.random.randint(ks[0], (E,), 0, N)
        dst = jax.random.randint(ks[1], (E,), 0, N)
        dst = jnp.where(src == dst, (dst + 1) % N, dst)
        edge_index = jnp.stack([src, dst]).astype(jnp.int32)
        s = 1.0 / np.sqrt(D)
        return {'edge_index': edge_index, 'embed': jax.random.normal(ks[2], (N, D), jnp.float32), 'Wl1': jax.random.normal(ks[3], (D, D), jnp.float32) * s, 'bl1': jnp.zeros((D,), jnp.float32), 'Wr1': jax.random.normal(ks[4], (D, D), jnp.float32) * s, 'br1': jnp.zeros((D,), jnp.float32), 'att1': jax.random.normal(ks[5], (4, D // 4), jnp.float32) * s, 'b1': jnp.zeros((D,), jnp.float32), 'Wl2': jax.random.normal(ks[6], (D, D), jnp.float32) * s, 'bl2': jnp.zeros((D,), jnp.float32), 'Wr2': jax.random.normal(ks[7], (D, D), jnp.float32) * s, 'br2': jnp.zeros((D,), jnp.float32), 'att2': jax.random.normal(ks[8], (1, D), jnp.float32) * s, 'b2': jnp.zeros((D,), jnp.float32)}
    _L2_gnn_all = _L2_gnn_setup()
    _L2_gnn_in = {k: v for k, v in _L2_gnn_all.items() if k in ('Wl1', 'bl1', 'Wr1', 'br1', 'att1', 'b1', 'Wl2', 'bl2', 'Wr2', 'br2', 'att2', 'b2')}
    del _L2_gnn_all

    def _L3_gnn_setup():
        import jax, jax.numpy as jnp
        import numpy as np
        N = 3125
        E = 25000
        HID = 128
        H = 8
        HS = HID // H
        TN = 8
        R = 8
        L = 2
        OUT = 128
        EPS = 1e-05
        SQRT_D = float(np.sqrt(HS))

        def typed_linear(x, types, W):
            out = jnp.zeros((x.shape[0], W.shape[-1]), x.dtype)
            for t in range(W.shape[0]):
                out = out + jnp.where((types == t)[:, None], x @ W[t], 0.0)
            return out

        def rel_apply(h, etype, W):
            out = jnp.zeros_like(h)
            for r in range(W.shape[1]):
                out = out + jnp.where((etype == r)[:, None, None], jnp.einsum('ehi,hio->eho', h, W[:, r]), 0.0)
            return out

        def gt_layer(x, src, dst, ntype, etype, Wk, Wq, Wv, Wa, pri, Watt, Wmsg, skip, g, b):
            n = x.shape[0]
            k = typed_linear(x, ntype, Wk).reshape(n, H, HS)
            q = typed_linear(x, ntype, Wq).reshape(n, H, HS)
            v = typed_linear(x, ntype, Wv).reshape(n, H, HS)
            k_j, q_i, v_j = (k[src], q[dst], v[src])
            kw = rel_apply(k_j, etype, Watt)
            a = (kw * q_i).sum(-1) * pri[:, etype].T / SQRT_D
            amax = jax.ops.segment_max(a, dst, num_segments=n)
            ex = jnp.exp(a - amax[dst])
            den = jax.ops.segment_sum(ex, dst, num_segments=n)
            alpha = ex / (den[dst] + 1e-16)
            m = rel_apply(v_j, etype, Wmsg)
            agg = jax.ops.segment_sum(alpha[..., None] * m, dst, num_segments=n)
            out = jax.nn.silu(typed_linear(agg.reshape(n, HID), ntype, Wa))
            al = jax.nn.sigmoid(skip[ntype])[:, None]
            out = out * al + x * (1.0 - al)
            mu = out.mean(-1, keepdims=True)
            var = ((out - mu) ** 2).mean(-1, keepdims=True)
            return (out - mu) / jnp.sqrt(var + EPS) * g + b
        key = jax.random.key(seed)
        ks = jax.random.split(key, 12)
        s = 1.0 / np.sqrt(HID)
        sh = 1.0 / np.sqrt(HS)
        return {'x': jax.random.normal(ks[0], (N, HID), jnp.float32), 'edge_index': jax.random.randint(ks[1], (2, E), 0, N, dtype=jnp.int32), 'ntype': jax.random.randint(ks[2], (N,), 0, TN, dtype=jnp.int32), 'etype': jax.random.randint(ks[3], (E,), 0, R, dtype=jnp.int32), 'Wk': jax.random.normal(ks[4], (L, TN, HID, HID), jnp.float32) * s, 'Wq': jax.random.normal(ks[5], (L, TN, HID, HID), jnp.float32) * s, 'Wv': jax.random.normal(ks[6], (L, TN, HID, HID), jnp.float32) * s, 'Wa': jax.random.normal(ks[7], (L, TN, HID, HID), jnp.float32) * s, 'pri': jnp.ones((L, H, R), jnp.float32), 'Watt': jax.random.normal(ks[8], (L, H, R, HS, HS), jnp.float32) * sh, 'Wmsg': jax.random.normal(ks[9], (L, H, R, HS, HS), jnp.float32) * sh, 'skip': jnp.ones((L, TN), jnp.float32), 'ln_g': jnp.ones((L, HID), jnp.float32), 'ln_b': jnp.zeros((L, HID), jnp.float32), 'Wff': jax.random.normal(ks[10], (HID, OUT), jnp.float32) * s, 'bff': jnp.zeros((OUT,), jnp.float32)}
    _L3_gnn_all = _L3_gnn_setup()
    _L3_gnn_in = {k: v for k, v in _L3_gnn_all.items() if k in ('Wk', 'Wq', 'Wv', 'Wa', 'pri', 'Watt', 'Wmsg', 'skip', 'ln_g', 'ln_b', 'Wff', 'bff')}
    del _L3_gnn_all
    return {'x': x, 'src': src, 'dst': dst, 'edge_type_8': edge_type_8, 'edge_weight': edge_weight, 'node_type_8': node_type_8, 'L0_gnn_W1': _L0_gnn_in['W1'], 'L0_gnn_b1': _L0_gnn_in['b1'], 'L0_gnn_W2': _L0_gnn_in['W2'], 'L0_gnn_b2': _L0_gnn_in['b2'], 'L1_gnn_Wq': _L1_gnn_in['Wq'], 'L1_gnn_bq': _L1_gnn_in['bq'], 'L1_gnn_Wk': _L1_gnn_in['Wk'], 'L1_gnn_bk': _L1_gnn_in['bk'], 'L1_gnn_Wv': _L1_gnn_in['Wv'], 'L1_gnn_bv': _L1_gnn_in['bv'], 'L1_gnn_Ws': _L1_gnn_in['Ws'], 'L1_gnn_bs': _L1_gnn_in['bs'], 'L1_gnn_Wg': _L1_gnn_in['Wg'], 'L1_gnn_bg': _L1_gnn_in['bg'], 'L1_gnn_gamma': _L1_gnn_in['gamma'], 'L1_gnn_beta': _L1_gnn_in['beta'], 'L1_gnn_alpha': _L1_gnn_in['alpha'], 'L2_gnn_Wl1': _L2_gnn_in['Wl1'], 'L2_gnn_bl1': _L2_gnn_in['bl1'], 'L2_gnn_Wr1': _L2_gnn_in['Wr1'], 'L2_gnn_br1': _L2_gnn_in['br1'], 'L2_gnn_att1': _L2_gnn_in['att1'], 'L2_gnn_b1': _L2_gnn_in['b1'], 'L2_gnn_Wl2': _L2_gnn_in['Wl2'], 'L2_gnn_bl2': _L2_gnn_in['bl2'], 'L2_gnn_Wr2': _L2_gnn_in['Wr2'], 'L2_gnn_br2': _L2_gnn_in['br2'], 'L2_gnn_att2': _L2_gnn_in['att2'], 'L2_gnn_b2': _L2_gnn_in['b2'], 'L3_gnn_Wk': _L3_gnn_in['Wk'], 'L3_gnn_Wq': _L3_gnn_in['Wq'], 'L3_gnn_Wv': _L3_gnn_in['Wv'], 'L3_gnn_Wa': _L3_gnn_in['Wa'], 'L3_gnn_pri': _L3_gnn_in['pri'], 'L3_gnn_Watt': _L3_gnn_in['Watt'], 'L3_gnn_Wmsg': _L3_gnn_in['Wmsg'], 'L3_gnn_skip': _L3_gnn_in['skip'], 'L3_gnn_ln_g': _L3_gnn_in['ln_g'], 'L3_gnn_ln_b': _L3_gnn_in['ln_b'], 'L3_gnn_Wff': _L3_gnn_in['Wff'], 'L3_gnn_bff': _L3_gnn_in['bff']}

def reference(x, src, dst, edge_type_8, edge_weight, node_type_8, L0_gnn_W1, L0_gnn_b1, L0_gnn_W2, L0_gnn_b2, L1_gnn_Wq, L1_gnn_bq, L1_gnn_Wk, L1_gnn_bk, L1_gnn_Wv, L1_gnn_bv, L1_gnn_Ws, L1_gnn_bs, L1_gnn_Wg, L1_gnn_bg, L1_gnn_gamma, L1_gnn_beta, L1_gnn_alpha, L2_gnn_Wl1, L2_gnn_bl1, L2_gnn_Wr1, L2_gnn_br1, L2_gnn_att1, L2_gnn_b1, L2_gnn_Wl2, L2_gnn_bl2, L2_gnn_Wr2, L2_gnn_br2, L2_gnn_att2, L2_gnn_b2, L3_gnn_Wk, L3_gnn_Wq, L3_gnn_Wv, L3_gnn_Wa, L3_gnn_pri, L3_gnn_Watt, L3_gnn_Wmsg, L3_gnn_skip, L3_gnn_ln_g, L3_gnn_ln_b, L3_gnn_Wff, L3_gnn_bff):
    import jax
    import jax.numpy as jnp

    def _L0_gnn_ref(x, edge_index, edge_weight, W1, b1, W2, b2):
        import jax, jax.numpy as jnp
        import numpy as np
        N = 6250
        D = 128
        E = 37500
        row, col = (edge_index[0], edge_index[1])
        msgs = edge_weight[:, None] * x[row]
        agg = jax.ops.segment_sum(msgs, col, num_segments=x.shape[0])
        h = (agg + x) @ W1.T + b1 + agg * x @ W2.T + b2
        out = jax.nn.leaky_relu(h, negative_slope=0.2)
        return out

    def _L1_gnn_ref(feat, src, dst, Wq, bq, Wk, bk, Wv, bv, Ws, bs, Wg, bg, gamma, beta, alpha):
        import jax, jax.numpy as jnp
        import numpy as np
        N, IN, H, D = (3125, 128, 4, 32)
        HID = H * D
        E = 50000
        n = feat.shape[0]
        q = (feat @ Wq + bq).reshape(n, H, D)
        k = (feat @ Wk + bk).reshape(n, H, D)
        v = (feat @ Wv + bv).reshape(n, H, D)
        a = jnp.einsum('ehd,ehd->eh', q[src], k[dst]) / jnp.sqrt(jnp.float32(D))
        m = jax.ops.segment_max(a, dst, num_segments=n)
        m = jax.lax.stop_gradient(jnp.where(jnp.isfinite(m), m, 0.0))
        ex = jnp.exp(a - m[dst])
        denom = jax.ops.segment_sum(ex, dst, num_segments=n)
        denom = jnp.where(denom > 0, denom, 1.0)
        sa = ex / denom[dst]
        msg = v[src] * sa[:, :, None]
        agg = jax.ops.segment_sum(msg, dst, num_segments=n).reshape(n, HID)
        skip = feat @ Ws + bs
        g = jax.nn.sigmoid(jnp.concatenate([skip, agg, skip - agg], axis=-1) @ Wg + bg)
        rst = g * skip + (1.0 - g) * agg
        mu = rst.mean(-1, keepdims=True)
        var = rst.var(-1, keepdims=True)
        rst = (rst - mu) * jax.lax.rsqrt(var + 1e-05) * gamma + beta
        rst = jnp.where(rst >= 0, rst, alpha * rst)
        return rst

    def _L2_gnn_ref(edge_index, embed, Wl1, bl1, Wr1, br1, att1, b1, Wl2, bl2, Wr2, br2, att2, b2):
        import jax, jax.numpy as jnp
        import numpy as np
        N, D, E = (3125, 128, 50000)
        NEG_SLOPE = 0.2

        def gatv2(x, src, dst, Wl, bl, Wr, br, att, bias, heads, out_ch):
            n = x.shape[0]
            xl = (x @ Wl + bl).reshape(n, heads, out_ch)
            xr = (x @ Wr + br).reshape(n, heads, out_ch)
            e = jax.nn.leaky_relu(xl[src] + xr[dst], NEG_SLOPE)
            score = jnp.einsum('ehc,hc->eh', e, att)
            smax = jax.ops.segment_max(score, dst, num_segments=n)
            ex = jnp.exp(score - smax[dst])
            denom = jax.ops.segment_sum(ex, dst, num_segments=n)
            alpha = ex / (denom[dst] + 1e-16)
            out = jax.ops.segment_sum(xl[src] * alpha[:, :, None], dst, num_segments=n)
            return out.reshape(n, heads * out_ch) + bias
        loops = jnp.arange(N, dtype=edge_index.dtype)
        src = jnp.concatenate([edge_index[0], loops])
        dst = jnp.concatenate([edge_index[1], loops])
        x = gatv2(embed, src, dst, Wl1, bl1, Wr1, br1, att1, b1, 4, D // 4)
        x = jax.nn.relu(x)
        return gatv2(x, src, dst, Wl2, bl2, Wr2, br2, att2, b2, 1, D)

    def _L3_gnn_ref(x, edge_index, ntype, etype, Wk, Wq, Wv, Wa, pri, Watt, Wmsg, skip, ln_g, ln_b, Wff, bff):
        import jax, jax.numpy as jnp
        import numpy as np
        N = 3125
        E = 25000
        HID = 128
        H = 8
        HS = HID // H
        TN = 8
        R = 8
        L = 2
        OUT = 128
        EPS = 1e-05
        SQRT_D = float(np.sqrt(HS))

        def typed_linear(x, types, W):
            out = jnp.zeros((x.shape[0], W.shape[-1]), x.dtype)
            for t in range(W.shape[0]):
                out = out + jnp.where((types == t)[:, None], x @ W[t], 0.0)
            return out

        def rel_apply(h, etype, W):
            out = jnp.zeros_like(h)
            for r in range(W.shape[1]):
                out = out + jnp.where((etype == r)[:, None, None], jnp.einsum('ehi,hio->eho', h, W[:, r]), 0.0)
            return out

        def gt_layer(x, src, dst, ntype, etype, Wk, Wq, Wv, Wa, pri, Watt, Wmsg, skip, g, b):
            n = x.shape[0]
            k = typed_linear(x, ntype, Wk).reshape(n, H, HS)
            q = typed_linear(x, ntype, Wq).reshape(n, H, HS)
            v = typed_linear(x, ntype, Wv).reshape(n, H, HS)
            k_j, q_i, v_j = (k[src], q[dst], v[src])
            kw = rel_apply(k_j, etype, Watt)
            a = (kw * q_i).sum(-1) * pri[:, etype].T / SQRT_D
            amax = jax.ops.segment_max(a, dst, num_segments=n)
            ex = jnp.exp(a - amax[dst])
            den = jax.ops.segment_sum(ex, dst, num_segments=n)
            alpha = ex / (den[dst] + 1e-16)
            m = rel_apply(v_j, etype, Wmsg)
            agg = jax.ops.segment_sum(alpha[..., None] * m, dst, num_segments=n)
            out = jax.nn.silu(typed_linear(agg.reshape(n, HID), ntype, Wa))
            al = jax.nn.sigmoid(skip[ntype])[:, None]
            out = out * al + x * (1.0 - al)
            mu = out.mean(-1, keepdims=True)
            var = ((out - mu) ** 2).mean(-1, keepdims=True)
            return (out - mu) / jnp.sqrt(var + EPS) * g + b
        src, dst = (edge_index[0], edge_index[1])
        emb = x
        for l in range(L):
            emb = gt_layer(emb, src, dst, ntype, etype, Wk[l], Wq[l], Wv[l], Wa[l], pri[l], Watt[l], Wmsg[l], skip[l], ln_g[l], ln_b[l])
        return emb @ Wff + bff
    edge_index = jnp.stack([src, dst])
    h = jnp.maximum(_layernorm(x, axis=-1), 0.0)
    x = x + _L0_gnn_ref(h, edge_index, edge_weight, L0_gnn_W1, L0_gnn_b1, L0_gnn_W2, L0_gnn_b2)
    h = jnp.maximum(_layernorm(x, axis=-1), 0.0)
    x = x + _L1_gnn_ref(h, src, dst, L1_gnn_Wq, L1_gnn_bq, L1_gnn_Wk, L1_gnn_bk, L1_gnn_Wv, L1_gnn_bv, L1_gnn_Ws, L1_gnn_bs, L1_gnn_Wg, L1_gnn_bg, L1_gnn_gamma, L1_gnn_beta, L1_gnn_alpha)
    h = jnp.maximum(_layernorm(x, axis=-1), 0.0)
    x = x + _L2_gnn_ref(edge_index, h, L2_gnn_Wl1, L2_gnn_bl1, L2_gnn_Wr1, L2_gnn_br1, L2_gnn_att1, L2_gnn_b1, L2_gnn_Wl2, L2_gnn_bl2, L2_gnn_Wr2, L2_gnn_br2, L2_gnn_att2, L2_gnn_b2)
    h = jnp.maximum(_layernorm(x, axis=-1), 0.0)
    x = x + _L3_gnn_ref(h, edge_index, node_type_8, edge_type_8, L3_gnn_Wk, L3_gnn_Wq, L3_gnn_Wv, L3_gnn_Wa, L3_gnn_pri, L3_gnn_Watt, L3_gnn_Wmsg, L3_gnn_skip, L3_gnn_ln_g, L3_gnn_ln_b, L3_gnn_Wff, L3_gnn_bff)
    return x

_drawn_inputs = setup_inputs


def setup_inputs(seed=0):
    import zlib

    import numpy as np

    out = dict(_drawn_inputs(seed))
    spreads = {'L1_gnn_bq': (0.0, 2.0),
     'L1_gnn_bk': (0.0, 0.8),
     'L1_gnn_bv': (0.0, 0.275),
     'L1_gnn_bs': (0.0, 0.7),
     'L1_gnn_gamma': (1.0, 0.2),
     'L1_gnn_beta': (0.0, 0.342),
     'L2_gnn_bl1': (0.0, 0.321),
     'L2_gnn_br1': (0.0, 2.0),
     'L2_gnn_b1': (0.0, 0.393),
     'L2_gnn_bl2': (0.0, 0.296),
     'L2_gnn_br2': (0.0, 2.0),
     'L2_gnn_b2': (0.0, 0.315),
     'L3_gnn_pri': (1.0, 0.2),
     'L3_gnn_skip': (1.0, 0.584),
     'L3_gnn_ln_g': (1.0, 0.2),
     'L3_gnn_ln_b': (0.0, 0.1),
     'L3_gnn_bff': (0.0, 0.295)}
    factors = {'L0_gnn_b1': 5.328,
     'L0_gnn_b2': 5.453,
     'L1_gnn_Wq': 3.49,
     'L1_gnn_Wk': 3.365,
     'L2_gnn_Wr1': 25.838,
     'L2_gnn_att1': 8.0,
     'L2_gnn_Wr2': 54.859,
     'L2_gnn_att2': 34.752}
    for name, (base, spread) in spreads.items():
        noise = np.random.default_rng([zlib.crc32(name.encode()), seed]).standard_normal(out[name].shape)
        drawn = base * np.exp(spread * noise) if base else spread * noise
        out[name] = jnp.asarray(drawn.astype(out[name].dtype))
    for name, factor in factors.items():
        out[name] = (out[name] * factor).astype(out[name].dtype)
    return out
```

```python
from contextlib import ExitStack

import numpy as np

import concourse.bass as bass
from concourse import mybir

F32 = mybir.dt.float32
I32 = mybir.dt.int32
ALU = mybir.AluOpType
ACT = mybir.ActivationFunctionType
AX = mybir.AxisListType.X

P = 128
N = 3125
D = 128
E = 103125
NB = (N + P - 1) // P
NPAD = NB * P
NLAST = N - (NB - 1) * P
EPC = (E + P - 1) // P
ELAST = E - (P - 1) * EPC
GC = 4
CE = GC * P
J = 4
GT = GC * J
NC_MAX = (E + NB * (CE - 1)) // CE
NG = (NC_MAX + J - 1) // J
NV = NG * J
HALF = NV // 2
NT = NV * GC
PAD_ROWS = 8 * P
EPAD = P * EPC + PAD_ROWS
NO_NODE = 4000.0
BIG = 1.0e30
TYPES = 8
RELS = 8
L3H = 8
HS3 = D // L3H


MERGE_STEPS = 2 + 3 * J + 2 + 1 + 2 * J


def bc(ap, n):
    return ap.unsqueeze(len(ap.shape)).to_broadcast(list(ap.shape) + [n])


class Shared:
    pass


class Chain:

    def __init__(self, sem):
        self.sem, self.n = sem, 0

    def step(self, eng, ins):
        self.n += 1
        ins.then_inc(self.sem, 1)
        eng.wait_ge(self.sem, self.n)


class Signal:

    def __init__(self, sem, per_pass):
        self.sem, self.per_pass = sem, per_pass

    def wait(self, eng, pass_no, n):
        if isinstance(n, int) and pass_no * self.per_pass + n <= 0:
            return
        eng.wait_ge(self.sem, n + pass_no * self.per_pass)


def over_blocks(eng, body):
    body(0, 0, True)
    body(1, 1, True)
    with eng.Fori(0, (NB - 3) // 2) as i:
        body(2 * i + 2, 0, False)
        body(2 * i + 3, 1, False)
    body(NB - 1, 0, False)


def build(nc, A, out):
    st = ExitStack()
    with st:
        def sb(name, shape, dt=F32):
            return st.enter_context(nc.sbuf_tensor(name, shape, dt))[tuple(slice(None) for _ in shape)]

        def sem(name):
            return st.enter_context(nc.semaphore(name))

        def table(name, shape, dt=F32):
            return nc.dram_tensor(name, shape, dt, kind="Internal").ap()

        edges_d = table("edges_sorted", (EPAD, 4), I32)
        seg_d = table("segment_flags", (NV, CE + 4))
        t0_d = table("table_l0", (NPAD, D))
        t1_d = table("table_l1", (NPAD, 2 * D))
        t2_d = table("table_l2", (NPAD, D))
        t3_d = table("table_l3", (NPAD * RELS, 2 * D))

        xN = sb("x_nodes", [P, NB, D])
        hN = sb("h_nodes", [P, NB, D])
        kN = sb("dst_side", [P, NB, D])
        acc = sb("acc", [P, NB * 136])
        mx = sb("running_max", [P, NB * 8])
        srcE = sb("src_edges", [P, NT], I32)
        relE = sb("src_rel_edges", [P, NT], I32)
        ewE = sb("weight_edges", [P, NT])
        dlE = sb("dst_local_edges", [P, NT])
        lastE = sb("last_of_segment", [P, NT])
        blkI = sb("chunk_block", [P, NV], I32)
        startI = sb("chunk_start", [P, NV], I32)
        ident = sb("ident", [P, P])
        iotaF = sb("iota_row", [P, P])
        onesF = sb("ones", [P, P])
        typeM = sb("type_mask", [P, NB, TYPES])
        wts = sb("weights", [P, 6288])
        small = sb("small", [P, 512])
        rows = sb("gathered_rows", [P, 2, GT * 2 * D])
        oh = sb("onehot", [P, 2, GT, P])
        ohT = sb("onehot_t", [P, 2, CE])
        prod = sb("products", [P, 2, CE])
        exv = sb("weighted_rows", [P, GT * 144])
        segF = sb("segment_flags_sb", [32, 2, CE + 4])
        segS = sb("segment_work", [32, 2, CE])
        exT = sb("exp_scores_t", [32, CE])
        sc = sb("scores", [P, 2, J * GC * 8])
        exb = sb("exps_and_maxima", [P, 2 * J * GC * 8])
        idx = sb("gather_index", [P, 2, GT], I32)
        ps = st.enter_context(nc.psum_tensor("ps", [P, 8, 512], F32))

        rflat = rows[:, :, :].rearrange("p u n -> p (u n)")
        tA = rflat[:, 0:NB * D].rearrange("p (b d) -> p b d", d=D)
        tB = rflat[:, NB * D:2 * NB * D].rearrange("p (b d) -> p b d", d=D)
        tC = oh[:, :, :, :].rearrange("p u t n -> p (u t n)")[:, 0:NB * D].rearrange("p (b d) -> p b d", d=D)
        skN = wts[:, 3072:3072 + NB * D].rearrange("p (b d) -> p b d", d=D)

        tP = sb("scaled_partial", [P, J * 136])
        mwork = sb("max_work", [P, 8, J * 8])
        vecs = sb("vectors", [P, 1024])
        r_at = sb("row_scalars", [P, 8 * 32])

        rows_here = [[Signal(sem(f"rows_here_{u}{j}"), 64 * ((NG + 1 - u) // 2)) for j in range(J)] for u in range(2)]
        gate = sem("gate")
        idx_ready = Signal(sem("idx_ready"), NG)
        oh_ready = Signal(sem("onehot_ready"), NV)
        p_ready = Signal(sem("partial_ready"), NV)
        added = Signal(sem("partial_added"), NV)
        flags_here = [Signal(sem(f"flags_here_{u}"), 16 * J * ((NG + 1 - u) // 2)) for u in range(2)]
        oht_made = Signal(sem("onehot_t_in_psum"), NV)
        oht_ready = Signal(sem("onehot_t_ready"), NV)
        kd_ready = Signal(sem("dst_rows_ready"), NV)
        lr_ready = Signal(sem("pair_sums_in_sbuf"), NV)
        leaky_done = Signal(sem("leaky_done"), NV)
        prod_ready = Signal(sem("product_ready"), NV)
        score_ready = Signal(sem("score_ready"), NV)
        st_ready = Signal(sem("scores_t_ready"), NG)
        scan_step = Signal(sem("scan_step"), 2 * NG)
        seg_ready = Signal(sem("segment_max_ready"), NG)
        ex_ready = Signal(sem("exp_ready"), NG)
        back_ready = Signal(sem("exp_back_ready"), NG)
        exb_ready = Signal(sem("exp_in_sbuf"), NG)
        exv_ready = Signal(sem("weighted_rows_ready"), NV)
        excol_ready = Signal(sem("exp_columns_ready"), NG)
        merge_step = Signal(sem("merge_step"), MERGE_STEPS * NG)
        d2_ready = Signal(sem("shift_ready"), NG)
        e2_ready = Signal(sem("shift_exp_ready"), NG)
        merged = Signal(sem("merged"), NG)

        env = Shared()
        env.acc, env.added, env.back_ready, env.blkI, env.d2_ready = acc, added, back_ready, blkI, d2_ready
        env.dlE, env.e2_ready, env.edges_d, env.ewE, env.exT = dlE, e2_ready, edges_d, ewE, exT
        env.ex_ready, env.exb, env.exb_ready, env.excol_ready, env.exv = ex_ready, exb, exb_ready, excol_ready, exv
        env.exv_ready, env.flags_here, env.gate, env.hN, env.ident = exv_ready, flags_here, gate, hN, ident
        env.idx, env.idx_ready, env.iotaF, env.kN, env.kd_ready = idx, idx_ready, iotaF, kN, kd_ready
        env.lastE, env.leaky_done, env.lr_ready, env.merge_step, env.merged = lastE, leaky_done, lr_ready, merge_step, merged
        env.mwork, env.mx, env.nc, env.oh, env.ohT = mwork, mx, nc, oh, ohT
        env.oh_ready, env.oht_made, env.oht_ready, env.onesF, env.p_ready = oh_ready, oht_made, oht_ready, onesF, p_ready
        env.prod, env.prod_ready, env.ps, env.r_at, env.relE = prod, prod_ready, ps, r_at, relE
        env.rflat, env.rows, env.rows_here, env.sc, env.scan_step = rflat, rows, rows_here, sc, scan_step
        env.score_ready, env.segF, env.segS, env.seg_d, env.seg_ready = score_ready, segF, segS, seg_d, seg_ready
        env.sem, env.skN, env.small, env.srcE, env.st_ready = sem, skN, small, srcE, st_ready
        env.startI, env.t0_d, env.t1_d, env.t2_d, env.t3_d = startI, t0_d, t1_d, t2_d, t3_d
        env.tA, env.tB, env.tC, env.tP, env.table = tA, tB, tC, tP, table
        env.typeM, env.vecs, env.wts, env.xN = typeM, vecs, wts, xN
        prepare(nc, A, env)
        first_norm(nc, A, env)
        weighted_pass(nc, env)
        after_l0(nc, A, env)
        attention_pass(nc, env, 1, H=4, table=t1_d, width=2 * D, index=srcE, scale=32 ** -0.5, gat=False)
        after_l1(nc, A, env)
        attention_pass(nc, env, 2, H=4, table=t2_d, width=D, index=srcE, scale=1.0, gat=True)
        after_l2a(nc, A, env)
        attention_pass(nc, env, 3, H=1, table=t2_d, width=D, index=srcE, scale=1.0, gat=True)
        after_l2b(nc, A, env)
        attention_pass(nc, env, 4, H=L3H, table=t3_d, width=2 * D, index=relE, scale=1.0, gat=False)
        after_l3(nc, A, env, 0, out)
        attention_pass(nc, env, 5, H=L3H, table=t3_d, width=2 * D, index=relE, scale=1.0, gat=False)
        after_l3(nc, A, env, 1, out)
    return nc


def prepare(nc, A, e):
    sem = e.sem
    rflat, oh, small, ps = e.rflat, e.oh, e.small, e.ps
    ident, iotaF, onesF = e.ident, e.iotaF, e.onesF
    edges_d, xN = e.edges_d, e.xN
    V = nc.vector
    pay = rflat[:, 0:4 * EPC].rearrange("p (c f) -> p c f", f=4)
    tail = rflat[:, 4 * EPC:4 * EPC + 4 * (PAD_ROWS // P)].rearrange("p (c f) -> p c f", f=4)
    dstF = rflat[:, 4000:4000 + EPC]
    scratch = rflat[:, 5000:5000 + EPC]
    ohf = oh[:, :, :, :].rearrange("p u t n -> p (u t n)")
    raw = [ohf[:, f * EPC:(f + 1) * EPC] for f in range(4)]
    names = ["src", "dst", "edge_type_8", "edge_weight"]
    loaded, zeroed, consts, built, stored, checked, check_sum, nodes_in = (sem(n) for n in (
        "edges_loaded", "pads_zeroed", "consts_made", "payload_built", "payload_stored", "order_checked",
        "order_summed", "nodes_loaded"))
    ntI = small[:, 160:192].bitcast(I32)
    nextI = small[:, 262:263].bitcast(I32)
    nextF = small[:, 263:264]
    bad = small[:, 264:266]
    flagI = small[:, 266:267].bitcast(I32)
    chain = Chain(sem("prepare_step"))

    with nc.Block() as block:
        @block.gpsimd
        def _(pool):
            pool.memset(ident[:, :], 0.0).then_inc(consts, 1)
            pool.memset(onesF[:, :], 1.0).then_inc(consts, 1)
            pool.wait_ge(consts, 2)
            pool.affine_select(out=ident[:, :], in_=ident[:, :], compare_op=ALU.not_equal, fill=1.0,
                               base=0, pattern=[[-1, P]], channel_multiplier=1).then_inc(consts, 1)
            pool.iota(iotaF[:, :].bitcast(I32), pattern=[[1, P]], base=0, channel_multiplier=0).then_inc(consts, 1)

        @block.sync
        def _(sp):
            sp.wait_ge(zeroed, 7)
            for f, name in enumerate(names):
                dst = raw[f] if name == "edge_weight" else raw[f].bitcast(I32)
                a = A[name]
                sp.dma_start(dst[0:P - 1, :], a[0:(P - 1) * EPC].rearrange("(p c) -> p c", c=EPC)).then_inc(loaded, 16)
                sp.dma_start(dst[P - 1:P, 0:ELAST], a[(P - 1) * EPC:E].rearrange("(p c) -> p c", c=ELAST)).then_inc(loaded, 16)
            with nc.allow_non_contiguous_dma(reason="one destination a partition"):
                firsts = A["dst"][EPC:(P - 1) * EPC].rearrange("(p c) -> p c", c=EPC)[:, 0:1]
                sp.dma_start(nextI[0:P - 2, :], firsts).then_inc(loaded, 16)
                last = A["dst"][(P - 1) * EPC:(P - 1) * EPC + 1].rearrange("(p c) -> p c", c=1)
                sp.dma_start(nextI[P - 2:P - 1, :], last).then_inc(loaded, 16)
            x = A["x"]
            sp.dma_start(xN[:, 0:NB - 1, :], x[0:(NB - 1) * P, :].rearrange("(b p) d -> p b d", p=P)).then_inc(nodes_in, 16)
            sp.dma_start(xN[0:NLAST, NB - 1, :], x[(NB - 1) * P:N, :]).then_inc(nodes_in, 16)
            t = A["node_type_8"]
            with nc.allow_non_contiguous_dma(reason="12 KB of node types"):
                sp.dma_start(ntI[:, 0:NB - 1], t[0:(NB - 1) * P].rearrange("(b p) -> p b", p=P)).then_inc(nodes_in, 16)
                sp.dma_start(ntI[0:NLAST, NB - 1:NB], t[(NB - 1) * P:N].rearrange("(p b) -> p b", b=1)).then_inc(nodes_in, 16)
            sp.wait_ge(built, 1)
            sp.dma_start(edges_d[0:P * EPC, :].rearrange("(p c) f -> p c f", p=P), pay.bitcast(I32)).then_inc(stored, 16)
            sp.dma_start(edges_d[P * EPC:EPAD, :].rearrange("(p c) f -> p c f", p=P), tail.bitcast(I32)).then_inc(stored, 16)
            sp.wait_ge(stored, 32)
            sp.wait_ge(nodes_in, 64)

        @block.vector
        def _(dve):
            c = chain
            V.memset(raw[0].bitcast(I32), 0).then_inc(zeroed, 1)
            V.memset(raw[1].bitcast(I32), int(NO_NODE)).then_inc(zeroed, 1)
            V.memset(raw[2].bitcast(I32), 0).then_inc(zeroed, 1)
            V.memset(raw[3], 0.0).then_inc(zeroed, 1)
            V.memset(xN[:, NB - 1, :], 0.0).then_inc(zeroed, 1)
            V.memset(ntI[:, 0:32], 0).then_inc(zeroed, 1)
            V.memset(nextI, int(NO_NODE)).then_inc(zeroed, 1)
            c.step(dve, V.memset(tail, 0.0))
            c.step(dve, V.memset(tail.bitcast(I32)[:, :, 1], int(NO_NODE)))
            dve.wait_ge(consts, 4)
            c.step(dve, V.tensor_copy(iotaF[:, :], iotaF[:, :].bitcast(I32)))
            dve.wait_ge(loaded, 16 * 10)
            for f in range(4):
                if names[f] == "edge_weight":
                    ins = V.tensor_copy(pay[:, :, f], raw[f])
                else:
                    ins = V.tensor_copy(pay.bitcast(I32)[:, :, f], raw[f].bitcast(I32))
            ins.then_inc(built, 1)
            c.step(dve, V.tensor_copy(dstF, raw[1].bitcast(I32)))
            c.step(dve, V.tensor_copy(nextF, nextI))
            c.step(dve, V.tensor_tensor(scratch[:, 0:EPC - 1], dstF[:, 0:EPC - 1], dstF[:, 1:EPC], ALU.is_gt))
            c.step(dve, V.tensor_reduce(bad[:, 0:1], scratch[:, 0:EPC - 1], AX, ALU.max))
            V.tensor_tensor(bad[:, 1:2], dstF[:, EPC - 1:EPC], nextF, ALU.is_gt).then_inc(checked, 1)
            dve.wait_ge(check_sum, 1)
            c.step(dve, V.tensor_reduce(nextF, ps[:, 0, 0:2], AX, ALU.max))
            c.step(dve, V.tensor_scalar(flagI, nextF, 0.5, None, ALU.is_gt))

        @block.tensor
        def _(pe):
            pe.wait_ge(consts, 2)
            pe.wait_ge(checked, 1)
            nc.tensor.matmul(ps[:, 0, 0:2], onesF[:, :], bad, start=True, stop=True).then_inc(check_sum, 1)

    out_of_order = nc.values_load(flagI[0:1, 0:1], min_val=0, max_val=1)
    with nc.If(out_of_order):
        sort_edges(nc, e, pay, dstF, scratch, edges_d)
    nc.end_ifs()
    cut_chunks(nc, e, dstF, scratch, ntI)


def sort_edges(nc, e, pay, dstF, cum, edges_d):
    sem, ps, onesF = e.sem, e.ps, e.onesF
    V = nc.vector
    mask, place, ones, term = (e.wts[:, n * EPC:(n + 1) * EPC] for n in range(4))
    placeI = e.rows[:, 1, 2048:2048 + EPC].bitcast(I32)
    s = e.small
    tri, node, base, off, total = e.oh[:, 0, 0, :], s[:, 270:271], s[:, 271:272], s[:, 272:273], s[:, 273:274]
    stage_rows = [s[:, 280 + 4 * k:284 + 4 * k].bitcast(I32) for k in range(2)]
    stage_place = [s[:, 290 + k:291 + k].bitcast(I32) for k in range(2)]
    made, set_up, step, counted, summed, placed = (sem(f"sort_{n}") for n in (
        "triangle_made", "set_up", "step", "node_counted", "node_summed", "places_made"))
    staged, gone = sem("sort_staged"), [sem("sort_gone_0"), sem("sort_gone_1")]
    PER = 9

    with nc.Block() as block:
        @block.gpsimd
        def _(pool):
            pool.memset(tri, 1.0).then_inc(made, 1)
            pool.iota(placeI, pattern=[[1, EPC]], base=0, channel_multiplier=EPC).then_inc(made, 1)
            pool.wait_ge(made, 2)
            pool.affine_select(out=tri, in_=tri, compare_op=ALU.is_gt, fill=0.0, base=0, pattern=[[1, P]],
                               channel_multiplier=-1).then_inc(made, 1)
            pool.wait_ge(placed, 1)
            with pool.Fori(0, EPC // 2) as i:
                for k in range(2):
                    pool.wait_ge(gone[k], 16 * i)
                    nc.gpsimd.tensor_copy(stage_rows[k], pay.bitcast(I32)[:, bass.ds(2 * i + k, 1), :].rearrange("p c f -> p (c f)"))
                    nc.gpsimd.tensor_copy(stage_place[k], placeI[:, bass.ds(2 * i + k, 1)]).then_inc(staged, 1)
                    pool.wait_ge(staged, 2 * i + k + 1)
                    pool.sem_inc(e.gate, 1)
                    pool.indirect_dma_start(out=edges_d, out_offset=bass.IndirectOffsetOnAxis(ap=stage_place[k], axis=0),
                                            in_=stage_rows[k], in_offset=None).then_inc(gone[k], 16)
            for k in range(2):
                pool.wait_ge(gone[k], 16 * (EPC // 2))

        @block.vector
        def _(dve):
            c = Chain(set_up)
            dve.wait_ge(made, 2)
            c.step(dve, V.tensor_copy(place, placeI))
            c.step(dve, V.tensor_scalar(term, dstF, float(N), None, ALU.is_ge))
            c.step(dve, V.tensor_tensor(place, place, term, ALU.mult))
            c.step(dve, V.memset(ones, 1.0))
            c.step(dve, V.memset(node, 0.0))
            c.step(dve, V.memset(base, -1.0))
            with dve.Fori(0, N) as i:
                n = 0

                def do(ins, wait=True):
                    nonlocal n
                    n += 1
                    ins.then_inc(step, 1)
                    if wait:
                        dve.wait_ge(step, PER * i + n)
                do(V.tensor_scalar(mask, dstF, node, None, ALU.is_equal))
                do(V.tensor_tensor_scan(cum, ones, mask, 0.0, ALU.mult, ALU.add))
                do(V.tensor_scalar(total, cum[:, EPC - 1:EPC], 1.0, None, ALU.mult))
                V.memset(s[:, 275:276], 0.0).then_inc(counted, 1)
                dve.wait_ge(summed, i + 1)
                do(V.tensor_tensor(off, base, ps[:, 0, 0:1], ALU.add))
                do(V.tensor_tensor(base, base, ps[:, 0, 1:2], ALU.add))
                do(V.scalar_tensor_tensor(term, cum, off, mask, ALU.add, ALU.mult))
                do(V.tensor_tensor(place, place, term, ALU.add))
                do(V.tensor_scalar(node, node, 1.0, None, ALU.add))
                do(V.memset(s[:, 276:277], 0.0))
                assert n == PER
            V.tensor_copy(placeI, place).then_inc(placed, 1)

        @block.sync
        def _(sp):
            sp.wait_ge(placed, 1)

        @block.scalar
        def _(act):
            act.wait_ge(placed, 1)

        @block.tensor
        def _(pe):
            pe.wait_ge(made, 3)
            with pe.Fori(0, N) as i:
                pe.wait_ge(counted, i + 1)
                nc.tensor.matmul(ps[:, 0, 0:1], tri, total, start=True, stop=True)
                nc.tensor.matmul(ps[:, 0, 1:2], onesF[:, :], total, start=True, stop=True).then_inc(summed, 1)


def cut_chunks(nc, e, dstF, scratch, ntI):
    sem = e.sem
    rflat, oh, small, ps = e.rflat, e.oh, e.small, e.ps
    ident, onesF, edges_d, seg_d, typeM = e.ident, e.onesF, e.edges_d, e.seg_d, e.typeM
    srcE, relE, ewE, dlE, lastE, blkI, startI = e.srcE, e.relE, e.ewE, e.dlE, e.lastE, e.blkI, e.startI
    V = nc.vector
    ohf = oh[:, :, :, :].rearrange("p u t n -> p (u t n)")
    consts, counted, totals, visits, meta_in, meta_cut, tposed, flagged, flags_out, back, cut = (sem(n) for n in (
        "chunk_numbers", "counts_made", "totals_made", "chunks_placed", "chunks_loaded", "chunks_cut", "dst_turned",
        "flags_made", "flags_stored", "last_back", "cut_step"))
    cnt = small[:, 0:32]
    R = small[:, 32:64]
    Cs = small[:, 64:96]
    g = small[:, 96:128]
    nci = small[:, 128:160].bitcast(I32)
    ntF = small[:, 192:224]
    t25 = small[:, 224:256]
    iotaI = ohf[:, 3300:3300 + NV].bitcast(I32)
    iotaV = ohf[:, 3530:3530 + NV]
    blkF = ohf[:, 3760:3760 + NV]
    meta = rflat[:, 0:NV * 16].bitcast(I32).rearrange("p (v g f) -> p v g f", g=GC, f=4)
    startF = rflat[:, 6000:6000 + NV]
    geF = rflat[:, 6300:6300 + NV]
    relF = rflat[:, 4000:4000 + NT]
    dT = [ohf[:, h * 1040:h * 1040 + CE] for h in range(2)]
    fT = [ohf[:, 520 + h * 1040:520 + h * 1040 + CE + 4] for h in range(2)]

    with nc.Block() as block:
        @block.gpsimd
        def _(pool):
            pool.iota(iotaI, pattern=[[1, NV]], base=0, channel_multiplier=0).then_inc(consts, 1)

        @block.sync
        def _(sp):
            sp.wait_ge(visits, 1)
            with sp.Fori(0, NV // 2) as i:
                s = sp.value_load(startI[0:1, bass.ds(2 * i, 1)], min_val=0, max_val=E)
                sp.dma_start(meta[:, bass.ds(2 * i, 1), :, :].rearrange("p v g f -> p (v g f)"),
                             edges_d[bass.ds(s, CE), :].rearrange("(p g) f -> p (g f)", g=GC)).then_inc(meta_in, 16)
            for h in range(2):
                sp.wait_ge(flagged, h + 1)
                sp.dma_start(seg_d[h * HALF:(h + 1) * HALF, :], fT[h][0:HALF, :]).then_inc(flags_out, 16)
            sp.wait_ge(flags_out, 32)

        @block.scalar
        def _(act):
            act.wait_ge(visits, 1)
            with act.Fori(0, NV // 2) as i:
                s = act.value_load(startI[0:1, bass.ds(2 * i + 1, 1)], min_val=0, max_val=E)
                act.dma_start(meta[:, bass.ds(2 * i + 1, 1), :, :].rearrange("p v g f -> p (v g f)"),
                              edges_d[bass.ds(s, CE), :].rearrange("(p g) f -> p (g f)", g=GC)).then_inc(meta_in, 16)

        @block.vector
        def _(dve):
            c = Chain(cut)
            dve.wait_ge(consts, 1)
            c.step(dve, V.tensor_copy(iotaV, iotaI))
            for b in range(1, NB):
                c.step(dve, V.tensor_scalar(scratch, dstF, float(b * P), 0.0, ALU.is_lt, ALU.add, accum_out=cnt[:, b:b + 1]))
            V.memset(small[:, 258:259], 0.0).then_inc(counted, 1)
            dve.wait_ge(totals, 1)
            V.tensor_copy(R[:, 1:NB], ps[:, 0, 1:NB])
            V.memset(R[:, 0:1], 0.0)
            c.step(dve, V.memset(R[:, NB:NB + 1], float(E)))
            c.step(dve, V.tensor_tensor(t25[:, 0:NB], R[:, 1:NB + 1], R[:, 0:NB], ALU.subtract))
            c.step(dve, V.tensor_scalar(nci[:, 0:NB], t25[:, 0:NB], float(CE - 1), None, ALU.add))
            c.step(dve, V.tensor_scalar(nci[:, 0:NB], nci[:, 0:NB], 9, None, ALU.logical_shift_right))
            c.step(dve, V.tensor_copy(t25[:, 0:NB], nci[:, 0:NB]))
            V.memset(Cs[:, 0:1], 0.0)
            c.step(dve, V.tensor_tensor_scan(Cs[:, 1:NB + 1], onesF[:, 0:NB], t25[:, 0:NB], 0.0, ALU.mult, ALU.add))
            c.step(dve, V.scalar_tensor_tensor(g[:, 0:NB], Cs[:, 0:NB], -float(CE), R[:, 0:NB], ALU.mult, ALU.add))
            c.step(dve, V.tensor_tensor(t25[:, 1:NB], g[:, 1:NB], g[:, 0:NB - 1], ALU.subtract))
            V.memset(blkF, 0.0)
            c.step(dve, V.tensor_scalar(startF, iotaV, float(CE), None, ALU.mult))
            for b in range(1, NB):
                c.step(dve, V.scalar_tensor_tensor(blkF, iotaV, Cs[:, b:b + 1], blkF, ALU.is_ge, ALU.add))
                c.step(dve, V.tensor_scalar(geF, iotaV, Cs[:, b:b + 1], t25[:, b:b + 1], ALU.is_ge, ALU.mult))
                c.step(dve, V.tensor_tensor(startF, startF, geF, ALU.add))
            V.tensor_scalar(startI[:, :], startF, float(E), None, ALU.min)
            c.step(dve, V.tensor_copy(blkI[:, :], blkF))
            c.step(dve, V.tensor_scalar(blkF, blkF, float(P), None, ALU.mult))
            V.memset(small[:, 256:257], 0.0).then_inc(visits, 1)
            c.step(dve, V.tensor_copy(ntF, ntI))
            for t in range(TYPES):
                V.tensor_scalar(typeM[:, :, t], ntF[:, 0:NB], float(t), None, ALU.is_equal)
            dve.wait_ge(meta_in, 16 * NV)
            m2 = meta.rearrange("p v g f -> p (v g) f")
            V.tensor_copy(srcE[:, :], m2[:, :, 0])
            V.tensor_copy(ewE[:, :], m2.bitcast(F32)[:, :, 3])
            V.tensor_copy(relF, m2[:, :, 2])
            c.step(dve, V.tensor_copy(dlE[:, :], m2[:, :, 1]))
            c.step(dve, V.scalar_tensor_tensor(relE[:, :], m2[:, :, 0], float(RELS), relF, ALU.mult, ALU.add))
            c.step(dve, V.tensor_tensor(dlE[:, :].rearrange("p (v g) -> p v g", g=GC),
                                        dlE[:, :].rearrange("p (v g) -> p v g", g=GC), bc(blkF, GC), ALU.subtract))
            V.memset(small[:, 257:258], 0.0).then_inc(meta_cut, 1)
            for h in range(2):
                dve.wait_ge(tposed, h + 1)
                c.step(dve, V.tensor_scalar(dT[h][0:HALF, :], ps[0:HALF, h, 0:CE], 2.0 ** 100, None, ALU.mult))
                V.memset(fT[h][0:HALF, 0:1], 0.0)
                V.memset(fT[h][0:HALF, CE:CE + 4], 0.0)
                c.step(dve, V.tensor_tensor(fT[h][0:HALF, 1:CE], dT[h][0:HALF, 0:CE - 1], dT[h][0:HALF, 1:CE], ALU.subtract))
                c.step(dve, V.tensor_scalar(dT[h][0:HALF, 0:CE - 1], fT[h][0:HALF, 1:CE], 0.0, None, ALU.is_lt))
                V.memset(dT[h][0:HALF, CE - 1:CE], 1.0).then_inc(flagged, 1)
            dve.wait_ge(back, 1)
            V.tensor_copy(lastE[:, :].rearrange("p (v g) -> p g v", g=GC),
                          ps[:, 2:6, 0:NV]).then_inc(cut, 1)

        @block.tensor
        def _(pe):
            pe.wait_ge(counted, 1)
            nc.tensor.matmul(ps[:, 0, 1:NB], onesF[:, :], cnt[:, 1:NB], start=True, stop=True).then_inc(totals, 1)
            pe.wait_ge(meta_cut, 1)
            dl = dlE[:, :].rearrange("p (v g) -> p v g", g=GC)
            for h in range(2):
                for q in range(GC):
                    ins = nc.tensor.transpose(ps[0:HALF, h, q:CE:GC], dl[:, h * HALF:(h + 1) * HALF, q], ident[:, :])
                ins.then_inc(tposed, 1)
            for h in range(2):
                pe.wait_ge(flagged, h + 1)
                for q in range(GC):
                    ins = nc.tensor.transpose(ps[:, 2 + q, h * HALF:(h + 1) * HALF], dT[h][0:HALF, q:CE:GC], ident[0:HALF, 0:HALF])
            ins.then_inc(back, 1)



def turns(eng, slot, first, last):
    pairs = (last - first) // 2
    with eng.Fori(0, pairs) as i:
        for k in range(2):
            s = first + k
            slot(2 * i + s, s % 2, i + s // 2)
    for s in range(first + 2 * pairs, last):
        slot(s, s % 2, s // 2)


def gather_rows(nc, e, block, pass_no, table, width, index, free, free_per_group):
    rv = e.rows[:, :, 0:GT * width].rearrange("p u (t d) -> p u t d", d=width)

    @block.gpsimd
    def _(pool):
        def group(s, u, q):
            if not (isinstance(s, int) and s < 2):
                free.wait(pool, pass_no - (free_per_group[1]), free_per_group[0] * (s - 1))
            nc.gpsimd.tensor_copy(e.idx[:, u, :], index[:, bass.ds(s * GT, GT)]).then_inc(e.idx_ready.sem, 1)
            e.idx_ready.wait(pool, pass_no, s + 1)
            pool.sem_inc(e.gate, 1)
            for t in range(GT):
                pool.indirect_dma_start(out=rv[:, u, t, :], out_offset=None, in_=table,
                                        in_offset=bass.IndirectOffsetOnAxis(ap=e.idx[:, u, t:t + 1], axis=0))\
                    .then_inc(e.rows_here[u][t // GC].sem, 16)

        group(0, 0, 0)
        group(1, 1, 0)
        turns(pool, group, 2, NG)
    return rv


def weighted_pass(nc, e):
    V = nc.vector
    with nc.Block() as block:
        rv = gather_rows(nc, e, block, 0, e.t0_d, D, e.srcE, e.p_ready, (J, 0))

        @block.vector
        def _(dve):
            def onehots(s, u):
                for j in range(J):
                    if not (isinstance(s, int) and s < 2):
                        e.p_ready.wait(dve, 0, J * (s - 2) + j + 1)
                    for g in range(GC):
                        t = GC * j + g
                        ins = V.tensor_scalar(e.oh[:, u, t, :], e.iotaF[:, :], e.dlE[:, bass.ds(s * GT + t, 1)],
                                              e.ewE[:, bass.ds(s * GT + t, 1)], ALU.is_equal, ALU.mult)
                    ins.then_inc(e.oh_ready.sem, 1)

            def add(s, u):
                for j in range(J):
                    b = dve.value_load(e.blkI[0:1, bass.ds(J * s + j, 1)], min_val=0, max_val=NB - 1)
                    a = e.acc[:, bass.ds(b * D, D)]
                    e.p_ready.wait(dve, 0, J * s + j + 1)
                    e.added.wait(dve, 0, J * s + j)
                    V.tensor_tensor(a, a, e.ps[:, 4 * u + j, 0:D], ALU.add).then_inc(e.added.sem, 1)

            def slot(s, u, q):
                onehots(s, u)
                add(s - 1, 1 - u)

            onehots(0, 0)
            slot(1, 1, 0)
            turns(dve, slot, 2, NG)
            add(NG - 1, (NG - 1) % 2)

        @block.tensor
        def _(pe):
            def slot(s, u, q):
                for j in range(J):
                    e.oh_ready.wait(pe, 0, J * s + j + 1)
                    e.rows_here[u][j].wait(pe, 0, 64 * (q + 1))
                    if not (isinstance(s, int) and s < 2):
                        e.added.wait(pe, 0, J * (s - 2) + j + 1)
                    for g in range(GC):
                        ins = nc.tensor.matmul(e.ps[:, 4 * u + j, 0:D], e.oh[:, u, GC * j + g, :], rv[:, u, GC * j + g, :],
                                               start=(g == 0), stop=(g == GC - 1))
                    ins.then_inc(e.p_ready.sem, 1)
            slot(0, 0, 0)
            slot(1, 1, 0)
            turns(pe, slot, 2, NG)


def attention_pass(nc, e, no, H, table, width, index, scale, gat):
    V, ps = nc.vector, e.ps
    a_no = no - 1
    gat_no = no - 2
    hs = D // H
    W = hs + 1
    HW = H * W
    PW = HW + H
    JH = J * H
    BT, BK, BS, BE = 0, 2, 4, 5
    pP = ps[:, 6:8, :].rearrange("p a (c w) -> p (a c) w", w=256)
    pPh = pP[:, :, 0:HW].rearrange("p j (h c) -> p j h c", c=W)
    exvT = e.exv[:, 0:GT * PW].rearrange("p (t w) -> p t w", w=PW)
    exvH = exvT[:, :, 0:HW].rearrange("p t (h c) -> p t h c", c=W)
    exP = ps[:, BE, 0:GC * JH].rearrange("p (g j h) -> p g j h", g=GC, j=J)
    exE = e.exb[:, 0:GC * JH].rearrange("p (g j h) -> p g j h", g=GC, j=J)
    mxE = e.exb[:, GC * JH:2 * GC * JH].rearrange("p (g j h) -> p g j h", g=GC, j=J)
    tPh = e.tP[:, 0:J * HW].rearrange("p (j h c) -> p j h c", j=J, h=H)
    scv = e.sc[:, :, 0:GC * JH].rearrange("p u (g j h) -> p u g j h", g=GC, j=J)
    mw = [e.mwork[:, n, 0:JH].rearrange("p (j h) -> p j h", j=J) for n in range(3)]
    pen, ml, mold = mw
    mn = e.mwork[:, 3, 0:JH].rearrange("p (j h) -> p j h", j=J)
    d2 = e.mwork[:, 4:6, 0:JH]
    e2 = e.mwork[:, 6:8, 0:JH]
    e2v = [e.mwork[:, 6 + n, 0:JH].rearrange("p (j h) -> p j h", j=J) for n in range(2)]
    att = e.vecs[:, 0:D]

    def static(s, below):
        return isinstance(s, int) and s < below

    with nc.Block() as block:
        rv = gather_rows(nc, e, block, no, table, width, index, e.exv_ready, (J, 1))
        vrow = width - D

        @block.sync
        def _(sp):
            def slot(s, u, q):
                if not static(s, 2):
                    e.seg_ready.wait(sp, a_no, s - 1)
                for j in range(J):
                    sp.dma_start(e.segF[j * H:(j + 1) * H, u, :],
                                 e.seg_d[bass.ds(s * J + j, 1), :].to_broadcast([H, CE + 4])).then_inc(e.flags_here[u].sem, 16)
            slot(0, 0, 0)
            slot(1, 1, 0)
            turns(sp, slot, 2, NG)

        @block.scalar
        def _(act):
            def chunks(s, u, q):
                for j in range(J):
                    c = J * s + j
                    k = j % 2
                    e.oht_made.wait(act, a_no, c + 1)
                    if not (static(s, 1) and j < 2):
                        e.kd_ready.wait(act, a_no, c - 1)
                    nc.scalar.activation(e.ohT[:, k, :], ps[:, BT + k, :], ACT.Copy).then_inc(e.oht_ready.sem, 1)
                    if gat:
                        e.kd_ready.wait(act, a_no, c + 1)
                        if not (static(s, 1) and j < 2):
                            e.score_ready.wait(act, a_no, c - 1)
                        nc.scalar.activation(e.prod[:, k, :], ps[:, BK + k, :], ACT.Copy).then_inc(e.lr_ready.sem, 1)

            def exp_columns(s):
                e.back_ready.wait(act, a_no, s + 1)
                nc.scalar.activation(e.exb[:, 0:2 * GC * JH], ps[:, BE, 0:2 * GC * JH], ACT.Copy).then_inc(e.exb_ready.sem, 1)
                nc.scalar.activation(exvH[:, :, :, hs].rearrange("p (j g) h -> p j g h", j=J),
                                     exP.rearrange("p g j h -> p j g h"), ACT.Copy).then_inc(e.excol_ready.sem, 1)

            def exps(s):
                e.seg_ready.wait(act, a_no, s + 1)
                nc.scalar.activation(e.exT[0:JH, :], e.segS[0:JH, 0, :], ACT.Exp, scale=scale).then_inc(e.ex_ready.sem, 1)

            def shift_exps(s):
                e.d2_ready.wait(act, a_no, s + 1)
                nc.scalar.activation(e2, d2, ACT.Exp, scale=scale).then_inc(e.e2_ready.sem, 1)

            def slot(s, u, q):
                chunks(s, u, q)
                exp_columns(s - 1)
                exps(s)
                shift_exps(s - 1)

            chunks(0, 0, 0)
            exps(0)
            turns(act, slot, 1, NG)
            exp_columns(NG - 1)
            shift_exps(NG - 1)

        @block.vector
        def _(dve):
            def onehots(s, u):
                for j in range(J):
                    if not static(s, 2):
                        e.p_ready.wait(dve, no, J * (s - 2) + j + 1)
                    V.tensor_tensor(e.oh[:, u, GC * j:GC * (j + 1), :],
                                    e.iotaF[:, :].unsqueeze(1).to_broadcast([P, GC, P]),
                                    bc(e.dlE[:, bass.ds(s * GT + GC * j, GC)], P), ALU.is_equal).then_inc(e.oh_ready.sem, 1)

            def product(s, u, q, j):
                c, k = J * s + j, j % 2
                pr = e.prod[:, k, :].rearrange("p (g d) -> p g d", d=D)
                if not (static(s, 1) and j < 2):
                    e.score_ready.wait(dve, a_no, c - 1)
                if gat:
                    e.lr_ready.wait(dve, gat_no, c + 1)
                    V.scalar_tensor_tensor(e.prod[:, k, :], ps[:, BK + k, :], 0.2, e.prod[:, k, :], ALU.mult, ALU.max)\
                        .then_inc(e.leaky_done.sem, 1)
                    e.leaky_done.wait(dve, gat_no, c + 1)
                    V.tensor_tensor(pr, pr, att.unsqueeze(1).to_broadcast([P, GC, D]), ALU.mult).then_inc(e.prod_ready.sem, 1)
                else:
                    e.kd_ready.wait(dve, a_no, c + 1)
                    e.rows_here[u][j].wait(dve, no, 64 * (q + 1))
                    V.tensor_tensor(pr, rv[:, u, GC * j:GC * (j + 1), 0:D],
                                    ps[:, BK + k, :].rearrange("p (g d) -> p g d", d=D), ALU.mult).then_inc(e.prod_ready.sem, 1)

            def score(s, u, j):
                e.prod_ready.wait(dve, a_no, J * s + j + 1)
                V.tensor_reduce(scv[:, u, :, j, :], e.prod[:, j % 2, :].rearrange("p (g h d) -> p g h d", g=GC, h=H),
                                AX, ALU.add).then_inc(e.score_ready.sem, 1)

            def last_maxima(s):
                e.exb_ready.wait(dve, a_no, s + 1)
                V.tensor_tensor(exvT[:, :, HW:PW].rearrange("p (j g) h -> p j g h", j=J),
                                mxE.rearrange("p g j h -> p j g h"),
                                bc(e.lastE[:, bass.ds(s * GT, GT)].rearrange("p (j g) -> p j g", j=J), H), ALU.mult)

            def weigh(s, u, q, j):
                e.rows_here[u][j].wait(dve, no, 64 * (q + 1))
                V.tensor_tensor(exvH[:, GC * j:GC * (j + 1), :, 0:hs],
                                rv[:, u, GC * j:GC * (j + 1), vrow:vrow + D].rearrange("p g (h d) -> p g h d", h=H),
                                bc(exE[:, :, j, :], hs), ALU.mult).then_inc(e.exv_ready.sem, 1)

            def scans(s, u, q):
                S = ps[0:JH, BS, :]
                e.st_ready.wait(dve, a_no, s + 1)
                e.flags_here[u].wait(dve, a_no, 16 * J * (q + 1))
                V.tensor_tensor_scan(e.segS[0:JH, 0, :], e.segF[0:JH, u, 0:CE], S, -BIG, ALU.add, ALU.max)\
                    .then_inc(e.scan_step.sem, 1)
                e.scan_step.wait(dve, a_no, 2 * s + 1)
                V.tensor_tensor_scan(e.segS[0:JH, 1, CE - 1::-1], e.segF[0:JH, u, CE:0:-1], e.segS[0:JH, 0, CE - 1::-1],
                                     -BIG, ALU.add, ALU.max).then_inc(e.scan_step.sem, 1)
                e.scan_step.wait(dve, a_no, 2 * s + 2)
                V.tensor_tensor(e.segS[0:JH, 0, :], S, e.segS[0:JH, 1, :], ALU.subtract).then_inc(e.seg_ready.sem, 1)

            def merge_maxima(s):
                n = MERGE_STEPS * s
                bs = [dve.value_load(e.blkI[0:1, bass.ds(J * s + j, 1)], min_val=0, max_val=NB - 1) for j in range(J)]

                def step(ins):
                    nonlocal n
                    n = n + 1
                    ins.then_inc(e.merge_step.sem, 1)

                def done():
                    e.merge_step.wait(dve, a_no, n)
                e.p_ready.wait(dve, no, J * (s + 1))
                step(V.tensor_scalar(pen, pPh[:, :, :, hs], 0.5, -BIG, ALU.is_lt, ALU.mult))
                done()
                step(V.tensor_tensor(ml, pen, pP[:, :, HW:PW], ALU.add))
                for j in range(J):
                    m = e.mx[:, bass.ds(bs[j] * H, H)]
                    done()
                    step(V.tensor_scalar(mold[:, j, :], m, 1.0, None, ALU.mult))
                    step(V.tensor_tensor(mn[:, j, :], m, ml[:, j, :], ALU.max))
                    done()
                    step(V.tensor_scalar(m, mn[:, j, :], 1.0, None, ALU.mult))
                step(V.tensor_tensor(e.mwork[:, 4, 0:JH], e.mwork[:, 2, 0:JH], e.mwork[:, 3, 0:JH], ALU.subtract))
                step(V.tensor_tensor(e.mwork[:, 5, 0:JH], e.mwork[:, 1, 0:JH], e.mwork[:, 3, 0:JH], ALU.subtract))
                done()
                V.memset(e.mwork[:, 0, 0:1], 0.0).then_inc(e.d2_ready.sem, 1)
                return bs, n

            def merge_sums(s, bs, n):
                def step(ins):
                    nonlocal n
                    n = n + 1
                    ins.then_inc(e.merge_step.sem, 1)

                def done():
                    e.merge_step.wait(dve, a_no, n)
                e.e2_ready.wait(dve, a_no, s + 1)
                step(V.tensor_tensor(tPh, pPh, bc(e2v[1], W), ALU.mult))
                for j in range(J):
                    a = e.acc[:, bass.ds(bs[j] * HW, HW)].rearrange("p (h c) -> p h c", h=H)
                    done()
                    step(V.tensor_tensor(a, a, bc(e2v[0][:, j, :], W), ALU.mult))
                    done()
                    step(V.tensor_tensor(a, a, tPh[:, j, :, :], ALU.add))
                done()
                V.memset(e.mwork[:, 0, 0:1], 0.0).then_inc(e.merged.sem, 1)

            def slot(s, u, q, cur=True, prev=True):
                pq = q if u == 1 else q - 1
                if cur:
                    product(s, u, q, 0)
                    product(s, u, q, 1)
                    score(s, u, 0)
                    score(s, u, 1)
                if prev:
                    last_maxima(s - 1)
                    weigh(s - 1, 1 - u, pq, 0)
                    weigh(s - 1, 1 - u, pq, 1)
                if cur:
                    product(s, u, q, 2)
                    product(s, u, q, 3)
                    score(s, u, 2)
                    score(s, u, 3)
                if prev:
                    weigh(s - 1, 1 - u, pq, 2)
                    weigh(s - 1, 1 - u, pq, 3)
                if cur:
                    scans(s, u, q)
                    if not (isinstance(s, int) and s == NG - 1):
                        onehots(s + 1, 1 - u)
                if prev:
                    bs, n = merge_maxima(s - 1)
                    merge_sums(s - 1, bs, n)

            onehots(0, 0)
            slot(0, 0, 0, prev=False)
            turns(dve, slot, 1, NG - 1)
            slot(NG - 1, (NG - 1) % 2, (NG - 1) // 2)
            slot(NG, NG % 2, NG // 2, cur=False)

        @block.tensor
        def _(pe):
            def turn_onehots(s, u, j):
                c = J * s + j
                e.oh_ready.wait(pe, no, c + 1)
                if not (static(s, 1) and j < 2):
                    e.oht_ready.wait(pe, a_no, c - 1)
                for g in range(GC):
                    ins = nc.tensor.transpose(ps[:, BT + j % 2, g * P:(g + 1) * P], e.oh[:, u, GC * j + g, :], e.ident[:, :])
                ins.then_inc(e.oht_made.sem, 1)

            def dst_rows(s, u, q, j, b):
                c, k = J * s + j, j % 2
                e.oht_ready.wait(pe, a_no, c + 1)
                if gat:
                    e.rows_here[u][j].wait(pe, no, 64 * (q + 1))
                if not (static(s, 1) and j < 2):
                    if gat:
                        e.leaky_done.wait(pe, gat_no, c - 1)
                    else:
                        e.prod_ready.wait(pe, a_no, c - 1)
                for g in range(GC):
                    o = ps[:, BK + k, g * P:(g + 1) * P]
                    ins = nc.tensor.matmul(o, e.ohT[:, k, g * P:(g + 1) * P], e.kN[:, bass.ds(b, 1), :].rearrange("p b d -> p (b d)"),
                                           start=True, stop=not gat)
                    if gat:
                        ins = nc.tensor.matmul(o, e.ident[:, :], rv[:, u, GC * j + g, :], start=False, stop=True)
                ins.then_inc(e.kd_ready.sem, 1)

            def turn_scores(s, u):
                e.score_ready.wait(pe, a_no, J * (s + 1))
                if not static(s, 1):
                    e.seg_ready.wait(pe, a_no, s)
                for g in range(GC):
                    ins = nc.tensor.transpose(ps[0:JH, BS, g:CE:GC], e.sc[:, u, g * JH:(g + 1) * JH], e.ident[:, :])
                ins.then_inc(e.st_ready.sem, 1)

            def turn_back(s):
                e.ex_ready.wait(pe, a_no, s + 1)
                pe.sem_inc(e.gate, 1)
                for g in range(GC):
                    nc.tensor.transpose(ps[:, BE, g * JH:(g + 1) * JH], e.exT[0:JH, g:CE:GC], e.ident[0:JH, 0:JH])
                    ins = nc.tensor.transpose(ps[:, BE, (GC + g) * JH:(GC + g + 1) * JH], e.segS[0:JH, 1, g:CE:GC],
                                              e.ident[0:JH, 0:JH])
                ins.then_inc(e.back_ready.sem, 1)

            def sums(s, u, j):
                e.exv_ready.wait(pe, a_no, J * s + j + 1)
                e.excol_ready.wait(pe, a_no, s + 1)
                if not static(s, 1):
                    e.merged.wait(pe, a_no, s)
                for g in range(GC):
                    ins = nc.tensor.matmul(pP[:, j, 0:PW], e.oh[:, u, GC * j + g, :], exvT[:, GC * j + g, :],
                                           start=(g == 0), stop=(g == GC - 1))
                ins.then_inc(e.p_ready.sem, 1)

            def slot(s, u, q, cur=True, prev=True):
                if cur:
                    bs = [pe.value_load(e.blkI[0:1, bass.ds(J * s + j, 1)], min_val=0, max_val=NB - 1) for j in range(J)]
                    turn_onehots(s, u, 0)
                    turn_onehots(s, u, 1)
                    dst_rows(s, u, q, 0, bs[0])
                    turn_onehots(s, u, 2)
                    dst_rows(s, u, q, 1, bs[1])
                if prev:
                    turn_back(s - 1)
                if cur:
                    turn_onehots(s, u, 3)
                    dst_rows(s, u, q, 2, bs[2])
                    dst_rows(s, u, q, 3, bs[3])
                if prev:
                    sums(s - 1, 1 - u, 0)
                    sums(s - 1, 1 - u, 1)
                if cur:
                    turn_scores(s, u)
                if prev:
                    sums(s - 1, 1 - u, 2)
                    sums(s - 1, 1 - u, 3)

            slot(0, 0, 0, prev=False)
            turns(pe, slot, 1, NG)
            slot(NG, NG % 2, NG // 2, cur=False)


class Stage:

    def __init__(self, e, name):
        self.e, self.name, self.sems = e, name, {}

    def __getitem__(self, what):
        if what not in self.sems:
            self.sems[what] = self.e.nc.alloc_semaphore(name=f"{self.name}_{what}")
        return self.sems[what]

    def __enter__(self):
        return self

    def __exit__(self, *_):
        self.e.nc.clear_and_free_semaphores(list(self.sems.values()))
        self.e.nc.all_engine_barrier()


def load_row(nc, eng, dst, src, done):
    n = dst.shape[1]
    eng.dma_start(dst, src.rearrange("(a n) -> a n", a=1).to_broadcast([P, n])).then_inc(done, 16)


def over(ap, n=NB):
    return ap.unsqueeze(1).to_broadcast([P, n, ap.shape[1]])


def project(nc, e, block, S, tag, parts, nout):
    turned, copied, done, taken, ready = (S[f"{tag}_{w}"] for w in ("turned", "copied", "done", "taken", "ready"))
    np_ = len(parts)
    at_hand = S[f"{tag}_at_hand"]

    @block.gpsimd
    def _(pool):
        pool.wait_ge(ready, 1)

        def body(b, k, first):
            if not first:
                pool.wait_ge(turned, b - 1)
            for n, (nodes, _) in enumerate(parts):
                ins = nc.gpsimd.tensor_copy(e.prod[:, k, n * P:(n + 1) * P], nodes[:, bass.ds(b, 1), :].rearrange("p b d -> p (b d)"))
            ins.then_inc(at_hand, 1)
        over_blocks(pool, body)

    @block.tensor
    def _(pe):
        def body(b, k, first):
            pe.wait_ge(at_hand, b + 1)
            for n in range(np_):
                ins = nc.tensor.transpose(e.ps[:, k, n * P:(n + 1) * P], e.prod[:, k, n * P:(n + 1) * P], e.ident[:, :])
            ins.then_inc(turned, 1)
            pe.wait_ge(copied, b + 1)
            if not first:
                pe.wait_ge(taken, b - 1)
            for n, (_, w) in enumerate(parts):
                ins = nc.tensor.matmul(e.ps[:, 2 + k, 0:nout], e.ohT[:, k, n * P:(n + 1) * P], w, start=(n == 0), stop=(n == np_ - 1))
            ins.then_inc(done, 1)
        over_blocks(pe, body)

    @block.scalar
    def _(act):
        def body(b, k, first):
            act.wait_ge(turned, b + 1)
            if not first:
                act.wait_ge(done, b - 1)
            nc.scalar.activation(e.ohT[:, k, 0:np_ * P], e.ps[:, k, 0:np_ * P], ACT.Copy).then_inc(copied, 1)
        over_blocks(act, body)


def norm(nc, e, dve, c, S, tag, src, dst, tmp, relu):
    V = nc.vector
    mean, var = e.r_at[:, 0:NB], e.r_at[:, 32:32 + NB]
    c.step(dve, V.tensor_reduce(mean, src, AX, ALU.add))
    c.step(dve, V.tensor_scalar(mean, mean, 1.0 / D, None, ALU.mult))
    c.step(dve, V.tensor_tensor(dst, src, bc(mean, D), ALU.subtract))
    c.step(dve, V.tensor_tensor(tmp, dst, dst, ALU.mult))
    c.step(dve, V.tensor_reduce(var, tmp, AX, ALU.add))
    V.tensor_scalar(var, var, 1.0 / D, 1e-5, ALU.mult, ALU.add).then_inc(S[tag + "_var"], 1)
    dve.wait_ge(S[tag + "_std"], 1)
    c.step(dve, V.reciprocal(var, var))
    c.step(dve, V.tensor_tensor(dst, dst, bc(var, D), ALU.mult))
    if relu:
        c.step(dve, V.tensor_scalar(dst, dst, 0.0, None, ALU.max))


def norm_sqrt(nc, e, act, S, tag):
    act.wait_ge(S[tag + "_var"], 1)
    nc.scalar.activation(e.r_at[:, 32:32 + NB], e.r_at[:, 32:32 + NB], ACT.Sqrt).then_inc(S[tag + "_std"], 1)


def normalized(nc, e, dve, c, dst, H):
    V = nc.vector
    W = D // H + 1
    a = e.acc[:, 0:NB * H * W].rearrange("p (n c) -> p n c", c=W)
    r = e.r_at[:, 0:NB * H]
    c.step(dve, V.tensor_scalar(r, a[:, :, W - 1], 0.5, None, ALU.max))
    c.step(dve, V.reciprocal(r, r))
    c.step(dve, V.tensor_tensor(dst.rearrange("p b (h d) -> p (b h) d", h=H), a[:, :, 0:W - 1], bc(r, W - 1), ALU.mult))


def first_norm(nc, A, e):
    S = Stage(e, "n0")
    with S, nc.Block() as block:
        @block.vector
        def _(dve):
            c = Chain(S["step"])
            norm(nc, e, dve, c, S, "ln", e.xN, e.hN, e.tA, True)
            c.step(dve, nc.vector.memset(e.acc[:, :], 0.0))
            nc.vector.memset(e.small[:, 0:1], 0.0).then_inc(S["h"], 1)

        @block.scalar
        def _(act):
            norm_sqrt(nc, e, act, S, "ln")

        @block.sync
        def _(sp):
            sp.wait_ge(S["h"], 1)
            sp.dma_start(e.t0_d.rearrange("(b p) d -> p b d", p=P), e.hN[:, :, :]).then_inc(S["out"], 16)
            sp.wait_ge(S["out"], 16)


def after_l0(nc, A, e):
    S = Stage(e, "n1")
    V = nc.vector
    w = e.wts
    agg = e.acc[:, 0:NB * D].rearrange("p (b d) -> p b d", d=D)
    with S, nc.Block() as block:
        @block.sync
        def _(sp):
            sp.dma_start(w[:, 0:D], A["L0_gnn_W1"]).then_inc(S["w"], 16)
            sp.dma_start(w[:, D:2 * D], A["L0_gnn_W2"]).then_inc(S["w"], 16)
            load_row(nc, sp, w[:, 1536:1664], A["L0_gnn_b1"], S["w"])
            load_row(nc, sp, w[:, 1664:1792], A["L0_gnn_b2"], S["w"])
            for n, name in enumerate("qvks"):
                sp.dma_start(w[:, 512 + n * D:512 + (n + 1) * D], A[f"L1_gnn_W{name}"]).then_inc(S["w"], 16)
                load_row(nc, sp, w[:, 1024 + n * D:1024 + (n + 1) * D], A[f"L1_gnn_b{name}"], S["w"])
            sp.wait_ge(S["tables"], 1)
            t1 = e.t1_d.rearrange("(b p) d -> p b d", p=P)
            sp.dma_start(t1[:, :, 0:D], e.tA).then_inc(S["out"], 16)
            sp.dma_start(t1[:, :, D:2 * D], e.tB).then_inc(S["out"], 16)
            sp.wait_ge(S["out"], 32)

        @block.vector
        def _(dve):
            c = Chain(S["step"])
            c.step(dve, V.tensor_tensor(e.tA, agg, e.hN[:, :, :], ALU.add))
            c.step(dve, V.tensor_tensor(e.tB, agg, e.hN[:, :, :], ALU.mult))
            dve.wait_ge(S["wt"], 1)
            c.step(dve, V.tensor_copy(w[:, 256:512], e.ps[:, 7, 0:256]))
            c.step(dve, V.tensor_tensor(w[:, 1536:1664], w[:, 1536:1664], w[:, 1664:1792], ALU.add))
            V.memset(e.small[:, 0:1], 0.0).then_inc(S["a_ready"], 1)

            def take(b, k, first):
                dve.wait_ge(S["a_done"], b + 1)
                V.tensor_tensor(e.tC[:, bass.ds(b, 1), :].rearrange("p b d -> p (b d)"), e.ps[:, 2 + k, 0:D],
                                w[:, 1536:1664], ALU.add).then_inc(S["a_taken"], 1)
            over_blocks(dve, take)
            dve.wait_ge(S["a_taken"], NB)
            c.step(dve, V.scalar_tensor_tensor(e.tC, e.tC, 0.2, e.tC, ALU.mult, ALU.max))
            c.step(dve, V.tensor_tensor(e.xN[:, :, :], e.xN[:, :, :], e.tC, ALU.add))
            norm(nc, e, dve, c, S, "ln", e.xN[:, :, :], e.hN[:, :, :], e.tA, True)
            V.memset(e.small[:, 0:1], 0.0).then_inc(S["b_ready"], 1)

            def take4(b, k, first):
                dve.wait_ge(S["b_done"], b + 1)
                for n, dst in enumerate((e.tA, e.tB, e.kN, e.skN)):
                    ins = V.tensor_tensor(dst[:, bass.ds(b, 1), :].rearrange("p b d -> p (b d)"),
                                          e.ps[:, 2 + k, n * D:(n + 1) * D], w[:, 1024 + n * D:1024 + (n + 1) * D], ALU.add)
                ins.then_inc(S["b_taken"], 1)
            over_blocks(dve, take4)
            dve.wait_ge(S["b_taken"], NB)
            V.memset(e.small[:, 0:1], 0.0).then_inc(S["tables"], 1)
            c.step(dve, V.memset(e.acc[:, :], 0.0))
            c.step(dve, V.memset(e.mx[:, :], -BIG))

        @block.tensor
        def _(pe):
            pe.wait_ge(S["w"], 16 * 12)
            nc.tensor.transpose(e.ps[:, 7, 0:P], w[:, 0:D], e.ident[:, :])
            nc.tensor.transpose(e.ps[:, 7, P:2 * P], w[:, D:2 * D], e.ident[:, :]).then_inc(S["wt"], 1)

        project(nc, e, block, S, "a", [(e.tA, w[:, 256:384]), (e.tB, w[:, 384:512])], D)

        @block.scalar
        def _(act):
            norm_sqrt(nc, e, act, S, "ln")

        project(nc, e, block, S, "b", [(e.hN, w[:, 512:1024])], 4 * D)


def gat_projections(nc, A, e, block, S, layer, H):
    w = e.wts
    V = nc.vector
    W = D // H + 1

    @block.sync
    def _(sp):
        sp.dma_start(w[:, 0:D], A[f"L2_gnn_Wl{layer}"]).then_inc(S["w"], 16)
        sp.dma_start(w[:, D:2 * D], A[f"L2_gnn_Wr{layer}"]).then_inc(S["w"], 16)
        load_row(nc, sp, w[:, 256:384], A[f"L2_gnn_bl{layer}"], S["w"])
        load_row(nc, sp, w[:, 384:512], A[f"L2_gnn_br{layer}"], S["w"])
        load_row(nc, sp, e.vecs[:, 0:D], A[f"L2_gnn_att{layer}"].rearrange("h c -> (h c)"), S["w"])
        sp.wait_ge(S["tables"], 1)
        sp.dma_start(e.t2_d.rearrange("(b p) d -> p b d", p=P), e.tA).then_inc(S["out"], 16)
        sp.wait_ge(S["out"], 16)

    project(nc, e, block, S, "p", [(e.hN, w[:, 0:256])], 2 * D)

    def on_dve(dve, c):
        dve.wait_ge(S["w"], 16 * 5)
        V.memset(e.small[:, 0:1], 0.0).then_inc(S["p_ready"], 1)

        def take(b, k, first):
            dve.wait_ge(S["p_done"], b + 1)
            V.tensor_tensor(e.tA[:, bass.ds(b, 1), :].rearrange("p b d -> p (b d)"), e.ps[:, 2 + k, 0:D], w[:, 256:384], ALU.add)
            V.tensor_tensor(e.kN[:, bass.ds(b, 1), :].rearrange("p b d -> p (b d)"), e.ps[:, 2 + k, D:2 * D], w[:, 384:512],
                            ALU.add).then_inc(S["p_taken"], 1)
        over_blocks(dve, take)
        dve.wait_ge(S["p_taken"], NB)
        V.memset(e.small[:, 0:1], 0.0).then_inc(S["tables"], 1)
        a = e.acc[:, 0:NB * H * W].rearrange("p (n c) -> p n c", c=W)
        c.step(dve, V.tensor_copy(a[:, :, 0:W - 1], e.tA.rearrange("p b (h d) -> p (b h) d", h=H)))
        c.step(dve, V.memset(a[:, :, W - 1:W], 1.0))
        c.step(dve, V.tensor_tensor(e.tC, e.tA, e.kN[:, :, :], ALU.add))
        c.step(dve, V.scalar_tensor_tensor(e.tC, e.tC, 0.2, e.tC, ALU.mult, ALU.max))
        c.step(dve, V.tensor_tensor(e.tC, e.tC, over(e.vecs[:, 0:D]), ALU.mult))
        c.step(dve, V.tensor_reduce(e.mx[:, 0:NB * H], e.tC.rearrange("p b (h d) -> p (b h) d", h=H), AX, ALU.add))
    return on_dve


def after_l1(nc, A, e):
    S = Stage(e, "n2")
    V = nc.vector
    vec = e.vecs
    wg, gam, bet = vec[:, 128:512], vec[:, 512:640], vec[:, 640:768]
    wa, wb = vec[:, 768:896], vec[:, 896:1024]
    bg, alpha = e.small[:, 300:301], e.small[:, 301:302]
    z = e.r_at[:, 192:192 + NB]
    with S, nc.Block() as block:
        @block.sync
        def _(sp):
            load_row(nc, sp, wg, A["L1_gnn_Wg"].rearrange("n a -> (n a)"), S["v"])
            load_row(nc, sp, gam, A["L1_gnn_gamma"], S["v"])
            load_row(nc, sp, bet, A["L1_gnn_beta"], S["v"])
            load_row(nc, sp, bg, A["L1_gnn_bg"], S["v"])
            load_row(nc, sp, alpha, A["L1_gnn_alpha"], S["v"])

        @block.scalar
        def _(act):
            act.wait_ge(S["z"], 1)
            nc.scalar.activation(z, z, ACT.Exp, scale=-1.0).then_inc(S["ez"], 1)
            norm_sqrt(nc, e, act, S, "ln1")
            norm_sqrt(nc, e, act, S, "ln2")

        on_dve = gat_projections(nc, A, e, block, S, 1, 4)

        @block.vector
        def _(dve):
            c = Chain(S["step"])
            agg, t, u, sk = e.tA, e.tB, e.tC, e.skN
            normalized(nc, e, dve, c, agg, 4)
            dve.wait_ge(S["v"], 16 * 5)
            c.step(dve, V.tensor_tensor(wa, wg[:, 0:D], wg[:, 2 * D:3 * D], ALU.add))
            c.step(dve, V.tensor_tensor(wb, wg[:, D:2 * D], wg[:, 2 * D:3 * D], ALU.subtract))
            c.step(dve, V.tensor_tensor(t, sk, over(wa), ALU.mult))
            c.step(dve, V.tensor_tensor(u, agg, over(wb), ALU.mult))
            c.step(dve, V.tensor_tensor(t, t, u, ALU.add))
            c.step(dve, V.tensor_reduce(z, t, AX, ALU.add))
            c.step(dve, V.tensor_scalar(z, z, bg, -80.0, ALU.add, ALU.max))
            V.memset(e.small[:, 0:1], 0.0).then_inc(S["z"], 1)
            dve.wait_ge(S["ez"], 1)
            c.step(dve, V.tensor_scalar(z, z, 1.0, None, ALU.add))
            c.step(dve, V.reciprocal(z, z))
            c.step(dve, V.tensor_tensor(t, sk, agg, ALU.subtract))
            c.step(dve, V.tensor_tensor(t, t, bc(z, D), ALU.mult))
            c.step(dve, V.tensor_tensor(agg, agg, t, ALU.add))
            norm(nc, e, dve, c, S, "ln1", agg, t, u, False)
            c.step(dve, V.tensor_tensor(t, t, over(gam), ALU.mult))
            c.step(dve, V.tensor_tensor(t, t, over(bet), ALU.add))
            c.step(dve, V.tensor_scalar(u, t, 0.0, alpha, ALU.min, ALU.mult))
            c.step(dve, V.scalar_tensor_tensor(t, t, 0.0, u, ALU.max, ALU.add))
            c.step(dve, V.tensor_tensor(e.xN[:, :, :], e.xN[:, :, :], t, ALU.add))
            norm(nc, e, dve, c, S, "ln2", e.xN[:, :, :], e.hN[:, :, :], t, True)
            on_dve(dve, c)


def after_l2a(nc, A, e):
    S = Stage(e, "n3")
    V = nc.vector
    with S, nc.Block() as block:
        @block.sync
        def _(sp):
            load_row(nc, sp, e.vecs[:, 128:256], A["L2_gnn_b1"], S["v"])

        on_dve = gat_projections(nc, A, e, block, S, 2, 1)

        @block.vector
        def _(dve):
            c = Chain(S["step"])
            normalized(nc, e, dve, c, e.tA, 4)
            dve.wait_ge(S["v"], 16)
            c.step(dve, V.tensor_tensor(e.tA, e.tA, over(e.vecs[:, 128:256]), ALU.add))
            c.step(dve, V.tensor_scalar(e.hN[:, :, :], e.tA, 0.0, None, ALU.max))
            on_dve(dve, c)


KW, WA, BD = 0, 3072, 4096


def masked_turn(nc, e, block, S, tag, nodes, before=None):
    ohf = e.oh[:, :, :, :].rearrange("p u t n -> p (u t n)")
    dm = [ohf[:, k * 1024:(k + 1) * 1024] for k in range(2)]
    hTm = [ohf[:, 2048 + k * 1024:2048 + (k + 1) * 1024] for k in range(2)]
    made, turned, copied, used, at_hand = (S[f"{tag}_{w}"] for w in ("masks", "turned", "copied", "used", "at_hand"))

    @block.gpsimd
    def _(pool):
        pool.wait_ge(S[f"{tag}_ready"], 1)

        def body(b, k, first):
            if not first:
                pool.wait_ge(turned, b - 1)
            nc.gpsimd.tensor_copy(e.prod[:, k, 0:P], nodes[:, bass.ds(b, 1), :].rearrange("p b d -> p (b d)")).then_inc(at_hand, 1)
        over_blocks(pool, body)

    def on_dve(dve, b, k, first):
        if not first:
            dve.wait_ge(turned, b - 1)
        nc.vector.tensor_tensor(dm[k].rearrange("p (t n) -> p t n", t=TYPES), e.ident[:, :].unsqueeze(1).to_broadcast([P, TYPES, P]),
                                bc(e.typeM[:, bass.ds(b, 1), :].rearrange("p b t -> p (b t)"), P), ALU.mult).then_inc(made, 1)

    def on_pe(pe, b, k, first):
        pe.wait_ge(made, b + 1)
        if not (isinstance(b, int) and b == 0):
            pe.wait_ge(copied, b)
        pe.wait_ge(at_hand, b + 1)
        for n in range(2):
            ins = nc.tensor.matmul(e.ps[:, n, :], e.prod[:, k, 0:P], dm[k][:, n * 512:(n + 1) * 512], start=True, stop=True)
        ins.then_inc(turned, 1)

    def on_act(act, b, k, first):
        act.wait_ge(turned, b + 1)
        if not first:
            act.wait_ge(used, b - 1)
        nc.scalar.activation(hTm[k], e.ps[:, 0:2, :].rearrange("p a n -> p (a n)"), ACT.Copy).then_inc(copied, 1)
    return on_dve, on_pe, on_act, hTm


def typed_weights(nc, A, e, sp, S, layer):
    w = e.wts
    for n, name in enumerate("kqv"):
        sp.dma_start(w[:, KW + n * 1024:KW + (n + 1) * 1024].rearrange("p (t o) -> p t o", t=TYPES),
                     A[f"L3_gnn_W{name}"][layer].rearrange("t i o -> i t o")).then_inc(S["w"], 16)
    sp.dma_start(w[:, WA:WA + 1024].rearrange("p (t o) -> p t o", t=TYPES),
                 A["L3_gnn_Wa"][layer].rearrange("t i o -> i t o")).then_inc(S["w"], 16)
    bd = w[:, BD:BD + 2048].rearrange("p (m r o) -> p m r o", m=2, r=RELS)
    sp.wait_ge(S["bd_zero"], 1)
    for m, name in enumerate(("Watt", "Wmsg")):
        for h in range(L3H):
            sp.dma_start(bd[h * HS3:(h + 1) * HS3, m, :, h * HS3:(h + 1) * HS3],
                         A[f"L3_gnn_{name}"][layer, h].rearrange("r i o -> i r o")).then_inc(S["w"], 16)
    for h in range(L3H):
        sp.dma_start(e.small[h * HS3:(h + 1) * HS3, 320:320 + RELS],
                     A["L3_gnn_pri"][layer, h:h + 1, :].to_broadcast([HS3, RELS])).then_inc(S["w"], 16)


TYPED_LOADS = 16 * (4 + 3 * L3H)


def typed_projections(nc, A, e, block, S, layer):
    w, V = e.wts, nc.vector
    m_dve, m_pe, m_act, hTm = masked_turn(nc, e, block, S, "t", e.hN)
    kv, kv_sb, q_out, rel, staged_k, staged, written = (S[n] for n in (
        "kv_done", "kv_copied", "q_taken", "rel_done", "k_staged", "v_staged", "table_written"))
    stage = [e.rflat[:, k * 2048:(k + 1) * 2048].rearrange("p (r c) -> p r c", r=RELS) for k in range(2)]

    @block.sync
    def _(sp):
        typed_weights(nc, A, e, sp, S, layer)
        t3 = e.t3_d.rearrange("(b p r) c -> b p (r c)", p=P, r=RELS)

        def body(b, k, first):
            sp.wait_ge(staged_k, b + 1)
            sp.wait_ge(staged, b + 1)
            sp.dma_start(t3[bass.ds(b, 1), :, :].rearrange("b p n -> p (b n)"), stage[k].rearrange("p r c -> p (r c)")).then_inc(written_k[k], 16)
        written_k = [S["written_0"], S["written_1"]]
        over_blocks(sp, body)
        sp.wait_ge(S["written_0"], 16 * ((NB + 1) // 2))
        sp.wait_ge(S["written_1"], 16 * (NB // 2))

    def stage_free(eng, b, k, first):
        if not first:
            eng.wait_ge(S[f"written_{k}"], 16 * half(b, k))

    def half(b, k):
        return b // 2 if isinstance(b, int) else (b - k) // 2

    @block.tensor
    def _(pe):
        pe.wait_ge(S["t_ready"], 1)

        def body(b, k, first):
            m_pe(pe, b, k, first)
            pe.wait_ge(S["t_copied"], b + 1)
            if not (isinstance(b, int) and b == 0):
                pe.wait_ge(kv_sb, b)
                pe.wait_ge(q_out, b)
            for t in range(TYPES):
                nc.tensor.matmul(e.ps[:, 2, 0:P], w[:, KW + t * D:KW + (t + 1) * D], hTm[k][:, t * P:(t + 1) * P],
                                 start=(t == 0), stop=(t == TYPES - 1))
            for t in range(TYPES):
                ins = nc.tensor.matmul(e.ps[:, 2, P:2 * P], w[:, KW + 2048 + t * D:KW + 2048 + (t + 1) * D],
                                       hTm[k][:, t * P:(t + 1) * P], start=(t == 0), stop=(t == TYPES - 1))
            ins.then_inc(kv, 1)
            for t in range(TYPES):
                ins = nc.tensor.matmul(e.ps[:, 3, 0:D], hTm[k][:, t * P:(t + 1) * P],
                                       w[:, KW + 1024 + t * D:KW + 1024 + (t + 1) * D], start=(t == 0), stop=(t == TYPES - 1))
            ins.then_inc(S["t_used"], 1)
            pe.wait_ge(kv_sb, b + 1)
            if not (isinstance(b, int) and b == 0):
                pe.wait_ge(staged_k, b)
                pe.wait_ge(staged, b)
            for m in range(2):
                for n in range(2):
                    ins = nc.tensor.matmul(e.ps[:, 4 + 2 * m + n, :], e.ohT[:, k, m * P:(m + 1) * P],
                                           w[:, BD + m * 1024 + n * 512:BD + m * 1024 + (n + 1) * 512], start=True, stop=True)
            ins.then_inc(rel, 1)
        over_blocks(pe, body)

    @block.scalar
    def _(act):
        def body(b, k, first):
            m_act(act, b, k, first)
            act.wait_ge(kv, b + 1)
            if not first:
                act.wait_ge(rel, b - 1)
            nc.scalar.activation(e.ohT[:, k, 0:2 * P], e.ps[:, 2, 0:2 * P], ACT.Copy).then_inc(kv_sb, 1)
            act.wait_ge(rel, b + 1)
            stage_free(act, b, k, first)
            nc.scalar.activation(stage[k][:, :, 0:D], e.ps[:, 4:6, :].rearrange("p a (r c) -> p (a r) c", c=D), ACT.Copy)\
                .then_inc(staged_k, 1)
        over_blocks(act, body)

    def on_dve(dve, c):
        dve.wait_ge(S["w"], TYPED_LOADS)
        c.step(dve, V.tensor_scalar(e.small[:, 320:320 + RELS], e.small[:, 320:320 + RELS], HS3 ** -0.5, None, ALU.mult))
        bd = w[:, BD:BD + 1024].rearrange("p (r o) -> p r o", r=RELS)
        c.step(dve, V.tensor_tensor(bd, bd, bc(e.small[:, 320:320 + RELS], D), ALU.mult))
        V.memset(e.small[:, 0:1], 0.0).then_inc(S["t_ready"], 1)

        def body(b, k, first):
            m_dve(dve, b, k, first)
            dve.wait_ge(S["t_used"], b + 1)
            V.tensor_scalar(e.kN[:, bass.ds(b, 1), :].rearrange("p b d -> p (b d)"), e.ps[:, 3, 0:D], 1.0, None, ALU.mult).then_inc(q_out, 1)
            dve.wait_ge(rel, b + 1)
            stage_free(dve, b, k, first)
            V.tensor_copy(stage[k][:, :, D:2 * D], e.ps[:, 6:8, :].rearrange("p a (r c) -> p (a r) c", c=D)).then_inc(staged, 1)
        over_blocks(dve, body)
        c.step(dve, V.memset(e.acc[:, :], 0.0))
        c.step(dve, V.memset(e.mx[:, :], -BIG))
    return on_dve


def after_l2b(nc, A, e):
    S = Stage(e, "n4")
    V = nc.vector
    with S, nc.Block() as block:
        @block.sync
        def _(sp):
            load_row(nc, sp, e.vecs[:, 128:256], A["L2_gnn_b2"], S["v"])

        @block.scalar
        def _(act):
            norm_sqrt(nc, e, act, S, "ln")

        on_dve = typed_projections(nc, A, e, block, S, 0)

        @block.vector
        def _(dve):
            c = Chain(S["step"])
            V.memset(e.wts[:, BD:BD + 2048], 0.0).then_inc(S["bd_zero"], 1)
            normalized(nc, e, dve, c, e.tA, 1)
            dve.wait_ge(S["v"], 16)
            c.step(dve, V.tensor_tensor(e.tA, e.tA, over(e.vecs[:, 128:256]), ALU.add))
            c.step(dve, V.tensor_tensor(e.xN[:, :, :], e.xN[:, :, :], e.tA, ALU.add))
            norm(nc, e, dve, c, S, "ln", e.xN[:, :, :], e.hN[:, :, :], e.tA, True)
            on_dve(dve, c)


def after_l3(nc, A, e, layer, out):
    S = Stage(e, f"n{5 + layer}")
    V = nc.vector
    w = e.wts
    gam, bet, skip = e.vecs[:, 128:256], e.vecs[:, 256:384], e.vecs[:, 384:384 + TYPES]
    wff, bff = e.vecs[:, 512:640], e.vecs[:, 640:768]
    al = e.r_at[:, 192:192 + NB]
    last = layer == 1
    with S, nc.Block() as block:
        m_dve, m_pe, m_act, hTm = masked_turn(nc, e, block, S, "a", e.tA)

        @block.sync
        def _(sp):
            load_row(nc, sp, gam, A["L3_gnn_ln_g"][layer], S["v"])
            load_row(nc, sp, bet, A["L3_gnn_ln_b"][layer], S["v"])
            load_row(nc, sp, skip, A["L3_gnn_skip"][layer], S["v"])
            sp.dma_start(wff, A["L3_gnn_Wff"]).then_inc(S["v"], 16)
            load_row(nc, sp, bff, A["L3_gnn_bff"], S["v"])
            sp.wait_ge(S["a_used"], NB)

        @block.tensor
        def _(pe):
            pe.wait_ge(S["a_ready"], 1)

            def body(b, k, first):
                m_pe(pe, b, k, first)
                pe.wait_ge(S["a_copied"], b + 1)
                if not (isinstance(b, int) and b == 0):
                    pe.wait_ge(S["y_taken"], b)
                for t in range(TYPES):
                    ins = nc.tensor.matmul(e.ps[:, 2, 0:D], hTm[k][:, t * P:(t + 1) * P], w[:, WA + t * D:WA + (t + 1) * D],
                                           start=(t == 0), stop=(t == TYPES - 1))
                ins.then_inc(S["a_used"], 1)
            over_blocks(pe, body)

        @block.scalar
        def _(act):
            over_blocks(act, lambda b, k, first: m_act(act, b, k, first))
            act.wait_ge(S["z"], 1)
            nc.scalar.activation(al, al, ACT.Exp, scale=-1.0)
            nc.scalar.activation(e.tC, e.tC, ACT.Exp, scale=-1.0).then_inc(S["ez"], 1)
            norm_sqrt(nc, e, act, S, "ln")

        if last:
            project(nc, e, block, S, "f", [(e.hN, wff)], D)

            @block.sync
            def _(sp):
                sp.wait_ge(S["x_done"], 1)
                sp.dma_start(out[0:(NB - 1) * P, :].rearrange("(b p) d -> p b d", p=P), e.xN[:, 0:NB - 1, :]).then_inc(S["out"], 16)
                sp.dma_start(out[(NB - 1) * P:N, :], e.xN[0:NLAST, NB - 1, :]).then_inc(S["out"], 16)
                sp.wait_ge(S["out"], 32)
        else:
            on_dve = typed_projections(nc, A, e, block, S, layer + 1)

        @block.vector
        def _(dve):
            c = Chain(S["step"])
            y, t, u = e.kN[:, :, :], e.tB, e.tC
            normalized(nc, e, dve, c, e.tA, L3H)
            V.memset(e.small[:, 0:1], 0.0).then_inc(S["a_ready"], 1)

            def body(b, k, first):
                m_dve(dve, b, k, first)
                dve.wait_ge(S["a_used"], b + 1)
                V.tensor_scalar(e.kN[:, bass.ds(b, 1), :].rearrange("p b d -> p (b d)"), e.ps[:, 2, 0:D], 1.0, None, ALU.mult).then_inc(S["y_taken"], 1)
            over_blocks(dve, body)
            dve.wait_ge(S["y_taken"], NB)
            dve.wait_ge(S["v"], 16 * 5)
            if not last:
                V.memset(w[:, BD:BD + 2048], 0.0).then_inc(S["bd_zero"], 1)
            tm = u[:, 0:1, :].rearrange("p b d -> p (b d)")
            gate = e.tP[:, 0:NB * TYPES].rearrange("p (b t) -> p b t", t=TYPES)
            c.step(dve, V.tensor_tensor(gate, e.typeM[:, :, :], over(skip), ALU.mult))
            c.step(dve, V.tensor_reduce(al, gate, AX, ALU.add))
            c.step(dve, V.tensor_scalar(al, al, -80.0, None, ALU.max))
            c.step(dve, V.tensor_scalar(u, y, -80.0, None, ALU.max))
            V.memset(e.small[:, 0:1], 0.0).then_inc(S["z"], 1)
            dve.wait_ge(S["ez"], 1)
            c.step(dve, V.tensor_scalar(al, al, 1.0, None, ALU.add))
            c.step(dve, V.reciprocal(al, al))
            c.step(dve, V.tensor_scalar(u, u, 1.0, None, ALU.add))
            c.step(dve, V.reciprocal(u, u))
            c.step(dve, V.tensor_tensor(t, y, u, ALU.mult))
            c.step(dve, V.tensor_tensor(t, t, e.hN[:, :, :], ALU.subtract))
            c.step(dve, V.tensor_tensor(t, t, bc(al, D), ALU.mult))
            c.step(dve, V.tensor_tensor(t, t, e.hN[:, :, :], ALU.add))
            norm(nc, e, dve, c, S, "ln", t, u, e.tA, False)
            c.step(dve, V.tensor_tensor(u, u, over(gam), ALU.mult))
            c.step(dve, V.tensor_tensor(e.hN[:, :, :], u, over(bet), ALU.add))
            if last:
                V.memset(e.small[:, 0:1], 0.0).then_inc(S["f_ready"], 1)

                def take(b, k, first):
                    dve.wait_ge(S["f_done"], b + 1)
                    V.tensor_tensor(e.kN[:, bass.ds(b, 1), :].rearrange("p b d -> p (b d)"), e.ps[:, 2 + k, 0:D], bff,
                                    ALU.add).then_inc(S["f_taken"], 1)
                over_blocks(dve, take)
                dve.wait_ge(S["f_taken"], NB)
                c.step(dve, V.tensor_tensor(e.xN[:, :, :], e.xN[:, :, :], e.kN[:, :, :], ALU.add))
                V.memset(e.small[:, 0:1], 0.0).then_inc(S["x_done"], 1)
            else:
                on_dve(dve, c)


_INS = ["x", "src", "dst", "edge_type_8", "edge_weight", "node_type_8", "L0_gnn_W1", "L0_gnn_b1", "L0_gnn_W2", "L0_gnn_b2",
        "L1_gnn_Wq", "L1_gnn_bq", "L1_gnn_Wk", "L1_gnn_bk", "L1_gnn_Wv", "L1_gnn_bv", "L1_gnn_Ws", "L1_gnn_bs", "L1_gnn_Wg",
        "L1_gnn_bg", "L1_gnn_gamma", "L1_gnn_beta", "L1_gnn_alpha", "L2_gnn_Wl1", "L2_gnn_bl1", "L2_gnn_Wr1", "L2_gnn_br1",
        "L2_gnn_att1", "L2_gnn_b1", "L2_gnn_Wl2", "L2_gnn_bl2", "L2_gnn_Wr2", "L2_gnn_br2", "L2_gnn_att2", "L2_gnn_b2",
        "L3_gnn_Wk", "L3_gnn_Wq", "L3_gnn_Wv", "L3_gnn_Wa", "L3_gnn_pri", "L3_gnn_Watt", "L3_gnn_Wmsg", "L3_gnn_skip",
        "L3_gnn_ln_g", "L3_gnn_ln_b", "L3_gnn_Wff", "L3_gnn_bff"]


def kernel(**inputs):
    import concourse.bacc as bacc
    from concourse.bass_utils import run_bass_kernel_spmd as run

    nc = bacc.Bacc("TRN2", target_bir_lowering=False, num_devices=1)
    arrays, A = {}, {}
    for name in _INS:
        a = np.ascontiguousarray(inputs[name])
        if a.ndim == 0:
            a = a.reshape(1)
        arrays[f"in_{name}"] = a
        A[name] = nc.dram_tensor(f"in_{name}", a.shape, mybir.dt.from_np(a.dtype), kind="ExternalInput").ap()
    out = nc.dram_tensor("out_nodes", (N, D), F32, kind="ExternalOutput").ap()
    build(nc, A, out)
    r = run(nc, [arrays], core_ids=[0])
    return r.results[0]["out_nodes"]
```

```python
from contextlib import ExitStack

import numpy as np

import concourse.bass as bass
from concourse import mybir

F32 = mybir.dt.float32
I32 = mybir.dt.int32
ALU = mybir.AluOpType
ACT = mybir.ActivationFunctionType
AX = mybir.AxisListType.X

P = 128
N = 3125
D = 128
E = 103125
NB = (N + P - 1) // P
NPAD = NB * P
NLAST = N - (NB - 1) * P
EPC = (E + P - 1) // P
ELAST = E - (P - 1) * EPC
GC = 4
CE = GC * P
J = 4
GT = GC * J
NC_MAX = (E + NB * (CE - 1)) // CE
NG = (NC_MAX + J - 1) // J
NV = NG * J
HALF = NV // 2
NT = NV * GC
PAD_ROWS = 8 * P
EPAD = P * EPC + PAD_ROWS
NO_NODE = 4000.0
BIG = 1.0e30
TYPES = 8
RELS = 8
L3H = 8
HS3 = D // L3H


MAX_STEPS = J + 7
ACC_STEPS = 1 + 2 * J


def bc(ap, n):
    return ap.unsqueeze(len(ap.shape)).to_broadcast(list(ap.shape) + [n])


class Shared:
    pass


class Chain:

    def __init__(self, sem):
        self.sem, self.n = sem, 0

    def step(self, eng, ins):
        self.n += 1
        ins.then_inc(self.sem, 1)
        eng.wait_ge(self.sem, self.n)


class Signal:

    def __init__(self, sem, per_pass):
        self.sem, self.per_pass = sem, per_pass

    def wait(self, eng, pass_no, n):
        if isinstance(n, int) and pass_no * self.per_pass + n <= 0:
            return
        eng.wait_ge(self.sem, n + pass_no * self.per_pass)


IN_BOUNDS = "prepare() computes the numbers within these bounds"


def over_blocks(eng, body):
    body(0, 0, True)
    body(1, 1, True)
    with eng.Fori(0, (NB - 3) // 2) as i:
        body(2 * i + 2, 0, False)
        body(2 * i + 3, 1, False)
    body(NB - 1, 0, False)


def ahead(part, eng, b, k):
    if isinstance(b, int):
        if b < NB - 1:
            part(eng, b + 1, 1 - k, b == 0)
    else:
        part(eng, b + 1, 1 - k, False)


def build(nc, A, out):
    st = ExitStack()
    with st:
        def sb(name, shape, dt=F32):
            return st.enter_context(nc.sbuf_tensor(name, shape, dt))[tuple(slice(None) for _ in shape)]

        def sem(name):
            return st.enter_context(nc.semaphore(name))

        def table(name, shape, dt=F32):
            return nc.dram_tensor(name, shape, dt, kind="Internal").ap()

        edges_d = table("edges_sorted", (EPAD, 4), I32)
        seg_d = table("segment_flags", (NV, CE + 4))
        t0_d = table("table_l0", (NPAD, D))
        t1_d = table("table_l1", (NPAD, 2 * D))
        t2_d = table("table_l2", (NPAD, D))
        t3_d = table("table_l3", (NPAD * RELS, 2 * D))

        xN = sb("x_nodes", [P, NB, D])
        hN = sb("h_nodes", [P, NB, D])
        kN = sb("dst_side", [P, NB, D])
        acc = sb("acc", [P, NB * 136])
        mx = sb("running_max", [P, NB * 8])
        srcE = sb("src_edges", [P, NT], I32)
        relE = sb("src_rel_edges", [P, NT], I32)
        ewE = sb("weight_edges", [P, NT])
        dlE = sb("dst_local_edges", [P, NT])
        lastE = sb("last_of_segment", [P, NT])
        blkI = sb("chunk_block", [P, NV], I32)
        startI = sb("chunk_start", [P, NV], I32)
        ident = sb("ident", [P, P])
        iotaF = sb("iota_row", [P, P])
        onesF = sb("ones", [P, P])
        typeM = sb("type_mask", [P, NB, TYPES])
        wts = sb("weights", [P, 6288])
        small = sb("small", [P, 512])
        rows = sb("gathered_rows", [P, 2, GT * 2 * D])
        oh = sb("onehot", [P, 2, GT, P])
        ohT = sb("onehot_t", [P, 2, CE])
        prod = sb("products", [P, 2, CE])
        exv = sb("weighted_rows", [P, GT * 144])
        segF = sb("segment_flags_sb", [32, 2, CE + 4])
        segS = sb("segment_work", [32, 2, CE])
        exT = sb("exp_scores_t", [32, CE])
        sc = sb("scores", [P, 2, J * GC * 8])
        exb = sb("exps_and_maxima", [P, 2 * J * GC * 8])
        idx = sb("gather_index", [P, 2, GT], I32)
        ps = st.enter_context(nc.psum_tensor("ps", [P, 8, 512], F32))

        rflat = rows[:, :, :].rearrange("p u n -> p (u n)")
        tA = rflat[:, 0:NB * D].rearrange("p (b d) -> p b d", d=D)
        tB = rflat[:, NB * D:2 * NB * D].rearrange("p (b d) -> p b d", d=D)
        tC = oh[:, :, :, :].rearrange("p u t n -> p (u t n)")[:, 0:NB * D].rearrange("p (b d) -> p b d", d=D)
        skN = wts[:, 3072:3072 + NB * D].rearrange("p (b d) -> p b d", d=D)

        tP = sb("scaled_partial", [P, J * 136])
        mwork = sb("max_work", [P, 8, J * 8])
        pairs = sb("chunk_pairs_work", [P, J * J * 8])
        samePair = sb("same_block_pairs", [P, NG * J * J])
        firstE = sb("first_of_block", [P, NV])
        vecs = sb("vectors", [P, 1024])
        r_at = sb("row_scalars", [P, 8 * 32])

        rows_here = [[Signal(sem(f"rows_here_{u}{j}"), 64 * ((NG + 1 - u) // 2)) for j in range(J)] for u in range(2)]
        gate = sem("gate")
        idx_ready = Signal(sem("idx_ready"), NG)
        oh_ready = Signal(sem("onehot_ready"), NV)
        p_ready = Signal(sem("partial_ready"), NV)
        added = Signal(sem("partial_added"), NV)
        flags_here = [Signal(sem(f"flags_here_{u}"), 16 * J * ((NG + 1 - u) // 2)) for u in range(2)]
        oht_made = Signal(sem("onehot_t_in_psum"), NV)
        oht_ready = Signal(sem("onehot_t_ready"), NV)
        kd_ready = Signal(sem("dst_rows_ready"), NV)
        lr_ready = Signal(sem("pair_sums_in_sbuf"), NV)
        leaky_done = Signal(sem("leaky_done"), NV)
        prod_ready = Signal(sem("product_ready"), NV)
        score_ready = Signal(sem("score_ready"), NV)
        st_ready = Signal(sem("scores_t_ready"), NG)
        scan_step = Signal(sem("scan_step"), 2 * NG)
        seg_ready = Signal(sem("segment_max_ready"), NG)
        ex_ready = Signal(sem("exp_ready"), NG)
        back_ready = Signal(sem("exp_back_ready"), NG)
        exb_ready = Signal(sem("exp_in_sbuf"), NG)
        exv_ready = Signal(sem("weighted_rows_ready"), NV)
        excol_ready = Signal(sem("exp_columns_ready"), NG)
        max_step = Signal(sem("max_step"), MAX_STEPS * NG)
        max_kept = Signal(sem("max_kept"), J * NG)
        acc_step = Signal(sem("acc_step"), ACC_STEPS * NG)
        d2_ready = Signal(sem("shift_ready"), NG)
        e2_ready = Signal(sem("shift_exp_ready"), NG)

        env = Shared()
        env.acc, env.acc_step, env.added, env.back_ready, env.blkI = acc, acc_step, added, back_ready, blkI
        env.d2_ready, env.dlE, env.e2_ready, env.edges_d, env.ewE = d2_ready, dlE, e2_ready, edges_d, ewE
        env.exT, env.ex_ready, env.exb, env.exb_ready, env.excol_ready = exT, ex_ready, exb, exb_ready, excol_ready
        env.exv, env.exv_ready, env.firstE, env.flags_here, env.gate = exv, exv_ready, firstE, flags_here, gate
        env.hN, env.ident, env.idx, env.idx_ready, env.iotaF = hN, ident, idx, idx_ready, iotaF
        env.kN, env.kd_ready, env.lastE, env.leaky_done, env.lr_ready = kN, kd_ready, lastE, leaky_done, lr_ready
        env.max_kept, env.max_step, env.mwork, env.mx, env.nc = max_kept, max_step, mwork, mx, nc
        env.oh, env.ohT, env.oh_ready, env.oht_made, env.oht_ready = oh, ohT, oh_ready, oht_made, oht_ready
        env.onesF, env.p_ready, env.pairs, env.prod, env.prod_ready = onesF, p_ready, pairs, prod, prod_ready
        env.ps, env.r_at, env.relE, env.rflat, env.rows = ps, r_at, relE, rflat, rows
        env.rows_here, env.samePair, env.sc, env.scan_step, env.score_ready = rows_here, samePair, sc, scan_step, score_ready
        env.segF, env.segS, env.seg_d, env.seg_ready, env.sem = segF, segS, seg_d, seg_ready, sem
        env.skN, env.small, env.srcE, env.st_ready, env.startI = skN, small, srcE, st_ready, startI
        env.t0_d, env.t1_d, env.t2_d, env.t3_d, env.tA = t0_d, t1_d, t2_d, t3_d, tA
        env.tB, env.tC, env.tP, env.table, env.typeM = tB, tC, tP, table, typeM
        env.vecs, env.wts, env.xN = vecs, wts, xN
        prepare(nc, A, env)
        first_norm(nc, A, env)
        weighted_pass(nc, env)
        after_l0(nc, A, env)
        attention_pass(nc, env, 1, H=4, table=t1_d, width=2 * D, index=srcE, scale=32 ** -0.5, gat=False)
        after_l1(nc, A, env)
        attention_pass(nc, env, 2, H=4, table=t2_d, width=D, index=srcE, scale=1.0, gat=True)
        after_l2a(nc, A, env)
        attention_pass(nc, env, 3, H=1, table=t2_d, width=D, index=srcE, scale=1.0, gat=True)
        after_l2b(nc, A, env)
        attention_pass(nc, env, 4, H=L3H, table=t3_d, width=2 * D, index=relE, scale=1.0, gat=False)
        after_l3(nc, A, env, 0, out)
        attention_pass(nc, env, 5, H=L3H, table=t3_d, width=2 * D, index=relE, scale=1.0, gat=False)
        after_l3(nc, A, env, 1, out)
    return nc


def prepare(nc, A, e):
    sem = e.sem
    rflat, oh, small, ps = e.rflat, e.oh, e.small, e.ps
    ident, iotaF, onesF = e.ident, e.iotaF, e.onesF
    edges_d, xN = e.edges_d, e.xN
    V = nc.vector
    pay = rflat[:, 0:4 * EPC].rearrange("p (c f) -> p c f", f=4)
    tail = rflat[:, 4 * EPC:4 * EPC + 4 * (PAD_ROWS // P)].rearrange("p (c f) -> p c f", f=4)
    dstF = rflat[:, 4000:4000 + EPC]
    scratch = rflat[:, 5000:5000 + EPC]
    ohf = oh[:, :, :, :].rearrange("p u t n -> p (u t n)")
    raw = [ohf[:, f * EPC:(f + 1) * EPC] for f in range(4)]
    names = ["src", "dst", "edge_type_8", "edge_weight"]
    loaded, zeroed, consts, built, stored, checked, check_sum, nodes_in = (sem(n) for n in (
        "edges_loaded", "pads_zeroed", "consts_made", "payload_built", "payload_stored", "order_checked",
        "order_summed", "nodes_loaded"))
    ntI = small[:, 160:192].bitcast(I32)
    nextI = small[:, 262:263].bitcast(I32)
    nextF = small[:, 263:264]
    bad = small[:, 264:266]
    flagI = small[:, 266:267].bitcast(I32)
    chain = Chain(sem("prepare_step"))

    with nc.Block() as block:
        @block.gpsimd
        def _(pool):
            pool.memset(ident[:, :], 0.0).then_inc(consts, 1)
            pool.memset(onesF[:, :], 1.0).then_inc(consts, 1)
            pool.wait_ge(consts, 2)
            pool.affine_select(out=ident[:, :], in_=ident[:, :], compare_op=ALU.not_equal, fill=1.0,
                               base=0, pattern=[[-1, P]], channel_multiplier=1).then_inc(consts, 1)
            pool.iota(iotaF[:, :].bitcast(I32), pattern=[[1, P]], base=0, channel_multiplier=0).then_inc(consts, 1)

        @block.sync
        def _(sp):
            sp.wait_ge(zeroed, 7)
            for f, name in enumerate(names):
                dst = raw[f] if name == "edge_weight" else raw[f].bitcast(I32)
                a = A[name]
                sp.dma_start(dst[0:P - 1, :], a[0:(P - 1) * EPC].rearrange("(p c) -> p c", c=EPC)).then_inc(loaded, 16)
                sp.dma_start(dst[P - 1:P, 0:ELAST], a[(P - 1) * EPC:E].rearrange("(p c) -> p c", c=ELAST)).then_inc(loaded, 16)
            with nc.allow_non_contiguous_dma(reason="one destination a partition"):
                firsts = A["dst"][EPC:(P - 1) * EPC].rearrange("(p c) -> p c", c=EPC)[:, 0:1]
                sp.dma_start(nextI[0:P - 2, :], firsts).then_inc(loaded, 16)
                last = A["dst"][(P - 1) * EPC:(P - 1) * EPC + 1].rearrange("(p c) -> p c", c=1)
                sp.dma_start(nextI[P - 2:P - 1, :], last).then_inc(loaded, 16)
            x = A["x"]
            sp.dma_start(xN[:, 0:NB - 1, :], x[0:(NB - 1) * P, :].rearrange("(b p) d -> p b d", p=P)).then_inc(nodes_in, 16)
            sp.dma_start(xN[0:NLAST, NB - 1, :], x[(NB - 1) * P:N, :]).then_inc(nodes_in, 16)
            t = A["node_type_8"]
            with nc.allow_non_contiguous_dma(reason="12 KB of node types"):
                sp.dma_start(ntI[:, 0:NB - 1], t[0:(NB - 1) * P].rearrange("(b p) -> p b", p=P)).then_inc(nodes_in, 16)
                sp.dma_start(ntI[0:NLAST, NB - 1:NB], t[(NB - 1) * P:N].rearrange("(p b) -> p b", b=1)).then_inc(nodes_in, 16)
            sp.wait_ge(built, 1)
            sp.dma_start(edges_d[0:P * EPC, :].rearrange("(p c) f -> p c f", p=P), pay.bitcast(I32)).then_inc(stored, 16)
            sp.dma_start(edges_d[P * EPC:EPAD, :].rearrange("(p c) f -> p c f", p=P), tail.bitcast(I32)).then_inc(stored, 16)
            sp.wait_ge(stored, 32)
            sp.wait_ge(nodes_in, 64)

        @block.vector
        def _(dve):
            c = chain
            V.memset(raw[0].bitcast(I32), 0).then_inc(zeroed, 1)
            V.memset(raw[1].bitcast(I32), int(NO_NODE)).then_inc(zeroed, 1)
            V.memset(raw[2].bitcast(I32), 0).then_inc(zeroed, 1)
            V.memset(raw[3], 0.0).then_inc(zeroed, 1)
            V.memset(xN[:, NB - 1, :], 0.0).then_inc(zeroed, 1)
            V.memset(ntI[:, 0:32], 0).then_inc(zeroed, 1)
            V.memset(nextI, int(NO_NODE)).then_inc(zeroed, 1)
            c.step(dve, V.memset(tail, 0.0))
            c.step(dve, V.memset(tail.bitcast(I32)[:, :, 1], int(NO_NODE)))
            dve.wait_ge(consts, 4)
            c.step(dve, V.tensor_copy(iotaF[:, :], iotaF[:, :].bitcast(I32)))
            dve.wait_ge(loaded, 16 * 10)
            for f in range(4):
                if names[f] == "edge_weight":
                    ins = V.tensor_copy(pay[:, :, f], raw[f])
                else:
                    ins = V.tensor_copy(pay.bitcast(I32)[:, :, f], raw[f].bitcast(I32))
            ins.then_inc(built, 1)
            c.step(dve, V.tensor_copy(dstF, raw[1].bitcast(I32)))
            c.step(dve, V.tensor_copy(nextF, nextI))
            c.step(dve, V.tensor_tensor(scratch[:, 0:EPC - 1], dstF[:, 0:EPC - 1], dstF[:, 1:EPC], ALU.is_gt))
            c.step(dve, V.tensor_reduce(bad[:, 0:1], scratch[:, 0:EPC - 1], AX, ALU.max))
            V.tensor_tensor(bad[:, 1:2], dstF[:, EPC - 1:EPC], nextF, ALU.is_gt).then_inc(checked, 1)
            dve.wait_ge(check_sum, 1)
            c.step(dve, V.tensor_reduce(nextF, ps[:, 0, 0:2], AX, ALU.max))
            c.step(dve, V.tensor_scalar(flagI, nextF, 0.5, None, ALU.is_gt))

        @block.tensor
        def _(pe):
            pe.wait_ge(consts, 2)
            pe.wait_ge(checked, 1)
            nc.tensor.matmul(ps[:, 0, 0:2], onesF[:, :], bad, start=True, stop=True).then_inc(check_sum, 1)

    out_of_order = nc.values_load(flagI[0:1, 0:1], min_val=0, max_val=1)
    with nc.If(out_of_order):
        sort_edges(nc, e, pay, dstF, scratch, edges_d)
    nc.end_ifs()
    cut_chunks(nc, e, dstF, scratch, ntI)


def sort_edges(nc, e, pay, dstF, cum, edges_d):
    sem, ps, onesF = e.sem, e.ps, e.onesF
    V = nc.vector
    mask, place, ones, term = (e.wts[:, n * EPC:(n + 1) * EPC] for n in range(4))
    placeI = e.rows[:, 1, 2048:2048 + EPC].bitcast(I32)
    s = e.small
    tri, node, base, off, total = e.oh[:, 0, 0, :], s[:, 270:271], s[:, 271:272], s[:, 272:273], s[:, 273:274]
    stage_rows = [s[:, 280 + 4 * k:284 + 4 * k].bitcast(I32) for k in range(2)]
    stage_place = [s[:, 290 + k:291 + k].bitcast(I32) for k in range(2)]
    made, set_up, step, counted, summed, placed = (sem(f"sort_{n}") for n in (
        "triangle_made", "set_up", "step", "node_counted", "node_summed", "places_made"))
    staged, gone = sem("sort_staged"), [sem("sort_gone_0"), sem("sort_gone_1")]
    PER = 9

    with nc.Block() as block:
        @block.gpsimd
        def _(pool):
            pool.memset(tri, 1.0).then_inc(made, 1)
            pool.iota(placeI, pattern=[[1, EPC]], base=0, channel_multiplier=EPC).then_inc(made, 1)
            pool.wait_ge(made, 2)
            pool.affine_select(out=tri, in_=tri, compare_op=ALU.is_gt, fill=0.0, base=0, pattern=[[1, P]],
                               channel_multiplier=-1).then_inc(made, 1)
            pool.wait_ge(placed, 1)
            with pool.Fori(0, EPC // 2) as i:
                for k in range(2):
                    pool.wait_ge(gone[k], 16 * i)
                    nc.gpsimd.tensor_copy(stage_rows[k], pay.bitcast(I32)[:, bass.ds(2 * i + k, 1), :].rearrange("p c f -> p (c f)"))
                    nc.gpsimd.tensor_copy(stage_place[k], placeI[:, bass.ds(2 * i + k, 1)]).then_inc(staged, 1)
                    pool.wait_ge(staged, 2 * i + k + 1)
                    pool.sem_inc(e.gate, 1)
                    pool.indirect_dma_start(out=edges_d, out_offset=bass.IndirectOffsetOnAxis(ap=stage_place[k], axis=0),
                                            in_=stage_rows[k], in_offset=None).then_inc(gone[k], 16)
            for k in range(2):
                pool.wait_ge(gone[k], 16 * (EPC // 2))

        @block.vector
        def _(dve):
            c = Chain(set_up)
            dve.wait_ge(made, 2)
            c.step(dve, V.tensor_copy(place, placeI))
            c.step(dve, V.tensor_scalar(term, dstF, float(N), None, ALU.is_ge))
            c.step(dve, V.tensor_tensor(place, place, term, ALU.mult))
            c.step(dve, V.memset(ones, 1.0))
            c.step(dve, V.memset(node, 0.0))
            c.step(dve, V.memset(base, -1.0))
            with dve.Fori(0, N) as i:
                n = 0

                def do(ins, wait=True):
                    nonlocal n
                    n += 1
                    ins.then_inc(step, 1)
                    if wait:
                        dve.wait_ge(step, PER * i + n)
                do(V.tensor_scalar(mask, dstF, node, None, ALU.is_equal))
                do(V.tensor_tensor_scan(cum, ones, mask, 0.0, ALU.mult, ALU.add))
                do(V.tensor_scalar(total, cum[:, EPC - 1:EPC], 1.0, None, ALU.mult))
                V.memset(s[:, 275:276], 0.0).then_inc(counted, 1)
                dve.wait_ge(summed, i + 1)
                do(V.tensor_tensor(off, base, ps[:, 0, 0:1], ALU.add))
                do(V.tensor_tensor(base, base, ps[:, 0, 1:2], ALU.add))
                do(V.scalar_tensor_tensor(term, cum, off, mask, ALU.add, ALU.mult))
                do(V.tensor_tensor(place, place, term, ALU.add))
                do(V.tensor_scalar(node, node, 1.0, None, ALU.add))
                do(V.memset(s[:, 276:277], 0.0))
                assert n == PER
            V.tensor_copy(placeI, place).then_inc(placed, 1)

        @block.sync
        def _(sp):
            sp.wait_ge(placed, 1)

        @block.scalar
        def _(act):
            act.wait_ge(placed, 1)

        @block.tensor
        def _(pe):
            pe.wait_ge(made, 3)
            with pe.Fori(0, N) as i:
                pe.wait_ge(counted, i + 1)
                nc.tensor.matmul(ps[:, 0, 0:1], tri, total, start=True, stop=True)
                nc.tensor.matmul(ps[:, 0, 1:2], onesF[:, :], total, start=True, stop=True).then_inc(summed, 1)


def cut_chunks(nc, e, dstF, scratch, ntI):
    sem = e.sem
    rflat, oh, small, ps = e.rflat, e.oh, e.small, e.ps
    ident, onesF, edges_d, seg_d, typeM = e.ident, e.onesF, e.edges_d, e.seg_d, e.typeM
    srcE, relE, ewE, dlE, lastE, blkI, startI = e.srcE, e.relE, e.ewE, e.dlE, e.lastE, e.blkI, e.startI
    V = nc.vector
    ohf = oh[:, :, :, :].rearrange("p u t n -> p (u t n)")
    consts, counted, totals, visits, meta_in, meta_cut, tposed, flagged, flags_out, back, cut = (sem(n) for n in (
        "chunk_numbers", "counts_made", "totals_made", "chunks_placed", "chunks_loaded", "chunks_cut", "dst_turned",
        "flags_made", "flags_stored", "last_back", "cut_step"))
    cnt = small[:, 0:32]
    R = small[:, 32:64]
    Cs = small[:, 64:96]
    g = small[:, 96:128]
    nci = small[:, 128:160].bitcast(I32)
    ntF = small[:, 192:224]
    t25 = small[:, 224:256]
    iotaI = ohf[:, 3300:3300 + NV].bitcast(I32)
    iotaV = ohf[:, 3530:3530 + NV]
    blkF = ohf[:, 3760:3760 + NV]
    meta = rflat[:, 0:NV * 16].bitcast(I32).rearrange("p (v g f) -> p v g f", g=GC, f=4)
    startF = rflat[:, 6000:6000 + NV]
    geF = rflat[:, 6300:6300 + NV]
    relF = rflat[:, 4000:4000 + NT]
    dT = [ohf[:, h * 1040:h * 1040 + CE] for h in range(2)]
    fT = [ohf[:, 520 + h * 1040:520 + h * 1040 + CE + 4] for h in range(2)]

    pool_meta_in = sem("chunks_loaded_by_pool")

    def load_chunks(eng, engine, part, done):
        with eng.Fori(0, NV // 12) as i:
            _, starts = nc.values_load_multi_w_load_instructions(
                startI[0:1, bass.ds(12 * i + 4 * part, 4)], engines=[engine], min_val=0, max_val=E,
                skip_runtime_bounds_check_because=IN_BOUNDS)
            for n, start in enumerate(starts):
                eng.dma_start(meta[:, bass.ds(12 * i + 4 * part + n, 1), :, :].rearrange("p v g f -> p (v g f)"),
                              edges_d[bass.ds(start, CE), :].rearrange("(p g) f -> p (g f)", g=GC)).then_inc(done, 16)

    with nc.Block() as block:
        @block.gpsimd
        def _(pool):
            pool.iota(iotaI, pattern=[[1, NV]], base=0, channel_multiplier=0).then_inc(consts, 1)
            pool.wait_ge(visits, 1)
            load_chunks(pool, mybir.EngineType.Pool, 2, pool_meta_in)

        @block.sync
        def _(sp):
            sp.wait_ge(visits, 1)
            load_chunks(sp, mybir.EngineType.SP, 0, meta_in)
            for h in range(2):
                sp.wait_ge(flagged, h + 1)
                sp.dma_start(seg_d[h * HALF:(h + 1) * HALF, :], fT[h][0:HALF, :]).then_inc(flags_out, 16)
            sp.wait_ge(flags_out, 32)

        @block.scalar
        def _(act):
            act.wait_ge(visits, 1)
            load_chunks(act, mybir.EngineType.Activation, 1, meta_in)

        @block.vector
        def _(dve):
            c = Chain(cut)
            dve.wait_ge(consts, 1)
            c.step(dve, V.tensor_copy(iotaV, iotaI))
            for b in range(1, NB):
                c.step(dve, V.tensor_scalar(scratch, dstF, float(b * P), 0.0, ALU.is_lt, ALU.add, accum_out=cnt[:, b:b + 1]))
            V.memset(small[:, 258:259], 0.0).then_inc(counted, 1)
            dve.wait_ge(totals, 1)
            V.tensor_copy(R[:, 1:NB], ps[:, 0, 1:NB])
            V.memset(R[:, 0:1], 0.0)
            c.step(dve, V.memset(R[:, NB:NB + 1], float(E)))
            c.step(dve, V.tensor_tensor(t25[:, 0:NB], R[:, 1:NB + 1], R[:, 0:NB], ALU.subtract))
            c.step(dve, V.tensor_scalar(nci[:, 0:NB], t25[:, 0:NB], float(CE - 1), None, ALU.add))
            c.step(dve, V.tensor_scalar(nci[:, 0:NB], nci[:, 0:NB], 9, None, ALU.logical_shift_right))
            c.step(dve, V.tensor_copy(t25[:, 0:NB], nci[:, 0:NB]))
            V.memset(Cs[:, 0:1], 0.0)
            c.step(dve, V.tensor_tensor_scan(Cs[:, 1:NB + 1], onesF[:, 0:NB], t25[:, 0:NB], 0.0, ALU.mult, ALU.add))
            c.step(dve, V.scalar_tensor_tensor(g[:, 0:NB], Cs[:, 0:NB], -float(CE), R[:, 0:NB], ALU.mult, ALU.add))
            c.step(dve, V.tensor_tensor(t25[:, 1:NB], g[:, 1:NB], g[:, 0:NB - 1], ALU.subtract))
            V.memset(blkF, 0.0)
            c.step(dve, V.tensor_scalar(startF, iotaV, float(CE), None, ALU.mult))
            for b in range(1, NB):
                c.step(dve, V.scalar_tensor_tensor(blkF, iotaV, Cs[:, b:b + 1], blkF, ALU.is_ge, ALU.add))
                c.step(dve, V.tensor_scalar(geF, iotaV, Cs[:, b:b + 1], t25[:, b:b + 1], ALU.is_ge, ALU.mult))
                c.step(dve, V.tensor_tensor(startF, startF, geF, ALU.add))
            V.tensor_scalar(startI[:, :], startF, float(E), None, ALU.min)
            c.step(dve, V.tensor_copy(blkI[:, :], blkF))
            b4 = blkF.rearrange("p (n j) -> p n j", j=J)
            same = e.samePair.rearrange("p (n j k) -> p n j k", j=J, k=J)
            c.step(dve, V.tensor_tensor(same, bc(b4, J), b4.unsqueeze(2).to_broadcast([P, NG, J, J]), ALU.is_equal))
            c.step(dve, V.tensor_scalar(e.samePair, e.samePair, -1.0, BIG, ALU.add, ALU.mult))
            c.step(dve, V.tensor_tensor(e.firstE[:, 1:NV], blkF[:, 1:NV], blkF[:, 0:NV - 1], ALU.not_equal))
            c.step(dve, V.memset(e.firstE.rearrange("p (n j) -> p n j", j=J)[:, :, 0], 1.0))
            c.step(dve, V.tensor_scalar(blkF, blkF, float(P), None, ALU.mult))
            V.memset(small[:, 256:257], 0.0).then_inc(visits, 1)
            c.step(dve, V.tensor_copy(ntF, ntI))
            for t in range(TYPES):
                V.tensor_scalar(typeM[:, :, t], ntF[:, 0:NB], float(t), None, ALU.is_equal)
            dve.wait_ge(meta_in, 16 * NV * 2 // 3)
            dve.wait_ge(pool_meta_in, 16 * NV // 3)
            m2 = meta.rearrange("p v g f -> p (v g) f")
            V.tensor_copy(srcE[:, :], m2[:, :, 0])
            V.tensor_copy(ewE[:, :], m2.bitcast(F32)[:, :, 3])
            V.tensor_copy(relF, m2[:, :, 2])
            c.step(dve, V.tensor_copy(dlE[:, :], m2[:, :, 1]))
            c.step(dve, V.scalar_tensor_tensor(relE[:, :], m2[:, :, 0], float(RELS), relF, ALU.mult, ALU.add))
            c.step(dve, V.tensor_tensor(dlE[:, :].rearrange("p (v g) -> p v g", g=GC),
                                        dlE[:, :].rearrange("p (v g) -> p v g", g=GC), bc(blkF, GC), ALU.subtract))
            V.memset(small[:, 257:258], 0.0).then_inc(meta_cut, 1)
            for h in range(2):
                dve.wait_ge(tposed, h + 1)
                c.step(dve, V.tensor_scalar(dT[h][0:HALF, :], ps[0:HALF, h, 0:CE], 2.0 ** 100, None, ALU.mult))
                V.memset(fT[h][0:HALF, 0:1], 0.0)
                V.memset(fT[h][0:HALF, CE:CE + 4], 0.0)
                c.step(dve, V.tensor_tensor(fT[h][0:HALF, 1:CE], dT[h][0:HALF, 0:CE - 1], dT[h][0:HALF, 1:CE], ALU.subtract))
                c.step(dve, V.tensor_scalar(dT[h][0:HALF, 0:CE - 1], fT[h][0:HALF, 1:CE], 0.0, None, ALU.is_lt))
                V.memset(dT[h][0:HALF, CE - 1:CE], 1.0).then_inc(flagged, 1)
            dve.wait_ge(back, 1)
            V.tensor_copy(lastE[:, :].rearrange("p (v g) -> p g v", g=GC),
                          ps[:, 2:6, 0:NV]).then_inc(cut, 1)

        @block.tensor
        def _(pe):
            pe.wait_ge(counted, 1)
            nc.tensor.matmul(ps[:, 0, 1:NB], onesF[:, :], cnt[:, 1:NB], start=True, stop=True).then_inc(totals, 1)
            pe.wait_ge(meta_cut, 1)
            dl = dlE[:, :].rearrange("p (v g) -> p v g", g=GC)
            for h in range(2):
                for q in range(GC):
                    ins = nc.tensor.transpose(ps[0:HALF, h, q:CE:GC], dl[:, h * HALF:(h + 1) * HALF, q], ident[:, :])
                ins.then_inc(tposed, 1)
            for h in range(2):
                pe.wait_ge(flagged, h + 1)
                for q in range(GC):
                    ins = nc.tensor.transpose(ps[:, 2 + q, h * HALF:(h + 1) * HALF], dT[h][0:HALF, q:CE:GC], ident[0:HALF, 0:HALF])
            ins.then_inc(back, 1)



def block_numbers(nc, e, engine, chunk, n):
    _, values = nc.values_load_multi_w_load_instructions(e.blkI[0:1, bass.ds(chunk, n)], engines=[engine], min_val=0,
                                                         max_val=NB - 1, skip_runtime_bounds_check_because=IN_BOUNDS)
    return values


def turns(eng, slot, first, last):
    pairs = (last - first) // 2
    with eng.Fori(0, pairs) as i:
        for k in range(2):
            s = first + k
            slot(2 * i + s, s % 2, i + s // 2)
    for s in range(first + 2 * pairs, last):
        slot(s, s % 2, s // 2)


def gather_rows(nc, e, block, pass_no, table, width, index, free, free_before):
    rv = e.rows[:, :, 0:GT * width].rearrange("p u (t d) -> p u t d", d=width)

    @block.gpsimd
    def _(pool):
        def group(s, u, q):
            if not (isinstance(s, int) and s < 2):
                for j in range(J):
                    e.rows_here[u][j].wait(pool, pass_no, 64 * q)
            nc.gpsimd.tensor_copy(e.idx[:, u, :], index[:, bass.ds(s * GT, GT)]).then_inc(e.idx_ready.sem, 1)
            e.idx_ready.wait(pool, pass_no, s + 1)
            pool.sem_inc(e.gate, 1)
            for t in range(GT):
                if t % GC == 0 and not (isinstance(s, int) and s < 2):
                    free.wait(pool, pass_no - free_before, J * (s - 2) + t // GC + 1)
                    pool.sem_inc(e.gate, 1)
                pool.indirect_dma_start(out=rv[:, u, t, :], out_offset=None, in_=table,
                                        in_offset=bass.IndirectOffsetOnAxis(ap=e.idx[:, u, t:t + 1], axis=0))\
                    .then_inc(e.rows_here[u][t // GC].sem, 16)

        group(0, 0, 0)
        group(1, 1, 0)
        turns(pool, group, 2, NG)
    return rv


def weighted_pass(nc, e):
    V = nc.vector
    with nc.Block() as block:
        rv = gather_rows(nc, e, block, 0, e.t0_d, D, e.srcE, e.p_ready, 0)

        @block.vector
        def _(dve):
            def onehots(s, u):
                for j in range(J):
                    if not (isinstance(s, int) and s < 2):
                        e.p_ready.wait(dve, 0, J * (s - 2) + j + 1)
                    for g in range(GC):
                        t = GC * j + g
                        ins = V.tensor_scalar(e.oh[:, u, t, :], e.iotaF[:, :], e.dlE[:, bass.ds(s * GT + t, 1)],
                                              e.ewE[:, bass.ds(s * GT + t, 1)], ALU.is_equal, ALU.mult)
                    ins.then_inc(e.oh_ready.sem, 1)

            def add(s, u):
                for j in range(J):
                    b = dve.value_load(e.blkI[0:1, bass.ds(J * s + j, 1)], min_val=0, max_val=NB - 1)
                    a = e.acc[:, bass.ds(b * D, D)]
                    e.p_ready.wait(dve, 0, J * s + j + 1)
                    e.added.wait(dve, 0, J * s + j)
                    V.tensor_tensor(a, a, e.ps[:, 4 * u + j, 0:D], ALU.add).then_inc(e.added.sem, 1)

            def slot(s, u, q):
                onehots(s, u)
                add(s - 1, 1 - u)

            onehots(0, 0)
            slot(1, 1, 0)
            turns(dve, slot, 2, NG)
            add(NG - 1, (NG - 1) % 2)

        @block.tensor
        def _(pe):
            def slot(s, u, q):
                for j in range(J):
                    e.oh_ready.wait(pe, 0, J * s + j + 1)
                    e.rows_here[u][j].wait(pe, 0, 64 * (q + 1))
                    if not (isinstance(s, int) and s < 2):
                        e.added.wait(pe, 0, J * (s - 2) + j + 1)
                    for g in range(GC):
                        ins = nc.tensor.matmul(e.ps[:, 4 * u + j, 0:D], e.oh[:, u, GC * j + g, :], rv[:, u, GC * j + g, :],
                                               start=(g == 0), stop=(g == GC - 1))
                    ins.then_inc(e.p_ready.sem, 1)
            slot(0, 0, 0)
            slot(1, 1, 0)
            turns(pe, slot, 2, NG)


def attention_pass(nc, e, no, H, table, width, index, scale, gat):
    V, ps = nc.vector, e.ps
    a_no = no - 1
    gat_no = no - 2
    hs = D // H
    W = hs + 1
    HW = H * W
    PW = HW + H
    JH = J * H
    BT, BK, BS, BE = 0, 2, 4, 5
    pP = ps[:, 6:8, :].rearrange("p a (c w) -> p (a c) w", w=256)
    pPh = pP[:, :, 0:HW].rearrange("p j (h c) -> p j h c", c=W)
    exvT = e.exv[:, 0:GT * PW].rearrange("p (t w) -> p t w", w=PW)
    exvH = exvT[:, :, 0:HW].rearrange("p t (h c) -> p t h c", c=W)
    exP = ps[:, BE, 0:GC * JH].rearrange("p (g j h) -> p g j h", g=GC, j=J)
    exE = e.exb[:, 0:GC * JH].rearrange("p (g j h) -> p g j h", g=GC, j=J)
    mxE = e.exb[:, GC * JH:2 * GC * JH].rearrange("p (g j h) -> p g j h", g=GC, j=J)
    tPh = e.tP[:, 0:J * HW].rearrange("p (j h c) -> p j h c", j=J, h=H)
    scv = e.sc[:, :, 0:GC * JH].rearrange("p u (g j h) -> p u g j h", g=GC, j=J)
    mw = [e.mwork[:, n, 0:JH].rearrange("p (j h) -> p j h", j=J) for n in range(3)]
    pen, ml, mold = mw
    mn = e.mwork[:, 3, 0:JH].rearrange("p (j h) -> p j h", j=J)
    d2 = e.mwork[:, 4:6, 0:JH]
    e2 = e.mwork[:, 6:8, 0:JH]
    e2v = [e.mwork[:, 6 + n, 0:JH].rearrange("p (j h) -> p j h", j=J) for n in range(2)]
    pair = e.pairs[:, 0:J * JH].rearrange("p (j k h) -> p j k h", j=J, k=J)
    att = e.vecs[:, 0:D]

    def static(s, below):
        return isinstance(s, int) and s < below

    with nc.Block() as block:
        rv = gather_rows(nc, e, block, no, table, width, index, e.exv_ready, 1)
        vrow = width - D

        @block.sync
        def _(sp):
            def slot(s, u, q):
                if not static(s, 2):
                    e.seg_ready.wait(sp, a_no, s - 1)
                for j in range(J):
                    sp.dma_start(e.segF[j * H:(j + 1) * H, u, :],
                                 e.seg_d[bass.ds(s * J + j, 1), :].to_broadcast([H, CE + 4])).then_inc(e.flags_here[u].sem, 16)
            slot(0, 0, 0)
            slot(1, 1, 0)
            turns(sp, slot, 2, NG)

        @block.scalar
        def _(act):
            def keep_turned(s, j):
                c, k = J * s + j, j % 2
                e.oht_made.wait(act, a_no, c + 1)
                if not (static(s, 1) and j < 2):
                    e.kd_ready.wait(act, a_no, c - 1)
                nc.scalar.activation(e.ohT[:, k, :], ps[:, BT + k, :], ACT.Copy).then_inc(e.oht_ready.sem, 1)

            def keep_pair_sums(s, j):
                c, k = J * s + j, j % 2
                if gat:
                    e.kd_ready.wait(act, a_no, c + 1)
                    if not (static(s, 1) and j < 2):
                        e.score_ready.wait(act, a_no, c - 1)
                    nc.scalar.activation(e.prod[:, k, :], ps[:, BK + k, :], ACT.Copy).then_inc(e.lr_ready.sem, 1)

            def exp_columns(s):
                e.back_ready.wait(act, a_no, s + 1)
                nc.scalar.activation(e.exb[:, 0:2 * GC * JH], ps[:, BE, 0:2 * GC * JH], ACT.Copy).then_inc(e.exb_ready.sem, 1)
                nc.scalar.activation(exvH[:, :, :, hs].rearrange("p (j g) h -> p j g h", j=J),
                                     exP.rearrange("p g j h -> p j g h"), ACT.Copy).then_inc(e.excol_ready.sem, 1)

            def exps(s):
                e.seg_ready.wait(act, a_no, s + 1)
                nc.scalar.activation(e.exT[0:JH, :], e.segS[0:JH, 0, :], ACT.Exp, scale=scale).then_inc(e.ex_ready.sem, 1)

            def shift_exps(s):
                e.d2_ready.wait(act, a_no, s + 1)
                nc.scalar.activation(e2, d2, ACT.Exp, scale=scale).then_inc(e.e2_ready.sem, 1)

            def slot(s, u, q, prev=True, ahead=True):
                keep_turned(s, 2)
                keep_turned(s, 3)
                if prev:
                    exp_columns(s - 1)
                keep_pair_sums(s, 2)
                keep_pair_sums(s, 3)
                if ahead:
                    keep_turned(s + 1, 0)
                    keep_turned(s + 1, 1)
                exps(s)
                if ahead:
                    keep_pair_sums(s + 1, 0)
                if prev:
                    shift_exps(s - 1)
                if ahead:
                    keep_pair_sums(s + 1, 1)

            for j in range(2):
                keep_turned(0, j)
            for j in range(2):
                keep_pair_sums(0, j)
            slot(0, 0, 0, prev=False)
            turns(act, slot, 1, NG - 1)
            slot(NG - 1, (NG - 1) % 2, (NG - 1) // 2, ahead=False)
            exp_columns(NG - 1)
            shift_exps(NG - 1)

        @block.vector
        def _(dve):
            def onehots(s, u, first, end):
                for j in range(first, end):
                    if not static(s, 2):
                        e.p_ready.wait(dve, no, J * (s - 2) + j + 1)
                    V.tensor_tensor(e.oh[:, u, GC * j:GC * (j + 1), :],
                                    e.iotaF[:, :].unsqueeze(1).to_broadcast([P, GC, P]),
                                    bc(e.dlE[:, bass.ds(s * GT + GC * j, GC)], P), ALU.is_equal).then_inc(e.oh_ready.sem, 1)

            def product(s, u, q, j):
                c, k = J * s + j, j % 2
                pr = e.prod[:, k, :].rearrange("p (g d) -> p g d", d=D)
                if not (static(s, 1) and j < 2):
                    e.score_ready.wait(dve, a_no, c - 1)
                if gat:
                    e.lr_ready.wait(dve, gat_no, c + 1)
                    V.scalar_tensor_tensor(e.prod[:, k, :], ps[:, BK + k, :], 0.2, e.prod[:, k, :], ALU.mult, ALU.max)\
                        .then_inc(e.leaky_done.sem, 1)
                else:
                    e.kd_ready.wait(dve, a_no, c + 1)
                    e.rows_here[u][j].wait(dve, no, 64 * (q + 1))
                    V.tensor_tensor(pr, rv[:, u, GC * j:GC * (j + 1), 0:D],
                                    ps[:, BK + k, :].rearrange("p (g d) -> p g d", d=D), ALU.mult).then_inc(e.prod_ready.sem, 1)

            def weight_att(s, j):
                if gat:
                    e.leaky_done.wait(dve, gat_no, J * s + j + 1)
                    pr = e.prod[:, j % 2, :].rearrange("p (g d) -> p g d", d=D)
                    V.tensor_tensor(pr, pr, att.unsqueeze(1).to_broadcast([P, GC, D]), ALU.mult).then_inc(e.prod_ready.sem, 1)

            def score(s, u, j):
                e.prod_ready.wait(dve, a_no, J * s + j + 1)
                V.tensor_reduce(scv[:, u, :, j, :], e.prod[:, j % 2, :].rearrange("p (g h d) -> p g h d", g=GC, h=H),
                                AX, ALU.add).then_inc(e.score_ready.sem, 1)

            def last_maxima(s):
                e.exb_ready.wait(dve, a_no, s + 1)
                V.tensor_tensor(exvT[:, :, HW:PW].rearrange("p (j g) h -> p j g h", j=J),
                                mxE.rearrange("p g j h -> p j g h"),
                                bc(e.lastE[:, bass.ds(s * GT, GT)].rearrange("p (j g) -> p j g", j=J), H), ALU.mult)

            def weigh(s, u, q, j):
                e.rows_here[u][j].wait(dve, no, 64 * (q + 1))
                V.tensor_tensor(exvH[:, GC * j:GC * (j + 1), :, 0:hs],
                                rv[:, u, GC * j:GC * (j + 1), vrow:vrow + D].rearrange("p g (h d) -> p g h d", h=H),
                                bc(exE[:, :, j, :], hs), ALU.mult).then_inc(e.exv_ready.sem, 1)

            def scan_forward(s, u, q):
                e.st_ready.wait(dve, a_no, s + 1)
                e.flags_here[u].wait(dve, a_no, 16 * J * (q + 1))
                V.tensor_tensor_scan(e.segS[0:JH, 0, :], e.segF[0:JH, u, 0:CE], ps[0:JH, BS, :], -BIG, ALU.add, ALU.max)\
                    .then_inc(e.scan_step.sem, 1)

            def scan_backward(s, u):
                e.scan_step.wait(dve, a_no, 2 * s + 1)
                V.tensor_tensor_scan(e.segS[0:JH, 1, CE - 1::-1], e.segF[0:JH, u, CE:0:-1], e.segS[0:JH, 0, CE - 1::-1],
                                     -BIG, ALU.add, ALU.max).then_inc(e.scan_step.sem, 1)

            def less_maximum(s):
                e.scan_step.wait(dve, a_no, 2 * s + 2)
                V.tensor_tensor(e.segS[0:JH, 0, :], ps[0:JH, BS, :], e.segS[0:JH, 1, :], ALU.subtract).then_inc(e.seg_ready.sem, 1)

            def kept_maximum(s, j, b):
                e.max_kept.wait(dve, a_no, J * s)
                V.tensor_scalar(mold[:, j, :], e.mx[:, bass.ds(b * H, H)], 1.0, None, ALU.mult).then_inc(e.max_step.sem, 1)

            def group_maxima(s):
                n = MAX_STEPS * s + J

                def step(ins):
                    nonlocal n
                    n = n + 1
                    ins.then_inc(e.max_step.sem, 1)

                def done():
                    e.max_step.wait(dve, a_no, n)
                e.p_ready.wait(dve, no, J * (s + 1))
                step(V.tensor_scalar(pen, pPh[:, :, :, hs], 0.5, -BIG, ALU.is_lt, ALU.mult))
                done()
                step(V.tensor_tensor(ml, pen, pP[:, :, HW:PW], ALU.add))
                if not last_group(s):
                    onehots(s + 2, s_parity[0], 2, 3)
                done()
                step(V.tensor_tensor(pair, ml.unsqueeze(1).to_broadcast([P, J, J, H]),
                                     bc(e.samePair[:, bass.ds(s * J * J, J * J)].rearrange("p (j k) -> p j k", j=J), H), ALU.add))
                if not last_group(s):
                    onehots(s + 2, s_parity[0], 3, 4)
                done()
                step(V.tensor_reduce(mn, pair.rearrange("p j k h -> p j h k"), AX, ALU.max))
                done()
                step(V.tensor_tensor(mn, mn, mold, ALU.max))
                done()
                step(V.tensor_tensor(e.mwork[:, 5, 0:JH], e.mwork[:, 1, 0:JH], e.mwork[:, 3, 0:JH], ALU.subtract))
                step(V.tensor_tensor(e.mwork[:, 4, 0:JH], e.mwork[:, 2, 0:JH], e.mwork[:, 3, 0:JH], ALU.subtract))
                done()
                d_old = e.mwork[:, 4, 0:JH].rearrange("p (j h) -> p j h", j=J)
                V.tensor_tensor(d_old, d_old, bc(e.firstE[:, bass.ds(s * J, J)], H), ALU.mult).then_inc(e.d2_ready.sem, 1)

            def keep_maximum(s, j, b):
                e.max_kept.wait(dve, a_no, J * s + j)
                V.tensor_scalar(e.mx[:, bass.ds(b * H, H)], mn[:, j, :], 1.0, None, ALU.mult).then_inc(e.max_kept.sem, 1)

            def scale_partial(s):
                e.e2_ready.wait(dve, a_no, s + 1)
                e.acc_step.wait(dve, a_no, ACC_STEPS * s)
                V.tensor_tensor(tPh, pPh, bc(e2v[1], W), ALU.mult).then_inc(e.acc_step.sem, 1)

            def rescale(s, j, b):
                e.acc_step.wait(dve, a_no, ACC_STEPS * s + 1 + 2 * j)
                a = e.acc[:, bass.ds(b * HW, HW)].rearrange("p (h c) -> p h c", h=H)
                V.tensor_tensor(a, a, bc(e2v[0][:, j, :], W), ALU.mult).then_inc(e.acc_step.sem, 1)

            def add_partial(s, j, b):
                e.acc_step.wait(dve, a_no, ACC_STEPS * s + 2 + 2 * j)
                a = e.acc[:, bass.ds(b * HW, HW)].rearrange("p (h c) -> p h c", h=H)
                V.tensor_tensor(a, a, tPh[:, j, :, :], ALU.add).then_inc(e.acc_step.sem, 1)

            def blocks_of(s):
                return block_numbers(nc, e, mybir.EngineType.DVE, J * s, J)

            def slot(s, u, q, cur=True, prev=True, before=True, tail=False):
                pq = q if u == 1 else q - 1
                s_parity[0] = 1 - u
                if before:
                    bb = blocks_of(s - 2)
                if cur:
                    product(s, u, q, 0)
                if before:
                    scale_partial(s - 2)
                if cur:
                    weight_att(s, 0)
                    product(s, u, q, 1)
                    score(s, u, 0)
                if before:
                    rescale(s - 2, 0, bb[0])
                    keep_maximum(s - 2, 0, bb[0])
                if cur:
                    weight_att(s, 1)
                    score(s, u, 1)
                if before:
                    add_partial(s - 2, 0, bb[0])
                    keep_maximum(s - 2, 1, bb[1])
                if prev:
                    last_maxima(s - 1)
                if before:
                    rescale(s - 2, 1, bb[1])
                    keep_maximum(s - 2, 2, bb[2])
                if prev:
                    weigh(s - 1, 1 - u, pq, 0)
                if before:
                    add_partial(s - 2, 1, bb[1])
                    keep_maximum(s - 2, 3, bb[3])
                if cur:
                    product(s, u, q, 2)
                if before:
                    rescale(s - 2, 2, bb[2])
                if prev:
                    weigh(s - 1, 1 - u, pq, 1)
                if before:
                    add_partial(s - 2, 2, bb[2])
                if cur:
                    weight_att(s, 2)
                    product(s, u, q, 3)
                    score(s, u, 2)
                if before:
                    rescale(s - 2, 3, bb[3])
                if cur:
                    weight_att(s, 3)
                if prev:
                    weigh(s - 1, 1 - u, pq, 2)
                if cur:
                    score(s, u, 3)
                if before:
                    add_partial(s - 2, 3, bb[3])
                if prev:
                    weigh(s - 1, 1 - u, pq, 3)
                    bp = blocks_of(s - 1)
                if cur:
                    scan_forward(s, u, q)
                if prev:
                    kept_maximum(s - 1, 0, bp[0])
                    kept_maximum(s - 1, 1, bp[1])
                if cur and not tail:
                    onehots(s + 1, 1 - u, 0, 1)
                if cur:
                    scan_backward(s, u)
                if prev:
                    kept_maximum(s - 1, 2, bp[2])
                    kept_maximum(s - 1, 3, bp[3])
                if cur and not tail:
                    onehots(s + 1, 1 - u, 1, 2)
                if cur:
                    less_maximum(s)
                if cur and not tail and not prev:
                    onehots(s + 1, 1 - u, 2, 4)
                if prev:
                    group_maxima(s - 1)

            s_parity = [0]

            def last_group(s):
                return isinstance(s, int) and s >= NG - 2

            onehots(0, 0, 0, J)
            slot(0, 0, 0, prev=False, before=False)
            slot(1, 1, 0, before=False)
            turns(dve, slot, 2, NG - 1)
            slot(NG - 1, (NG - 1) % 2, (NG - 1) // 2, tail=True)
            slot(NG, NG % 2, NG // 2, cur=False)
            slot(NG + 1, (NG + 1) % 2, (NG + 1) // 2, cur=False, prev=False)

        @block.tensor
        def _(pe):
            def turn_onehots(s, u, j):
                c = J * s + j
                e.oh_ready.wait(pe, no, c + 1)
                if not (static(s, 1) and j < 2):
                    e.oht_ready.wait(pe, a_no, c - 1)
                for g in range(GC):
                    ins = nc.tensor.transpose(ps[:, BT + j % 2, g * P:(g + 1) * P], e.oh[:, u, GC * j + g, :], e.ident[:, :])
                ins.then_inc(e.oht_made.sem, 1)

            def dst_rows(s, u, q, j, b):
                c, k = J * s + j, j % 2
                if gat:
                    e.rows_here[u][j].wait(pe, no, 64 * (q + 1))
                if not (static(s, 1) and j < 2):
                    if gat:
                        e.leaky_done.wait(pe, gat_no, c - 1)
                    else:
                        e.prod_ready.wait(pe, a_no, c - 1)
                if gat:
                    nc.tensor.matmul(ps[:, BK + k, :], e.ident[:, :],
                                     rv[:, u, GC * j:GC * (j + 1), :].rearrange("p g d -> p (g d)"), start=True, stop=False)
                e.oht_ready.wait(pe, a_no, c + 1)
                for g in range(GC):
                    ins = nc.tensor.matmul(ps[:, BK + k, g * P:(g + 1) * P], e.ohT[:, k, g * P:(g + 1) * P],
                                           e.kN[:, bass.ds(b, 1), :].rearrange("p b d -> p (b d)"), start=not gat, stop=not gat or g == GC - 1)
                ins.then_inc(e.kd_ready.sem, 1)

            def turn_scores(s, u):
                e.score_ready.wait(pe, a_no, J * (s + 1))
                if not static(s, 1):
                    e.seg_ready.wait(pe, a_no, s)
                for g in range(GC):
                    ins = nc.tensor.transpose(ps[0:JH, BS, g:CE:GC], e.sc[:, u, g * JH:(g + 1) * JH], e.ident[:, :])
                ins.then_inc(e.st_ready.sem, 1)

            def turn_back(s):
                e.ex_ready.wait(pe, a_no, s + 1)
                pe.sem_inc(e.gate, 1)
                for g in range(GC):
                    nc.tensor.transpose(ps[:, BE, g * JH:(g + 1) * JH], e.exT[0:JH, g:CE:GC], e.ident[0:JH, 0:JH])
                    ins = nc.tensor.transpose(ps[:, BE, (GC + g) * JH:(GC + g + 1) * JH], e.segS[0:JH, 1, g:CE:GC],
                                              e.ident[0:JH, 0:JH])
                ins.then_inc(e.back_ready.sem, 1)

            def sums(s, u, j):
                e.exv_ready.wait(pe, a_no, J * s + j + 1)
                e.excol_ready.wait(pe, a_no, s + 1)
                if not static(s, 1):
                    e.acc_step.wait(pe, a_no, ACC_STEPS * (s - 1) + 1)
                for g in range(GC):
                    ins = nc.tensor.matmul(pP[:, j, 0:PW], e.oh[:, u, GC * j + g, :], exvT[:, GC * j + g, :],
                                           start=(g == 0), stop=(g == GC - 1))
                ins.then_inc(e.p_ready.sem, 1)

            def first_half(s, u, q):
                bs = block_numbers(nc, e, mybir.EngineType.PE, J * s, 2)
                turn_onehots(s, u, 0)
                turn_onehots(s, u, 1)
                dst_rows(s, u, q, 0, bs[0])
                dst_rows(s, u, q, 1, bs[1])

            def slot(s, u, q, cur=True, prev=True, ahead=True):
                if cur:
                    bs = block_numbers(nc, e, mybir.EngineType.PE, J * s + 2, 2)
                    turn_onehots(s, u, 2)
                    turn_onehots(s, u, 3)
                if prev:
                    turn_back(s - 1)
                if cur:
                    dst_rows(s, u, q, 2, bs[0])
                    dst_rows(s, u, q, 3, bs[1])
                if prev:
                    sums(s - 1, 1 - u, 0)
                    sums(s - 1, 1 - u, 1)
                if cur:
                    turn_scores(s, u)
                if prev:
                    sums(s - 1, 1 - u, 2)
                    sums(s - 1, 1 - u, 3)
                if cur and ahead:
                    first_half(s + 1, 1 - u, q if u == 0 else q + 1)

            first_half(0, 0, 0)
            slot(0, 0, 0, prev=False)
            slot(1, 1, 0)
            turns(pe, slot, 2, NG - 1)
            slot(NG - 1, (NG - 1) % 2, (NG - 1) // 2, ahead=False)
            slot(NG, NG % 2, NG // 2, cur=False)


class Stage:

    def __init__(self, e, name):
        self.e, self.name, self.sems = e, name, {}

    def __getitem__(self, what):
        if what not in self.sems:
            self.sems[what] = self.e.nc.alloc_semaphore(name=f"{self.name}_{what}")
        return self.sems[what]

    def __enter__(self):
        return self

    def __exit__(self, *_):
        self.e.nc.clear_and_free_semaphores(list(self.sems.values()))
        self.e.nc.all_engine_barrier()


def load_row(nc, eng, dst, src, done):
    n = dst.shape[1]
    eng.dma_start(dst, src.rearrange("(a n) -> a n", a=1).to_broadcast([P, n])).then_inc(done, 16)


def over(ap, n=NB):
    return ap.unsqueeze(1).to_broadcast([P, n, ap.shape[1]])


def project(nc, e, block, S, tag, parts, nout):
    turned, copied, done, taken, ready = (S[f"{tag}_{w}"] for w in ("turned", "copied", "done", "taken", "ready"))
    np_ = len(parts)
    at_hand = S[f"{tag}_at_hand"]

    @block.gpsimd
    def _(pool):
        pool.wait_ge(ready, 1)

        def body(b, k, first):
            if not first:
                pool.wait_ge(turned, b - 1)
            for n, (nodes, _) in enumerate(parts):
                ins = nc.gpsimd.tensor_copy(e.prod[:, k, n * P:(n + 1) * P], nodes[:, bass.ds(b, 1), :].rearrange("p b d -> p (b d)"))
            ins.then_inc(at_hand, 1)
        over_blocks(pool, body)

    @block.tensor
    def _(pe):
        def turn(pe, b, k, first):
            pe.wait_ge(at_hand, b + 1)
            for n in range(np_):
                ins = nc.tensor.transpose(e.ps[:, k, n * P:(n + 1) * P], e.prod[:, k, n * P:(n + 1) * P], e.ident[:, :])
            ins.then_inc(turned, 1)
        turn(pe, 0, 0, True)

        def body(b, k, first):
            ahead(turn, pe, b, k)
            pe.wait_ge(copied, b + 1)
            if not first:
                pe.wait_ge(taken, b - 1)
            for n, (_, w) in enumerate(parts):
                ins = nc.tensor.matmul(e.ps[:, 2 + k, 0:nout], e.ohT[:, k, n * P:(n + 1) * P], w, start=(n == 0), stop=(n == np_ - 1))
            ins.then_inc(done, 1)
        over_blocks(pe, body)

    @block.scalar
    def _(act):
        def body(b, k, first):
            act.wait_ge(turned, b + 1)
            if not first:
                act.wait_ge(done, b - 1)
            nc.scalar.activation(e.ohT[:, k, 0:np_ * P], e.ps[:, k, 0:np_ * P], ACT.Copy).then_inc(copied, 1)
        over_blocks(act, body)


def norm(nc, e, dve, c, S, tag, src, dst, tmp, relu):
    V = nc.vector
    mean, var = e.r_at[:, 0:NB], e.r_at[:, 32:32 + NB]
    c.step(dve, V.tensor_reduce(mean, src, AX, ALU.add))
    c.step(dve, V.tensor_scalar(mean, mean, 1.0 / D, None, ALU.mult))
    c.step(dve, V.tensor_tensor(dst, src, bc(mean, D), ALU.subtract))
    c.step(dve, V.tensor_tensor(tmp, dst, dst, ALU.mult))
    c.step(dve, V.tensor_reduce(var, tmp, AX, ALU.add))
    V.tensor_scalar(var, var, 1.0 / D, 1e-5, ALU.mult, ALU.add).then_inc(S[tag + "_var"], 1)
    dve.wait_ge(S[tag + "_std"], 1)
    c.step(dve, V.reciprocal(var, var))
    c.step(dve, V.tensor_tensor(dst, dst, bc(var, D), ALU.mult))
    if relu:
        c.step(dve, V.tensor_scalar(dst, dst, 0.0, None, ALU.max))


def norm_sqrt(nc, e, act, S, tag):
    act.wait_ge(S[tag + "_var"], 1)
    nc.scalar.activation(e.r_at[:, 32:32 + NB], e.r_at[:, 32:32 + NB], ACT.Sqrt).then_inc(S[tag + "_std"], 1)


def normalized(nc, e, dve, c, dst, H):
    V = nc.vector
    W = D // H + 1
    a = e.acc[:, 0:NB * H * W].rearrange("p (n c) -> p n c", c=W)
    r = e.r_at[:, 0:NB * H]
    c.step(dve, V.tensor_scalar(r, a[:, :, W - 1], 0.5, None, ALU.max))
    c.step(dve, V.reciprocal(r, r))
    c.step(dve, V.tensor_tensor(dst.rearrange("p b (h d) -> p (b h) d", h=H), a[:, :, 0:W - 1], bc(r, W - 1), ALU.mult))


def first_norm(nc, A, e):
    S = Stage(e, "n0")
    with S, nc.Block() as block:
        @block.vector
        def _(dve):
            c = Chain(S["step"])
            norm(nc, e, dve, c, S, "ln", e.xN, e.hN, e.tA, True)
            c.step(dve, nc.vector.memset(e.acc[:, :], 0.0))
            nc.vector.memset(e.small[:, 0:1], 0.0).then_inc(S["h"], 1)

        @block.scalar
        def _(act):
            norm_sqrt(nc, e, act, S, "ln")

        @block.sync
        def _(sp):
            sp.wait_ge(S["h"], 1)
            sp.dma_start(e.t0_d.rearrange("(b p) d -> p b d", p=P), e.hN[:, :, :]).then_inc(S["out"], 16)
            sp.wait_ge(S["out"], 16)


def after_l0(nc, A, e):
    S = Stage(e, "n1")
    V = nc.vector
    w = e.wts
    agg = e.acc[:, 0:NB * D].rearrange("p (b d) -> p b d", d=D)
    with S, nc.Block() as block:
        @block.sync
        def _(sp):
            sp.dma_start(w[:, 0:D], A["L0_gnn_W1"]).then_inc(S["w"], 16)
            sp.dma_start(w[:, D:2 * D], A["L0_gnn_W2"]).then_inc(S["w"], 16)
            load_row(nc, sp, w[:, 1536:1664], A["L0_gnn_b1"], S["w"])
            load_row(nc, sp, w[:, 1664:1792], A["L0_gnn_b2"], S["w"])
            for n, name in enumerate("qvks"):
                sp.dma_start(w[:, 512 + n * D:512 + (n + 1) * D], A[f"L1_gnn_W{name}"]).then_inc(S["w"], 16)
                load_row(nc, sp, w[:, 1024 + n * D:1024 + (n + 1) * D], A[f"L1_gnn_b{name}"], S["w"])
            sp.wait_ge(S["tables"], 1)
            t1 = e.t1_d.rearrange("(b p) d -> p b d", p=P)
            sp.dma_start(t1[:, :, 0:D], e.tA).then_inc(S["out"], 16)
            sp.dma_start(t1[:, :, D:2 * D], e.tB).then_inc(S["out"], 16)
            sp.wait_ge(S["out"], 32)

        @block.vector
        def _(dve):
            c = Chain(S["step"])
            c.step(dve, V.tensor_tensor(e.tA, agg, e.hN[:, :, :], ALU.add))
            c.step(dve, V.tensor_tensor(e.tB, agg, e.hN[:, :, :], ALU.mult))
            dve.wait_ge(S["wt"], 1)
            c.step(dve, V.tensor_copy(w[:, 256:512], e.ps[:, 7, 0:256]))
            c.step(dve, V.tensor_tensor(w[:, 1536:1664], w[:, 1536:1664], w[:, 1664:1792], ALU.add))
            V.memset(e.small[:, 0:1], 0.0).then_inc(S["a_ready"], 1)

            def take(b, k, first):
                dve.wait_ge(S["a_done"], b + 1)
                V.tensor_tensor(e.tC[:, bass.ds(b, 1), :].rearrange("p b d -> p (b d)"), e.ps[:, 2 + k, 0:D],
                                w[:, 1536:1664], ALU.add).then_inc(S["a_taken"], 1)
            over_blocks(dve, take)
            dve.wait_ge(S["a_taken"], NB)
            c.step(dve, V.scalar_tensor_tensor(e.tC, e.tC, 0.2, e.tC, ALU.mult, ALU.max))
            c.step(dve, V.tensor_tensor(e.xN[:, :, :], e.xN[:, :, :], e.tC, ALU.add))
            norm(nc, e, dve, c, S, "ln", e.xN[:, :, :], e.hN[:, :, :], e.tA, True)
            V.memset(e.small[:, 0:1], 0.0).then_inc(S["b_ready"], 1)

            def take4(b, k, first):
                dve.wait_ge(S["b_done"], b + 1)
                for n, dst in enumerate((e.tA, e.tB, e.kN, e.skN)):
                    ins = V.tensor_tensor(dst[:, bass.ds(b, 1), :].rearrange("p b d -> p (b d)"),
                                          e.ps[:, 2 + k, n * D:(n + 1) * D], w[:, 1024 + n * D:1024 + (n + 1) * D], ALU.add)
                ins.then_inc(S["b_taken"], 1)
            over_blocks(dve, take4)
            dve.wait_ge(S["b_taken"], NB)
            V.memset(e.small[:, 0:1], 0.0).then_inc(S["tables"], 1)
            c.step(dve, V.memset(e.acc[:, :], 0.0))
            c.step(dve, V.memset(e.mx[:, :], -BIG))

        @block.tensor
        def _(pe):
            pe.wait_ge(S["w"], 16 * 12)
            nc.tensor.transpose(e.ps[:, 7, 0:P], w[:, 0:D], e.ident[:, :])
            nc.tensor.transpose(e.ps[:, 7, P:2 * P], w[:, D:2 * D], e.ident[:, :]).then_inc(S["wt"], 1)

        project(nc, e, block, S, "a", [(e.tA, w[:, 256:384]), (e.tB, w[:, 384:512])], D)

        @block.scalar
        def _(act):
            norm_sqrt(nc, e, act, S, "ln")

        project(nc, e, block, S, "b", [(e.hN, w[:, 512:1024])], 4 * D)


def gat_projections(nc, A, e, block, S, layer, H):
    w = e.wts
    V = nc.vector
    W = D // H + 1

    @block.sync
    def _(sp):
        sp.dma_start(w[:, 0:D], A[f"L2_gnn_Wl{layer}"]).then_inc(S["w"], 16)
        sp.dma_start(w[:, D:2 * D], A[f"L2_gnn_Wr{layer}"]).then_inc(S["w"], 16)
        load_row(nc, sp, w[:, 256:384], A[f"L2_gnn_bl{layer}"], S["w"])
        load_row(nc, sp, w[:, 384:512], A[f"L2_gnn_br{layer}"], S["w"])
        load_row(nc, sp, e.vecs[:, 0:D], A[f"L2_gnn_att{layer}"].rearrange("h c -> (h c)"), S["w"])
        sp.wait_ge(S["tables"], 1)
        sp.dma_start(e.t2_d.rearrange("(b p) d -> p b d", p=P), e.tA).then_inc(S["out"], 16)
        sp.wait_ge(S["out"], 16)

    project(nc, e, block, S, "p", [(e.hN, w[:, 0:256])], 2 * D)

    def on_dve(dve, c):
        dve.wait_ge(S["w"], 16 * 5)
        V.memset(e.small[:, 0:1], 0.0).then_inc(S["p_ready"], 1)

        def take(b, k, first):
            dve.wait_ge(S["p_done"], b + 1)
            V.tensor_tensor(e.tA[:, bass.ds(b, 1), :].rearrange("p b d -> p (b d)"), e.ps[:, 2 + k, 0:D], w[:, 256:384], ALU.add)
            V.tensor_tensor(e.kN[:, bass.ds(b, 1), :].rearrange("p b d -> p (b d)"), e.ps[:, 2 + k, D:2 * D], w[:, 384:512],
                            ALU.add).then_inc(S["p_taken"], 1)
        over_blocks(dve, take)
        dve.wait_ge(S["p_taken"], NB)
        V.memset(e.small[:, 0:1], 0.0).then_inc(S["tables"], 1)
        a = e.acc[:, 0:NB * H * W].rearrange("p (n c) -> p n c", c=W)
        c.step(dve, V.tensor_copy(a[:, :, 0:W - 1], e.tA.rearrange("p b (h d) -> p (b h) d", h=H)))
        c.step(dve, V.memset(a[:, :, W - 1:W], 1.0))
        c.step(dve, V.tensor_tensor(e.tC, e.tA, e.kN[:, :, :], ALU.add))
        c.step(dve, V.scalar_tensor_tensor(e.tC, e.tC, 0.2, e.tC, ALU.mult, ALU.max))
        c.step(dve, V.tensor_tensor(e.tC, e.tC, over(e.vecs[:, 0:D]), ALU.mult))
        c.step(dve, V.tensor_reduce(e.mx[:, 0:NB * H], e.tC.rearrange("p b (h d) -> p (b h) d", h=H), AX, ALU.add))
    return on_dve


def after_l1(nc, A, e):
    S = Stage(e, "n2")
    V = nc.vector
    vec = e.vecs
    wg, gam, bet = vec[:, 128:512], vec[:, 512:640], vec[:, 640:768]
    wa, wb = vec[:, 768:896], vec[:, 896:1024]
    bg, alpha = e.small[:, 300:301], e.small[:, 301:302]
    z = e.r_at[:, 192:192 + NB]
    with S, nc.Block() as block:
        @block.sync
        def _(sp):
            load_row(nc, sp, wg, A["L1_gnn_Wg"].rearrange("n a -> (n a)"), S["v"])
            load_row(nc, sp, gam, A["L1_gnn_gamma"], S["v"])
            load_row(nc, sp, bet, A["L1_gnn_beta"], S["v"])
            load_row(nc, sp, bg, A["L1_gnn_bg"], S["v"])
            load_row(nc, sp, alpha, A["L1_gnn_alpha"], S["v"])

        @block.scalar
        def _(act):
            act.wait_ge(S["z"], 1)
            nc.scalar.activation(z, z, ACT.Exp, scale=-1.0).then_inc(S["ez"], 1)
            norm_sqrt(nc, e, act, S, "ln1")
            norm_sqrt(nc, e, act, S, "ln2")

        on_dve = gat_projections(nc, A, e, block, S, 1, 4)

        @block.vector
        def _(dve):
            c = Chain(S["step"])
            agg, t, u, sk = e.tA, e.tB, e.tC, e.skN
            normalized(nc, e, dve, c, agg, 4)
            dve.wait_ge(S["v"], 16 * 5)
            c.step(dve, V.tensor_tensor(wa, wg[:, 0:D], wg[:, 2 * D:3 * D], ALU.add))
            c.step(dve, V.tensor_tensor(wb, wg[:, D:2 * D], wg[:, 2 * D:3 * D], ALU.subtract))
            c.step(dve, V.tensor_tensor(t, sk, over(wa), ALU.mult))
            c.step(dve, V.tensor_tensor(u, agg, over(wb), ALU.mult))
            c.step(dve, V.tensor_tensor(t, t, u, ALU.add))
            c.step(dve, V.tensor_reduce(z, t, AX, ALU.add))
            c.step(dve, V.tensor_scalar(z, z, bg, -80.0, ALU.add, ALU.max))
            V.memset(e.small[:, 0:1], 0.0).then_inc(S["z"], 1)
            dve.wait_ge(S["ez"], 1)
            c.step(dve, V.tensor_scalar(z, z, 1.0, None, ALU.add))
            c.step(dve, V.reciprocal(z, z))
            c.step(dve, V.tensor_tensor(t, sk, agg, ALU.subtract))
            c.step(dve, V.tensor_tensor(t, t, bc(z, D), ALU.mult))
            c.step(dve, V.tensor_tensor(agg, agg, t, ALU.add))
            norm(nc, e, dve, c, S, "ln1", agg, t, u, False)
            c.step(dve, V.tensor_tensor(t, t, over(gam), ALU.mult))
            c.step(dve, V.tensor_tensor(t, t, over(bet), ALU.add))
            c.step(dve, V.tensor_scalar(u, t, 0.0, alpha, ALU.min, ALU.mult))
            c.step(dve, V.scalar_tensor_tensor(t, t, 0.0, u, ALU.max, ALU.add))
            c.step(dve, V.tensor_tensor(e.xN[:, :, :], e.xN[:, :, :], t, ALU.add))
            norm(nc, e, dve, c, S, "ln2", e.xN[:, :, :], e.hN[:, :, :], t, True)
            on_dve(dve, c)


def after_l2a(nc, A, e):
    S = Stage(e, "n3")
    V = nc.vector
    with S, nc.Block() as block:
        @block.sync
        def _(sp):
            load_row(nc, sp, e.vecs[:, 128:256], A["L2_gnn_b1"], S["v"])

        on_dve = gat_projections(nc, A, e, block, S, 2, 1)

        @block.vector
        def _(dve):
            c = Chain(S["step"])
            normalized(nc, e, dve, c, e.tA, 4)
            dve.wait_ge(S["v"], 16)
            c.step(dve, V.tensor_tensor(e.tA, e.tA, over(e.vecs[:, 128:256]), ALU.add))
            c.step(dve, V.tensor_scalar(e.hN[:, :, :], e.tA, 0.0, None, ALU.max))
            on_dve(dve, c)


KW, WA, BD = 0, 3072, 4096


def masked_turn(nc, e, block, S, tag, nodes, banks):
    ohf = e.oh[:, :, :, :].rearrange("p u t n -> p (u t n)")
    dm = [ohf[:, k * 1024:(k + 1) * 1024] for k in range(2)]
    hTm = [ohf[:, 2048 + k * 1024:2048 + (k + 1) * 1024] for k in range(2)]
    made, turned, copied, used, at_hand = (S[f"{tag}_{w}"] for w in ("masks", "turned", "copied", "used", "at_hand"))

    @block.gpsimd
    def _(pool):
        pool.wait_ge(S[f"{tag}_ready"], 1)

        def body(b, k, first):
            if not first:
                pool.wait_ge(turned, b - 1)
            nc.gpsimd.tensor_copy(e.prod[:, k, 0:P], nodes[:, bass.ds(b, 1), :].rearrange("p b d -> p (b d)")).then_inc(at_hand, 1)
        over_blocks(pool, body)

    def on_dve(dve, b, k, first):
        if not first:
            dve.wait_ge(turned, b - 1)
        nc.vector.tensor_tensor(dm[k].rearrange("p (t n) -> p t n", t=TYPES), e.ident[:, :].unsqueeze(1).to_broadcast([P, TYPES, P]),
                                bc(e.typeM[:, bass.ds(b, 1), :].rearrange("p b t -> p (b t)"), P), ALU.mult).then_inc(made, 1)

    def on_pe(pe, b, k, first):
        pe.wait_ge(made, b + 1)
        if banks[0] != banks[1]:
            if not first:
                pe.wait_ge(copied, b - 1)
        elif not (isinstance(b, int) and b == 0):
            pe.wait_ge(copied, b)
        pe.wait_ge(at_hand, b + 1)
        for n in range(2):
            ins = nc.tensor.matmul(e.ps[:, banks[k] + n, :], e.prod[:, k, 0:P], dm[k][:, n * 512:(n + 1) * 512], start=True, stop=True)
        ins.then_inc(turned, 1)

    def on_act(act, b, k, first):
        act.wait_ge(turned, b + 1)
        if not first:
            act.wait_ge(used, b - 1)
        nc.scalar.activation(hTm[k], e.ps[:, banks[k]:banks[k] + 2, :].rearrange("p a n -> p (a n)"), ACT.Copy).then_inc(copied, 1)
    return on_dve, on_pe, on_act, hTm


def typed_weights(nc, A, e, sp, S, layer):
    w = e.wts
    for n, name in enumerate("kqv"):
        sp.dma_start(w[:, KW + n * 1024:KW + (n + 1) * 1024].rearrange("p (t o) -> p t o", t=TYPES),
                     A[f"L3_gnn_W{name}"][layer].rearrange("t i o -> i t o")).then_inc(S["w"], 16)
    sp.dma_start(w[:, WA:WA + 1024].rearrange("p (t o) -> p t o", t=TYPES),
                 A["L3_gnn_Wa"][layer].rearrange("t i o -> i t o")).then_inc(S["w"], 16)
    bd = w[:, BD:BD + 2048].rearrange("p (m r o) -> p m r o", m=2, r=RELS)
    sp.wait_ge(S["bd_zero"], 1)
    for m, name in enumerate(("Watt", "Wmsg")):
        for h in range(L3H):
            sp.dma_start(bd[h * HS3:(h + 1) * HS3, m, :, h * HS3:(h + 1) * HS3],
                         A[f"L3_gnn_{name}"][layer, h].rearrange("r i o -> i r o")).then_inc(S["w"], 16)
    for h in range(L3H):
        sp.dma_start(e.small[h * HS3:(h + 1) * HS3, 320:320 + RELS],
                     A["L3_gnn_pri"][layer, h:h + 1, :].to_broadcast([HS3, RELS])).then_inc(S["w"], 16)


TYPED_LOADS = 16 * (4 + 3 * L3H)


def typed_projections(nc, A, e, block, S, layer):
    w, V = e.wts, nc.vector
    m_dve, m_pe, m_act, hTm = masked_turn(nc, e, block, S, "t", e.hN, (0, 0))
    kv, kv_sb, q_out, rel, staged_k, staged, written = (S[n] for n in (
        "kv_done", "kv_copied", "q_taken", "rel_done", "k_staged", "v_staged", "table_written"))
    stage = [e.rflat[:, k * 2048:(k + 1) * 2048].rearrange("p (r c) -> p r c", r=RELS) for k in range(2)]

    @block.sync
    def _(sp):
        typed_weights(nc, A, e, sp, S, layer)
        t3 = e.t3_d.rearrange("(b p r) c -> b p (r c)", p=P, r=RELS)

        def body(b, k, first):
            sp.wait_ge(staged_k, b + 1)
            sp.wait_ge(staged, b + 1)
            sp.dma_start(t3[bass.ds(b, 1), :, :].rearrange("b p n -> p (b n)"), stage[k].rearrange("p r c -> p (r c)")).then_inc(written_k[k], 16)
        written_k = [S["written_0"], S["written_1"]]
        over_blocks(sp, body)
        sp.wait_ge(S["written_0"], 16 * ((NB + 1) // 2))
        sp.wait_ge(S["written_1"], 16 * (NB // 2))

    def stage_free(eng, b, k, first):
        if not first:
            eng.wait_ge(S[f"written_{k}"], 16 * half(b, k))

    def half(b, k):
        return b // 2 if isinstance(b, int) else (b - k) // 2

    @block.tensor
    def _(pe):
        pe.wait_ge(S["t_ready"], 1)
        m_pe(pe, 0, 0, True)

        def body(b, k, first):
            pe.wait_ge(S["t_copied"], b + 1)
            if not (isinstance(b, int) and b == 0):
                pe.wait_ge(kv_sb, b)
                pe.wait_ge(q_out, b)
            for t in range(TYPES):
                nc.tensor.matmul(e.ps[:, 2, 0:P], w[:, KW + t * D:KW + (t + 1) * D], hTm[k][:, t * P:(t + 1) * P],
                                 start=(t == 0), stop=(t == TYPES - 1))
            for t in range(TYPES):
                ins = nc.tensor.matmul(e.ps[:, 2, P:2 * P], w[:, KW + 2048 + t * D:KW + 2048 + (t + 1) * D],
                                       hTm[k][:, t * P:(t + 1) * P], start=(t == 0), stop=(t == TYPES - 1))
            ins.then_inc(kv, 1)
            for t in range(TYPES):
                ins = nc.tensor.matmul(e.ps[:, 3, 0:D], hTm[k][:, t * P:(t + 1) * P],
                                       w[:, KW + 1024 + t * D:KW + 1024 + (t + 1) * D], start=(t == 0), stop=(t == TYPES - 1))
            ins.then_inc(S["t_used"], 1)
            ahead(m_pe, pe, b, k)
            pe.wait_ge(kv_sb, b + 1)
            if not (isinstance(b, int) and b == 0):
                pe.wait_ge(staged_k, b)
                pe.wait_ge(staged, b)
            for m in range(2):
                for n in range(2):
                    ins = nc.tensor.matmul(e.ps[:, 4 + 2 * m + n, :], e.ohT[:, k, m * P:(m + 1) * P],
                                           w[:, BD + m * 1024 + n * 512:BD + m * 1024 + (n + 1) * 512], start=True, stop=True)
            ins.then_inc(rel, 1)
        over_blocks(pe, body)

    @block.scalar
    def _(act):
        m_act(act, 0, 0, True)

        def body(b, k, first):
            act.wait_ge(kv, b + 1)
            if not first:
                act.wait_ge(rel, b - 1)
            nc.scalar.activation(e.ohT[:, k, 0:2 * P], e.ps[:, 2, 0:2 * P], ACT.Copy).then_inc(kv_sb, 1)
            ahead(m_act, act, b, k)
            act.wait_ge(rel, b + 1)
            stage_free(act, b, k, first)
            nc.scalar.activation(stage[k][:, :, 0:D], e.ps[:, 4:6, :].rearrange("p a (r c) -> p (a r) c", c=D), ACT.Copy)\
                .then_inc(staged_k, 1)
        over_blocks(act, body)

    def on_dve(dve, c):
        dve.wait_ge(S["w"], TYPED_LOADS)
        c.step(dve, V.tensor_scalar(e.small[:, 320:320 + RELS], e.small[:, 320:320 + RELS], HS3 ** -0.5, None, ALU.mult))
        bd = w[:, BD:BD + 1024].rearrange("p (r o) -> p r o", r=RELS)
        c.step(dve, V.tensor_tensor(bd, bd, bc(e.small[:, 320:320 + RELS], D), ALU.mult))
        V.memset(e.small[:, 0:1], 0.0).then_inc(S["t_ready"], 1)

        m_dve(dve, 0, 0, True)

        def body(b, k, first):
            ahead(m_dve, dve, b, k)
            dve.wait_ge(S["t_used"], b + 1)
            V.tensor_scalar(e.kN[:, bass.ds(b, 1), :].rearrange("p b d -> p (b d)"), e.ps[:, 3, 0:D], 1.0, None, ALU.mult).then_inc(q_out, 1)
            dve.wait_ge(rel, b + 1)
            stage_free(dve, b, k, first)
            V.tensor_copy(stage[k][:, :, D:2 * D], e.ps[:, 6:8, :].rearrange("p a (r c) -> p (a r) c", c=D)).then_inc(staged, 1)
        over_blocks(dve, body)
        c.step(dve, V.memset(e.acc[:, :], 0.0))
        c.step(dve, V.memset(e.mx[:, :], -BIG))
    return on_dve


def after_l2b(nc, A, e):
    S = Stage(e, "n4")
    V = nc.vector
    with S, nc.Block() as block:
        @block.sync
        def _(sp):
            load_row(nc, sp, e.vecs[:, 128:256], A["L2_gnn_b2"], S["v"])

        @block.scalar
        def _(act):
            norm_sqrt(nc, e, act, S, "ln")

        on_dve = typed_projections(nc, A, e, block, S, 0)

        @block.vector
        def _(dve):
            c = Chain(S["step"])
            V.memset(e.wts[:, BD:BD + 2048], 0.0).then_inc(S["bd_zero"], 1)
            normalized(nc, e, dve, c, e.tA, 1)
            dve.wait_ge(S["v"], 16)
            c.step(dve, V.tensor_tensor(e.tA, e.tA, over(e.vecs[:, 128:256]), ALU.add))
            c.step(dve, V.tensor_tensor(e.xN[:, :, :], e.xN[:, :, :], e.tA, ALU.add))
            norm(nc, e, dve, c, S, "ln", e.xN[:, :, :], e.hN[:, :, :], e.tA, True)
            on_dve(dve, c)


def after_l3(nc, A, e, layer, out):
    S = Stage(e, f"n{5 + layer}")
    V = nc.vector
    w = e.wts
    gam, bet, skip = e.vecs[:, 128:256], e.vecs[:, 256:384], e.vecs[:, 384:384 + TYPES]
    wff, bff = e.vecs[:, 512:640], e.vecs[:, 640:768]
    al = e.r_at[:, 192:192 + NB]
    last = layer == 1
    with S, nc.Block() as block:
        m_dve, m_pe, m_act, hTm = masked_turn(nc, e, block, S, "a", e.tA, (0, 4))

        @block.sync
        def _(sp):
            load_row(nc, sp, gam, A["L3_gnn_ln_g"][layer], S["v"])
            load_row(nc, sp, bet, A["L3_gnn_ln_b"][layer], S["v"])
            load_row(nc, sp, skip, A["L3_gnn_skip"][layer], S["v"])
            sp.dma_start(wff, A["L3_gnn_Wff"]).then_inc(S["v"], 16)
            load_row(nc, sp, bff, A["L3_gnn_bff"], S["v"])
            sp.wait_ge(S["a_used"], NB)

        @block.tensor
        def _(pe):
            pe.wait_ge(S["a_ready"], 1)
            m_pe(pe, 0, 0, True)

            def body(b, k, first):
                ahead(m_pe, pe, b, k)
                pe.wait_ge(S["a_copied"], b + 1)
                if not (isinstance(b, int) and b == 0):
                    pe.wait_ge(S["y_taken"], b)
                for t in range(TYPES):
                    ins = nc.tensor.matmul(e.ps[:, 2, 0:D], hTm[k][:, t * P:(t + 1) * P], w[:, WA + t * D:WA + (t + 1) * D],
                                           start=(t == 0), stop=(t == TYPES - 1))
                ins.then_inc(S["a_used"], 1)
            over_blocks(pe, body)

        @block.scalar
        def _(act):
            over_blocks(act, lambda b, k, first: m_act(act, b, k, first))
            act.wait_ge(S["z"], 1)
            nc.scalar.activation(al, al, ACT.Exp, scale=-1.0)
            nc.scalar.activation(e.tC, e.tC, ACT.Exp, scale=-1.0).then_inc(S["ez"], 1)
            norm_sqrt(nc, e, act, S, "ln")

        if last:
            project(nc, e, block, S, "f", [(e.hN, wff)], D)

            @block.sync
            def _(sp):
                sp.wait_ge(S["x_done"], 1)
                sp.dma_start(out[0:(NB - 1) * P, :].rearrange("(b p) d -> p b d", p=P), e.xN[:, 0:NB - 1, :]).then_inc(S["out"], 16)
                sp.dma_start(out[(NB - 1) * P:N, :], e.xN[0:NLAST, NB - 1, :]).then_inc(S["out"], 16)
                sp.wait_ge(S["out"], 32)
        else:
            on_dve = typed_projections(nc, A, e, block, S, layer + 1)

        @block.vector
        def _(dve):
            c = Chain(S["step"])
            y, t, u = e.kN[:, :, :], e.tB, e.tC
            normalized(nc, e, dve, c, e.tA, L3H)
            V.memset(e.small[:, 0:1], 0.0).then_inc(S["a_ready"], 1)

            m_dve(dve, 0, 0, True)

            def body(b, k, first):
                ahead(m_dve, dve, b, k)
                dve.wait_ge(S["a_used"], b + 1)
                V.tensor_scalar(e.kN[:, bass.ds(b, 1), :].rearrange("p b d -> p (b d)"), e.ps[:, 2, 0:D], 1.0, None, ALU.mult).then_inc(S["y_taken"], 1)
            over_blocks(dve, body)
            dve.wait_ge(S["y_taken"], NB)
            dve.wait_ge(S["v"], 16 * 5)
            if not last:
                V.memset(w[:, BD:BD + 2048], 0.0).then_inc(S["bd_zero"], 1)
            gate = e.tP[:, 0:NB * TYPES].rearrange("p (b t) -> p b t", t=TYPES)
            c.step(dve, V.tensor_tensor(gate, e.typeM[:, :, :], over(skip), ALU.mult))
            c.step(dve, V.tensor_reduce(al, gate, AX, ALU.add))
            c.step(dve, V.tensor_scalar(al, al, -80.0, None, ALU.max))
            c.step(dve, V.tensor_scalar(u, y, -80.0, None, ALU.max))
            V.memset(e.small[:, 0:1], 0.0).then_inc(S["z"], 1)
            dve.wait_ge(S["ez"], 1)
            c.step(dve, V.tensor_scalar(al, al, 1.0, None, ALU.add))
            c.step(dve, V.reciprocal(al, al))
            c.step(dve, V.tensor_scalar(u, u, 1.0, None, ALU.add))
            c.step(dve, V.reciprocal(u, u))
            c.step(dve, V.tensor_tensor(t, y, u, ALU.mult))
            c.step(dve, V.tensor_tensor(t, t, e.hN[:, :, :], ALU.subtract))
            c.step(dve, V.tensor_tensor(t, t, bc(al, D), ALU.mult))
            c.step(dve, V.tensor_tensor(t, t, e.hN[:, :, :], ALU.add))
            norm(nc, e, dve, c, S, "ln", t, u, e.tA, False)
            c.step(dve, V.tensor_tensor(u, u, over(gam), ALU.mult))
            c.step(dve, V.tensor_tensor(e.hN[:, :, :], u, over(bet), ALU.add))
            if last:
                V.memset(e.small[:, 0:1], 0.0).then_inc(S["f_ready"], 1)

                def take(b, k, first):
                    dve.wait_ge(S["f_done"], b + 1)
                    V.tensor_tensor(e.kN[:, bass.ds(b, 1), :].rearrange("p b d -> p (b d)"), e.ps[:, 2 + k, 0:D], bff,
                                    ALU.add).then_inc(S["f_taken"], 1)
                over_blocks(dve, take)
                dve.wait_ge(S["f_taken"], NB)
                c.step(dve, V.tensor_tensor(e.xN[:, :, :], e.xN[:, :, :], e.kN[:, :, :], ALU.add))
                V.memset(e.small[:, 0:1], 0.0).then_inc(S["x_done"], 1)
            else:
                on_dve(dve, c)


_INS = ["x", "src", "dst", "edge_type_8", "edge_weight", "node_type_8", "L0_gnn_W1", "L0_gnn_b1", "L0_gnn_W2", "L0_gnn_b2",
        "L1_gnn_Wq", "L1_gnn_bq", "L1_gnn_Wk", "L1_gnn_bk", "L1_gnn_Wv", "L1_gnn_bv", "L1_gnn_Ws", "L1_gnn_bs", "L1_gnn_Wg",
        "L1_gnn_bg", "L1_gnn_gamma", "L1_gnn_beta", "L1_gnn_alpha", "L2_gnn_Wl1", "L2_gnn_bl1", "L2_gnn_Wr1", "L2_gnn_br1",
        "L2_gnn_att1", "L2_gnn_b1", "L2_gnn_Wl2", "L2_gnn_bl2", "L2_gnn_Wr2", "L2_gnn_br2", "L2_gnn_att2", "L2_gnn_b2",
        "L3_gnn_Wk", "L3_gnn_Wq", "L3_gnn_Wv", "L3_gnn_Wa", "L3_gnn_pri", "L3_gnn_Watt", "L3_gnn_Wmsg", "L3_gnn_skip",
        "L3_gnn_ln_g", "L3_gnn_ln_b", "L3_gnn_Wff", "L3_gnn_bff"]


def kernel(**inputs):
    import concourse.bacc as bacc
    from concourse.bass_utils import run_bass_kernel_spmd as run

    nc = bacc.Bacc("TRN2", target_bir_lowering=False, num_devices=1)
    arrays, A = {}, {}
    for name in _INS:
        a = np.ascontiguousarray(inputs[name])
        if a.ndim == 0:
            a = a.reshape(1)
        arrays[f"in_{name}"] = a
        A[name] = nc.dram_tensor(f"in_{name}", a.shape, mybir.dt.from_np(a.dtype), kind="ExternalInput").ap()
    out = nc.dram_tensor("out_nodes", (N, D), F32, kind="ExternalOutput").ap()
    build(nc, A, out)
    r = run(nc, [arrays], core_ids=[0])
    return r.results[0]["out_nodes"]
```
